# Optimizing a Trainium2 kernel written in Bass

```python
import numpy as np
import jax
import jax.numpy as jnp

def _softmax(x, axis=-1):
    return jax.nn.softmax(x, axis=axis)

def _gelu(x):
    return jax.nn.gelu(x, approximate=True)

def _silu(x):
    return jax.nn.silu(x)

def _sigmoid(x):
    return jax.nn.sigmoid(x)

def _layernorm(x, axis=-1, eps=1e-05):
    m = jnp.mean(x, axis=axis, keepdims=True)
    v = jnp.var(x, axis=axis, keepdims=True)
    return (x - m) / jnp.sqrt(v + eps)

def _scatter_add(tgt, idx, src, axis=0):
    return tgt.at[idx].add(src)

def _segment_sum(src, seg, n):
    return jax.ops.segment_sum(src, seg, n)
kernel_name = 'mk_macaron_d1_jaxref_r4_4f53df'

def setup_inputs(seed: int=0):
    np.random.seed(seed)
    _w = jnp.asarray

    def _L0_attn_setup():
        import jax, jax.numpy as jnp
        import numpy as np
        B, S, D, H, R = (8, 256, 256, 8, 32)
        DH = D // H

        def _lowrank(xh, U, V, b):
            t = jnp.einsum('bshd,hrd->bshr', xh, V)
            return jnp.einsum('bshr,hdr->bshd', t, U) + b
        key = jax.random.key(seed)
        ks = jax.random.split(key, 10)
        p = lambda k, shape: jax.random.normal(k, shape, dtype=jnp.float32) * 0.02
        return {'x': jax.random.normal(ks[0], (B, S, D), dtype=jnp.float32), 'Uq': p(ks[1], (H, DH, R)), 'Vq': p(ks[2], (H, R, DH)), 'bq': p(ks[3], (H, DH)), 'Uk': p(ks[4], (H, DH, R)), 'Vk': p(ks[5], (H, R, DH)), 'bk': p(ks[6], (H, DH)), 'Uv': p(ks[7], (H, DH, R)), 'Vv': p(ks[8], (H, R, DH)), 'bv': p(ks[9], (H, DH))}
    _L0_attn_in = _L0_attn_setup()

    def _L0_ffn_setup():
        import math
        import jax, jax.numpy as jnp
        import numpy as np
        B, T, D = (4, 1024, 256)
        H = 16
        HD = D // H
        CAP = int(1024 * 0.125)
        DFF = int(D * 4 * 2 / 3)
        EPS = 1e-06

        def rmsnorm(x, g):
            return x * jax.lax.rsqrt(jnp.mean(x * x, axis=-1, keepdims=True) + EPS) * g
        key = jax.random.key(seed)
        ks = jax.random.split(key, 9)
        s = lambda k, shape: jax.random.normal(k, shape, jnp.float32) * 0.02
        return {'x': jax.random.normal(ks[0], (B, T, D), jnp.float32), 'w_router': s(ks[1], (D,)), 'W_qkv': s(ks[2], (3 * D, D)), 'W_out': s(ks[3], (D, D)), 'g1': jnp.ones((D,), jnp.float32), 'g2': jnp.ones((D,), jnp.float32), 'W1': s(ks[4], (DFF, D)), 'W2': s(ks[5], (DFF, D)), 'W3': s(ks[6], (D, DFF))}
    _L0_ffn_in = _L0_ffn_setup()
    _d = {'L0_attn_x': _L0_attn_in['x'], 'L0_attn_Uq': _L0_attn_in['Uq'], 'L0_attn_Vq': _L0_attn_in['Vq'], 'L0_attn_bq': _L0_attn_in['bq'], 'L0_attn_Uk': _L0_attn_in['Uk'], 'L0_attn_Vk': _L0_attn_in['Vk'], 'L0_attn_bk': _L0_attn_in['bk'], 'L0_attn_Uv': _L0_attn_in['Uv'], 'L0_attn_Vv': _L0_attn_in['Vv'], 'L0_attn_bv': _L0_attn_in['bv'], 'L0_ffn_w_router': _L0_ffn_in['w_router'], 'L0_ffn_W_qkv': _L0_ffn_in['W_qkv'], 'L0_ffn_W_out': _L0_ffn_in['W_out'], 'L0_ffn_g1': _L0_ffn_in['g1'], 'L0_ffn_g2': _L0_ffn_in['g2'], 'L0_ffn_W1': _L0_ffn_in['W1'], 'L0_ffn_W2': _L0_ffn_in['W2'], 'L0_ffn_W3': _L0_ffn_in['W3']}
    _x0 = _d['L0_attn_x']
    _d['L0_attn_x'] = jax.random.normal(jax.random.fold_in(jax.random.key(seed), 1), (8, 2048, 256), dtype=_x0.dtype)
    del _x0
    return _d

def reference(L0_attn_x, L0_attn_Uq, L0_attn_Vq, L0_attn_bq, L0_attn_Uk, L0_attn_Vk, L0_attn_bk, L0_attn_Uv, L0_attn_Vv, L0_attn_bv, L0_ffn_w_router, L0_ffn_W_qkv, L0_ffn_W_out, L0_ffn_g1, L0_ffn_g2, L0_ffn_W1, L0_ffn_W2, L0_ffn_W3):

    def _L0_attn_ref(x, Uq, Vq, bq, Uk, Vk, bk, Uv, Vv, bv):
        import jax, jax.numpy as jnp
        import numpy as np
        B, S, D, H, R = (8, 256, 256, 8, 32)
        DH = D // H

        def _lowrank(xh, U, V, b):
            t = jnp.einsum('bshd,hrd->bshr', xh, V)
            return jnp.einsum('bshr,hdr->bshd', t, U) + b
        b_, s_, _ = x.shape
        xh = x.reshape(b_, s_, H, DH)
        q = _lowrank(xh, Uq, Vq, bq)
        k = _lowrank(xh, Uk, Vk, bk)
        v = _lowrank(xh, Uv, Vv, bv)
        scores = jnp.einsum('bqhd,bkhd->bhqk', q, k) / DH ** 0.5
        attn = jax.nn.softmax(scores, axis=-1)
        out = jnp.einsum('bhqk,bkhd->bqhd', attn, v)
        return out.reshape(b_, s_, D)

    def _L0_ffn_ref(x, w_router, W_qkv, W_out, g1, g2, W1, W2, W3):
        import math
        import jax, jax.numpy as jnp
        import numpy as np
        B, T, D = (4, 1024, 256)
        H = 16
        HD = D // H
        CAP = int(1024 * 0.125)
        DFF = int(D * 4 * 2 / 3)
        EPS = 1e-06

        def rmsnorm(x, g):
            return x * jax.lax.rsqrt(jnp.mean(x * x, axis=-1, keepdims=True) + EPS) * g
        Bq, Tq, Dq = x.shape
        scores = x @ w_router
        _, idx = jax.lax.top_k(scores, CAP)
        x_sel = jnp.take_along_axis(x, idx[:, :, None], axis=1)
        h = rmsnorm(x_sel, g1)
        qkv = (h @ W_qkv.T).reshape(Bq, CAP, 3, H, HD)
        q, k, v = jnp.moveaxis(qkv, 2, 0)
        att = jnp.einsum('bqhd,bkhd->bhqk', q, k) / math.sqrt(HD)
        mask = jnp.triu(jnp.ones((CAP, CAP), bool), 1)
        att = jnp.where(mask, -jnp.inf, att)
        att = jax.nn.softmax(att, axis=-1)
        o = jnp.einsum('bhqk,bkhd->bqhd', att, v).reshape(Bq, CAP, Dq)
        x_attn = o @ W_out.T
        h2 = rmsnorm(x_sel + x_attn, g2)
        x_ff = jax.nn.silu(h2 @ W1.T) * (h2 @ W2.T) @ W3.T
        x_proc = x_sel + x_attn + x_ff
        out = x.at[jnp.arange(Bq)[:, None], idx].set(x_proc)
        return out
    x = L0_attn_x
    x = x + 0.5 * _L0_ffn_ref(_layernorm(x, axis=-1), L0_ffn_w_router, L0_ffn_W_qkv, L0_ffn_W_out, L0_ffn_g1, L0_ffn_g2, L0_ffn_W1, L0_ffn_W2, L0_ffn_W3)
    x = x + _L0_attn_ref(_layernorm(x, axis=-1), L0_attn_Uq, L0_attn_Vq, L0_attn_bq, L0_attn_Uk, L0_attn_Vk, L0_attn_bk, L0_attn_Uv, L0_attn_Vv, L0_attn_bv)
    x = x + 0.5 * _L0_ffn_ref(_layernorm(x, axis=-1), L0_ffn_w_router, L0_ffn_W_qkv, L0_ffn_W_out, L0_ffn_g1, L0_ffn_g2, L0_ffn_W1, L0_ffn_W2, L0_ffn_W3)
    return x

_drawn_inputs = setup_inputs


def setup_inputs(seed=0):
    import zlib

    import numpy as np

    out = dict(_drawn_inputs(seed))
    spreads = {'L0_ffn_g1': (1.0, 0.6), 'L0_ffn_g2': (1.0, 0.6)}
    factors = {'L0_attn_Uq': 8.0,
     'L0_attn_Vq': 8.0,
     'L0_attn_bq': 8.0,
     'L0_attn_Uk': 8.0,
     'L0_attn_Vk': 8.0,
     'L0_attn_Uv': 8.0,
     'L0_attn_Vv': 8.0,
     'L0_attn_bv': 4.111,
     'L0_ffn_w_router': 8.0,
     'L0_ffn_W_qkv': 8.0,
     'L0_ffn_W_out': 8.0,
     'L0_ffn_W1': 8.0,
     'L0_ffn_W2': 8.0,
     'L0_ffn_W3': 8.0}
    for name, (base, spread) in spreads.items():
        noise = np.random.default_rng([zlib.crc32(name.encode()), seed]).standard_normal(out[name].shape)
        drawn = base * np.exp(spread * noise) if base else spread * noise
        out[name] = jnp.asarray(drawn.astype(out[name].dtype))
    for name, factor in factors.items():
        out[name] = (out[name] * factor).astype(out[name].dtype)
    return out
```

```python
from contextlib import ExitStack, contextmanager

import concourse.bass as bass
from concourse import mybir

P = 128
F32 = mybir.dt.float32
F32R = mybir.dt.float32r
U32 = mybir.dt.uint32
I32 = mybir.dt.int32
ALU = mybir.AluOpType
ACT = mybir.ActivationFunctionType
AX = mybir.AxisListType

B, S, D = 8, 2048, 256
T = S // P
H, DH = 8, 32
HG = P // DH
NG = H // HG
CAP = 128
FH, FD = 16, 16
DFF = 682
DFF_HALF = DFF // 2
DFF_TILES = (DFF + P - 1) // P
LN_EPS = 1e-5
RMS_EPS = 1e-6
LOWEST = -3.0e38


class Chain:

    def __init__(self, engine, semaphore, base=0):
        self.engine, self.semaphore, self.base, self.n = engine, semaphore, base, 0

    def step(self, instruction):
        self.n += 1
        instruction.then_inc(self.semaphore, 1)
        self.engine.wait_ge(self.semaphore, self.base + self.n)
        return instruction


@contextmanager
def cleared_semaphores(nc):
    used = []
    yield used
    nc.clear_and_free_semaphores(used)
    nc.all_engine_barrier()


def score_pass(nc, tag, x, add, w_router, y, scores):
    adding = add is not None
    with ExitStack() as ctx:
        used = ctx.enter_context(cleared_semaphores(nc))

        def sb(name, shape, dt=F32):
            return ctx.enter_context(nc.sbuf_tensor(f"{tag}_{name}", shape, dt))

        def sem(name):
            handle = nc.alloc_semaphore(f"{tag}_{name}")
            used.append(handle)
            return handle

        xb = sb("x", [P, 2, T, D])
        ab = sb("add", [P, 2, T, D]) if adding else None
        yb = sb("y", [P, 2, T, D])
        w = sb("w", [P, D])
        wsum = sb("wsum", [P, 1])
        junk = sb("junk", [P, 4, D])
        stats = sb("stats", [P, 2, T, 6])
        sm = sb("small", [P, 2, 12, T])
        sall = sb("sall", [P, B, T])
        sT = sb("sT", [P, P])
        ones = sb("ones", [P, P])
        ident = sb("ident", [P, P])
        pt = ctx.enter_context(nc.psum_tensor(f"{tag}_pt", [P, P], F32))

        w_in = sem("w_in")
        x_in = [sem(f"x_in{i}") for i in range(2)]
        a_in = [sem(f"a_in{i}") for i in range(2)]
        added = sem("added")
        dve_own = sem("dve_own")
        var_ready = sem("var_ready")
        std_ready = sem("std_ready")
        affine_ready = sem("affine_ready")
        products_done = sem("products_done")
        stats_done = sem("stats_done")
        y_done = sem("y_done")
        y_out = [sem(f"y_out{i}") for i in range(2)]
        id_ready = sem("id_ready")
        scores_done = sem("scores_done")
        transposed = sem("transposed")
        sT_done = sem("sT_done")
        s_out = sem("s_out")

        block = ctx.enter_context(nc.Block())

        @block.sync
        def _(sp):
            sp.dma_start(w[:], w_router.partition_broadcast(P)).then_inc(w_in, 16)

            def load(i, k):
                b = 2 * i + k
                src = x[bass.ds(b * S, S), :].rearrange("(t p) d -> p t d", p=P)
                sp.dma_start(xb[:, k], src).then_inc(x_in[k], 16)
                if adding:
                    src = add[bass.ds(b * S, S), :].rearrange("(t p) d -> p t d", p=P)
                    sp.dma_start(ab[:, k], src).then_inc(a_in[k], 16)

            for k in range(2):
                load(0, k)
            with sp.Fori(1, B // 2) as i:
                for k in range(2):
                    sp.wait_ge(products_done, ((i - 1) * 2 + k + 1) * T)
                    sp.wait_ge(y_done, (i - 1) * 2 + k + 1)
                    load(i, k)

        @block.gpsimd
        def _(pool):
            nc.gpsimd.memset(ones[:], 1.0).then_inc(id_ready, 1)
            pool.wait_ge(id_ready, 1)
            nc.gpsimd.affine_select(out=ident[:], in_=ones[:], compare_op=ALU.is_equal, fill=0.0, base=0,
                                    pattern=[[-1, P]], channel_multiplier=1).then_inc(id_ready, 1)
            if adding:
                with pool.Fori(0, B // 2) as i:
                    for k in range(2):
                        pool.wait_ge(x_in[k], i * 16 + 16)
                        pool.wait_ge(a_in[k], i * 16 + 16)
                        for q in range(4):
                            t4 = slice(4 * q, 4 * q + 4)
                            last = nc.gpsimd.tensor_tensor(xb[:, k, t4], xb[:, k, t4], ab[:, k, t4], ALU.add)
                            last.then_inc(added, 1)

        @block.vector
        def _(dve):
            dve.wait_ge(w_in, 16)
            own = Chain(dve, dve_own)
            own.step(nc.vector.reduce_sum(wsum[:], w[:], AX.X))
            with dve.Fori(0, B // 2) as i:
                own = Chain(dve, dve_own, i * 28 + 1)
                for k in range(2):
                    if not adding:
                        dve.wait_ge(x_in[k], i * 16 + 16)
                    v = [sm[:, k, n, :] for n in range(12)]
                    for t in range(T):
                        if adding and t % 4 == 0:
                            dve.wait_ge(added, i * 8 + 4 * k + t // 4 + 1)
                        nc.vector.bn_stats(stats[:, k, t, :], xb[:, k, t, :]).then_inc(stats_done, 1)
                        if t >= 4:
                            dve.wait_ge(products_done, (i * 2 + k) * T + t - 3)
                        nc.vector.tensor_tensor_reduce(out=junk[:, t % 4, :], in0=xb[:, k, t, :], in1=w[:], scale=1.0,
                                                       scalar=0.0, op0=ALU.mult, op1=ALU.add,
                                                       accum_out=v[11][:, t:t + 1]).then_inc(products_done, 1)
                    dve.wait_ge(stats_done, (i * 2 + k + 1) * T)
                    dve.wait_ge(products_done, (i * 2 + k + 1) * T)
                    me, m2e, mo, m2o = (stats[:, k, :, n] for n in (1, 2, 4, 5))
                    own.step(nc.vector.tensor_tensor(v[0], me, mo, ALU.add))
                    own.step(nc.vector.tensor_tensor(v[1], me, mo, ALU.subtract))
                    own.step(nc.vector.tensor_tensor(v[2], m2e, m2o, ALU.add))
                    own.step(nc.vector.scalar_tensor_tensor(v[3], v[1], 0.25, v[1], ALU.mult, ALU.mult))
                    own.step(nc.vector.tensor_scalar(v[4], v[2], 1.0 / D, LN_EPS, ALU.mult, ALU.add))
                    nc.vector.tensor_tensor(v[5], v[3], v[4], ALU.add).then_inc(var_ready, 1)
                    dve.wait_ge(std_ready, i * 2 + k + 1)
                    own.step(nc.vector.reciprocal(v[7], v[6]))
                    own.step(nc.vector.tensor_tensor(v[8], v[7], v[7], ALU.mult))
                    own.step(nc.vector.tensor_tensor(v[8], v[8], v[5], ALU.mult))
                    own.step(nc.vector.tensor_scalar(v[8], v[8], -0.5, 1.5, ALU.mult, ALU.add))
                    own.step(nc.vector.tensor_tensor(v[9], v[7], v[8], ALU.mult))
                    own.step(nc.vector.scalar_tensor_tensor(v[10], v[0], 0.5, v[9], ALU.mult, ALU.mult))
                    own.step(nc.vector.tensor_scalar(v[0], v[9], 0.5, 1.0, ALU.mult, ALU.add))
                    nc.vector.tensor_scalar(v[1], v[10], -0.5, None, ALU.mult).then_inc(affine_ready, 1)
                    own.step(nc.vector.tensor_tensor(v[2], v[11], v[9], ALU.mult))
                    own.step(nc.vector.tensor_scalar(v[3], v[10], wsum[:], None, ALU.mult))
                    nc.vector.tensor_tensor(sall[:, bass.ds(i * 2 + k, 1), :].rearrange("p a t -> p (a t)"),
                                            v[2], v[3], ALU.subtract).then_inc(scores_done, 1)

        @block.scalar
        def _(act):
            with act.Fori(0, B // 2) as i:
                for k in range(2):
                    act.wait_ge(var_ready, i * 2 + k + 1)
                    nc.scalar.activation(sm[:, k, 6, :], sm[:, k, 5, :], ACT.Sqrt).then_inc(std_ready, 1)
                    act.wait_ge(affine_ready, i * 2 + k + 1)
                    act.wait_ge(y_out[k], i * 16)
                    for t in range(T):
                        last = nc.scalar.activation(yb[:, k, t, :], xb[:, k, t, :], ACT.Identity,
                                                    scale=sm[:, k, 0, t:t + 1], bias=sm[:, k, 1, t:t + 1])
                    last.then_inc(y_done, 1)
                    act.wait_ge(y_done, i * 2 + k + 1)
                    act.dma_start(y[bass.ds((i * 2 + k) * S, S), :].rearrange("(t p) d -> p t d", p=P),
                                  yb[:, k]).then_inc(y_out[k], 16)
            act.wait_ge(transposed, 1)
            nc.scalar.copy(sT[:], pt[:]).then_inc(sT_done, 1)
            act.wait_ge(sT_done, 1)
            act.dma_start(scores, sT[:]).then_inc(s_out, 16)
            act.wait_ge(s_out, 16)
            for k in range(2):
                act.wait_ge(y_out[k], 16 * B // 2)

        @block.tensor
        def _(pe):
            pe.wait_ge(id_ready, 2)
            pe.wait_ge(scores_done, B)
            nc.tensor.transpose(pt[:], sall[:].rearrange("p b t -> p (b t)"), ident[:]).then_inc(transposed, 1)


def pick_tokens(nc, tag, scores, picked):
    with ExitStack() as ctx:
        used = ctx.enter_context(cleared_semaphores(nc))

        def sb(name, shape, dt=F32):
            return ctx.enter_context(nc.sbuf_tensor(f"{tag}_{name}", shape, dt))

        def sem(name):
            handle = nc.alloc_semaphore(f"{tag}_{name}")
            used.append(handle)
            return handle

        sc = sb("sc", [B, S])
        top = sb("top", [B, CAP])
        index = sb("index", [B, CAP], U32)
        indexf = sb("indexf", [B, CAP])
        ones = sb("ones", [B, B])
        ident = sb("ident", [B, B])
        first_row = sb("first_row", [P, B])
        first_row_i = sb("first_row_i", [P, B], I32)
        pt = ctx.enter_context(nc.psum_tensor(f"{tag}_pt", [P, B], F32))
        loaded = sem("loaded")
        own_done = sem("own")
        consts = sem("consts")
        indices_done = sem("indices_done")
        transposed = sem("transposed")
        picked_done = sem("picked_done")

        block = ctx.enter_context(nc.Block())

        @block.sync
        def _(sp):
            sp.dma_start(sc[:], scores.rearrange("(b t) p -> b (t p)", b=B)).then_inc(loaded, 16)

        @block.gpsimd
        def _(pool):
            nc.gpsimd.memset(ones[:], 1.0).then_inc(consts, 1)
            nc.gpsimd.iota(first_row_i[:], pattern=[[S, B]], base=0, channel_multiplier=0).then_inc(consts, 1)
            pool.wait_ge(consts, 2)
            nc.gpsimd.affine_select(out=ident[:], in_=ones[:], compare_op=ALU.is_equal, fill=0.0, base=0,
                                    pattern=[[-1, B]], channel_multiplier=1).then_inc(consts, 1)
            nc.gpsimd.tensor_copy(first_row[:], first_row_i[:]).then_inc(consts, 1)

        @block.vector
        def _(dve):
            own = Chain(dve, own_done)
            dve.wait_ge(loaded, 16)
            for r in range(CAP // 8):
                eight = slice(8 * r, 8 * r + 8)
                own.step(nc.vector.max(top[:, eight], sc[:]))
                own.step(nc.vector.max_index(index[:, eight], top[:, eight], sc[:]))
                if r < CAP // 8 - 1:
                    own.step(nc.vector.match_replace(sc[:], top[:, eight], sc[:], LOWEST))
            nc.vector.tensor_copy(indexf[:], index[:]).then_inc(indices_done, 1)
            dve.wait_ge(transposed, 1)
            dve.wait_ge(consts, 4)
            nc.vector.tensor_tensor(picked, pt[:], first_row[:], ALU.add).then_inc(picked_done, 1)
            dve.wait_ge(picked_done, 1)

        @block.tensor
        def _(pe):
            pe.wait_ge(consts, 4)
            pe.wait_ge(indices_done, 1)
            nc.tensor.transpose(pt[:], indexf[:], ident[:]).then_inc(transposed, 1)


def routed_ffn(nc, tag, x, add, picked, w_qkvT, w_outT, g1, g2, w1T, w2T, w3T, y):
    adding = add is not None
    NB = 4
    ROUNDS = B // NB
    NC = D // P
    PAIRS = P // (2 * FD)
    GH = P // FD
    with ExitStack() as ctx:
        used = ctx.enter_context(cleared_semaphores(nc))

        def sb(name, shape, dt=F32):
            return ctx.enter_context(nc.sbuf_tensor(f"{tag}_{name}", shape, dt))

        def sem(name):
            handle = nc.alloc_semaphore(f"{tag}_{name}")
            used.append(handle)
            return handle

        wqkv = sb("wqkv", [P, NC, 3 * D])
        wout = sb("wout", [P, NC, D])
        w1 = sb("w1", [P, NC, DFF])
        w2 = sb("w2", [P, NC, DFF])
        w3 = sb("w3", [P, DFF_TILES, D])
        gain = sb("gain", [P, 2, NC])
        ones = sb("ones", [P, P])
        zeros = sb("zeros", [P, P])
        ident = sb("ident", [P, P])
        causal = sb("causal", [P, P])
        head_half = sb("head_half", [P, GH])
        head_of = sb("head_of", [P, GH])
        parity = sb("parity", [P, 2])
        xs = sb("xs", [P, NB, D])
        ads = sb("ads", [P, NB, D]) if adding else None
        chosen = sb("chosen", [P, NB], U32)
        stats = sb("stats", [P, NB, 6])
        sm = sb("small", [P, 16, NB])
        xh = sb("xh", [P, NB, D])
        hn = sb("hn", [P, NB, D])
        hT = sb("hT", [P, NC, NB, P])
        qT = sb("qT", [P, NC, NB, P])
        v = sb("v", [P, NB, D])
        kspread = sb("kspread", [P, NB, NC, GH, P])
        att = sb("att", [P, NB, FH, P])
        rowmax = sb("rowmax", [P, NB, FH])
        rowsum = sb("rowsum", [P, NB, FH])
        attT = sb("attT", [P, 2, FH, P])
        odd = sb("odd", [P, 2, NC, P])
        oT = sb("oT", [P, NC, NB, P])
        xr = sb("xr", [P, NB, D])
        sq = sb("sq", [P, NB, D])
        sig = sb("sig", [P, 2, DFF])
        act1 = sb("act1", [P, 2, DFF])
        gated = sb("gated", [P, 2, DFF])
        gatedT = sb("gatedT", [P, 2, DFF_TILES, P])
        proc = sb("proc", [P, NB, D])
        row = sb("row", [P, NB, D])
        ps = ctx.enter_context(nc.psum_tensor(f"{tag}_ps", [P, 8, 512], F32))

        weights_in = sem("weights_in")
        consts = sem("consts")
        x_in = [sem(f"x_in{s}") for s in range(NB)]
        chosen_done = sem("chosen_done")
        rows_ready = sem("rows_ready")
        dve_own = sem("dve_own")
        var_ready = sem("var_ready")
        std_ready = sem("std_ready")
        rstd_ready = sem("rstd_ready")
        ms_ready = sem("ms_ready")
        rms_ready = sem("rms_ready")
        scale_ready = sem("scale_ready")
        xh_done = sem("xh_done")
        hn_done = sem("hn_done")
        h_turned = sem("h_turned")
        hT_done = sem("hT_done")
        qk_done = sem("qk_done")
        v_done = sem("v_done")
        qT_copied = sem("qT_copied")
        v_copied = sem("v_copied")
        spread_done = sem("spread_done")
        scores_done = sem("scores_done")
        max_done = sem("max_done")
        shifted_done = sem("shifted_done")
        exp_done = sem("exp_done")
        recip_done = sem("recip_done")
        probs_done = sem("probs_done")
        probs_turned = sem("probs_turned")
        probsT_copied = sem("probsT_copied")
        pv_done = sem("pv_done")
        oT_done = sem("oT_done")
        proj_done = sem("proj_done")
        xr_done = sem("xr_done")
        sq_done = sem("sq_done")
        ms2_ready = sem("ms2_ready")
        std2_ready = sem("std2_ready")
        r2_ready = sem("r2_ready")
        h2_done = sem("h2_done")
        h2_turned = sem("h2_turned")
        h2T_done = sem("h2T_done")
        up_done = sem("up_done")
        tanh_done = sem("tanh_done")
        gated_done = sem("gated_done")
        gated_turned = sem("gated_turned")
        gatedT_done = sem("gatedT_done")
        down_done = sem("down_done")
        row_done = sem("row_done")
        row_out = sem("row_out")
        scatter_turn = sem("scatter_turn")
        gather_turn = sem("gather_turn")

        BANK_H = 4
        BANK_K, BANK_Q = 4, 6
        BANK_V = 0
        BANK_S = 0
        BANK_PT = 4
        BANK_O = 6
        BANK_W = 0
        BANK_H2 = 2

        def bank_up(s):
            return 4 * ((s + 1) % 2)

        block = ctx.enter_context(nc.Block())

        @block.sync
        def _(sp):
            sp.dma_start(wqkv[:], w_qkvT.rearrange("(c p) n -> p c n", p=P)).then_inc(weights_in, 16)
            sp.dma_start(wout[:], w_outT.rearrange("(c p) n -> p c n", p=P)).then_inc(weights_in, 16)
            sp.dma_start(w1[:], w1T.rearrange("(c p) n -> p c n", p=P)).then_inc(weights_in, 16)
            sp.dma_start(w2[:], w2T.rearrange("(c p) n -> p c n", p=P)).then_inc(weights_in, 16)
            full = DFF // P
            sp.dma_start(w3[:, 0:full, :], w3T[0:full * P, :].rearrange("(c p) n -> p c n", p=P)
                         ).then_inc(weights_in, 16)
            sp.dma_start(w3[0:DFF - full * P, full, :], w3T[full * P:DFF, :]).then_inc(weights_in, 16)
            sp.dma_start(gain[:, 0, :], g1).then_inc(weights_in, 16)
            sp.dma_start(gain[:, 1, :], g2).then_inc(weights_in, 16)
        WEIGHTS = 8 * 16

        @block.gpsimd
        def _(pool):
            own = Chain(pool, consts)
            own.step(nc.gpsimd.memset(ones[:], 1.0))
            own.step(nc.gpsimd.memset(zeros[:], 0.0))
            nc.gpsimd.affine_select(out=ident[:], in_=ones[:], compare_op=ALU.is_equal, fill=0.0, base=0,
                                    pattern=[[-1, P]], channel_multiplier=1).then_inc(consts, 1)
            nc.gpsimd.affine_select(out=causal[:], in_=zeros[:], compare_op=ALU.is_ge, fill=-1e30, base=0,
                                    pattern=[[-1, P]], channel_multiplier=1).then_inc(consts, 1)
            nc.gpsimd.affine_select(out=head_half[:], in_=ones[:, 0:GH], compare_op=ALU.is_ge, fill=0.0, base=0,
                                    pattern=[[-FD, GH]], channel_multiplier=1).then_inc(consts, 1)
            pool.wait_ge(consts, 5)
            nc.gpsimd.affine_select(out=head_of[:], in_=head_half[:], compare_op=ALU.is_ge, fill=0.0, base=FD - 1,
                                    pattern=[[FD, GH]], channel_multiplier=-1).then_inc(consts, 1)
            with pool.Fori(0, ROUNDS) as i:
                def at(s):
                    return i * NB + s + 1

                pool.wait_ge(row_done, i * NB)
                nc.gpsimd.tensor_copy(chosen[:], picked[:, bass.ds(i * NB, NB)]).then_inc(chosen_done, 1)
                pool.wait_ge(chosen_done, i + 1)
                pool.sem_inc(gather_turn, 1)
                for s in range(NB):
                    index = chosen[:, s:s + 1]
                    nc.gpsimd.indirect_dma_start(
                        out=xs[:, s, :], out_offset=None, in_=x,
                        in_offset=bass.IndirectOffsetOnAxis(ap=index, axis=0)).then_inc(x_in[s], 16)
                    if adding:
                        nc.gpsimd.indirect_dma_start(
                            out=ads[:, s, :], out_offset=None, in_=add,
                            in_offset=bass.IndirectOffsetOnAxis(ap=index, axis=0)).then_inc(x_in[s], 16)
                if adding:
                    for s in range(NB):
                        pool.wait_ge(x_in[s], i * 32 + 32)
                        nc.gpsimd.tensor_tensor(xs[:, s, :], xs[:, s, :], ads[:, s, :],
                                                ALU.add).then_inc(rows_ready, 1)

                def shift(s):
                    pool.wait_ge(max_done, at(s))
                    nc.gpsimd.tensor_tensor(att[:, s], att[:, s], rowmax[:, s].unsqueeze(2).to_broadcast([P, FH, P]),
                                            ALU.subtract).then_inc(shifted_done, 1)

                def normalize(s):
                    pool.wait_ge(recip_done, at(s))
                    nc.gpsimd.tensor_tensor(att[:, s], att[:, s], rowsum[:, s].unsqueeze(2).to_broadcast([P, FH, P]),
                                            ALU.mult).then_inc(probs_done, 1)

                shift(0)
                for s in range(1, NB):
                    shift(s)
                    normalize(s - 1)
                normalize(NB - 1)
                for s in range(NB):
                    pool.wait_ge(row_done, at(s))
                    pool.sem_inc(scatter_turn, 1)
                    index = chosen[:, s:s + 1]
                    nc.gpsimd.indirect_dma_start(
                        out=y, out_offset=bass.IndirectOffsetOnAxis(ap=index, axis=0), in_=row[:, s, :],
                        in_offset=None).then_inc(row_out, 16)
                    pool.wait_ge(row_out, at(s) * 16)

        @block.vector
        def _(dve):
            dve.wait_ge(consts, 6)
            own = Chain(dve, dve_own)
            own.step(nc.vector.tensor_reduce(parity[:], head_of[:].rearrange("p (a two) -> p two a", two=2),
                                             AX.X, ALU.add))
            dve.wait_ge(weights_in, WEIGHTS)
            with dve.Fori(0, ROUNDS) as i:
                own = Chain(dve, dve_own, i * ROUND_STEPS + 1)

                def at(s):
                    return i * NB + s + 1

                def c(n):
                    return sm[:, n, :]

                def newton(r, var, scratch, out, done):
                    own.step(nc.vector.tensor_tensor(c(scratch), c(r), c(r), ALU.mult))
                    own.step(nc.vector.tensor_tensor(c(scratch), c(scratch), c(var), ALU.mult))
                    own.step(nc.vector.tensor_scalar(c(scratch), c(scratch), -0.5, 1.5, ALU.mult, ALU.add))
                    nc.vector.tensor_tensor(c(out), c(r), c(scratch), ALU.mult).then_inc(done, 1)
                    dve.wait_ge(done, i + 1)

                for s in range(NB):
                    if adding:
                        dve.wait_ge(rows_ready, at(s))
                    else:
                        dve.wait_ge(x_in[s], i * 16 + 16)
                    last = nc.vector.bn_stats(stats[:, s, :], xs[:, s, :])
                    own.step(last)
                me, m2e, mo, m2o = (stats[:, :, n] for n in (1, 2, 4, 5))
                own.step(nc.vector.tensor_tensor(c(0), me, mo, ALU.add))
                own.step(nc.vector.tensor_tensor(c(1), me, mo, ALU.subtract))
                own.step(nc.vector.tensor_tensor(c(2), m2e, m2o, ALU.add))
                own.step(nc.vector.scalar_tensor_tensor(c(1), c(1), 0.25, c(1), ALU.mult, ALU.mult))
                own.step(nc.vector.scalar_tensor_tensor(c(2), c(2), 1.0 / D, c(1), ALU.mult, ALU.add))
                nc.vector.tensor_scalar(c(3), c(2), LN_EPS, None, ALU.add).then_inc(var_ready, 1)
                dve.wait_ge(std_ready, i + 1)
                own.step(nc.vector.reciprocal(c(5), c(4)))
                newton(5, 3, 6, 7, rstd_ready)
                own.step(nc.vector.tensor_tensor(c(8), c(2), c(7), ALU.mult))
                own.step(nc.vector.tensor_tensor(c(8), c(8), c(7), ALU.mult))
                own.step(nc.vector.scalar_tensor_tensor(c(10), c(0), -0.5, c(7), ALU.mult, ALU.mult))
                nc.vector.tensor_scalar(c(8), c(8), RMS_EPS, None, ALU.add).then_inc(ms_ready, 1)
                dve.wait_ge(rms_ready, i + 1)
                own.step(nc.vector.reciprocal(c(5), c(9)))
                newton(5, 8, 6, 11, scale_ready)

                for s in range(NB):
                    for g in range(NC):
                        if s == 0 and g == 0:
                            dve.wait_ge(qk_done, i + 1)
                        last = nc.vector.tensor_tensor(
                            kspread[:, s, g],
                            ps[:, BANK_K + g, s * P:(s + 1) * P].unsqueeze(1).to_broadcast([P, GH, P]),
                            head_of[:].unsqueeze(2).to_broadcast([P, GH, P]), ALU.mult)
                    last.then_inc(spread_done, 1)
                for s in range(NB):
                    dve.wait_ge(scores_done, at(s))
                    own.step(nc.vector.tensor_tensor(
                        att[:, s], ps[:, BANK_S:BANK_S + 4, :].rearrange("p b (h k) -> p (b h) k", k=P),
                        causal[:].unsqueeze(1).to_broadcast([P, FH, P]), ALU.add))
                    nc.vector.reduce_max(rowmax[:, s], att[:, s], AX.X).then_inc(max_done, 1)
                for s in range(NB):
                    dve.wait_ge(exp_done, at(s))
                    own.step(nc.vector.reduce_sum(rowsum[:, s], att[:, s], AX.X))
                    nc.vector.reciprocal(rowsum[:, s], rowsum[:, s]).then_inc(recip_done, 1)
                for s in range(NB):
                    o = ps[:, BANK_O + s % 2, :].rearrange("p (g two t) -> p two g t", g=NC, two=2)
                    dve.wait_ge(pv_done, at(s))
                    own.step(nc.vector.tensor_scalar(odd[:, s % 2], o[:, 1], parity[:, 1:2], None, ALU.mult))
                    nc.vector.scalar_tensor_tensor(oT[:, :, s, :], o[:, 0], parity[:, 0:1], odd[:, s % 2],
                                                   ALU.mult, ALU.add).then_inc(oT_done, 1)
                for s in range(NB):
                    dve.wait_ge(proj_done, at(s))
                    nc.vector.tensor_tensor(xr[:, s, :], ps[:, BANK_W + s, 0:D], xh[:, s, :],
                                            ALU.add).then_inc(xr_done, 1)
                    dve.wait_ge(xr_done, at(s))
                    own.step(nc.vector.tensor_tensor_reduce(out=sq[:, s, :], in0=xr[:, s, :], in1=xr[:, s, :],
                                                            scale=1.0, scalar=0.0, op0=ALU.mult, op1=ALU.add,
                                                            accum_out=sm[:, 12, s:s + 1]))
                nc.vector.tensor_scalar(c(13), c(12), 1.0 / D, RMS_EPS, ALU.mult, ALU.add).then_inc(ms2_ready, 1)
                dve.wait_ge(std2_ready, i + 1)
                own.step(nc.vector.reciprocal(c(5), c(14)))
                newton(5, 13, 6, 15, r2_ready)
                def gate(s):
                    u = bank_up(s)
                    dve.wait_ge(tanh_done, at(s))
                    own.step(nc.vector.scalar_tensor_tensor(
                        act1[:, s % 2].rearrange("p (n f) -> p n f", n=2), sig[:, s % 2].rearrange("p (n f) -> p n f", n=2),
                        1.0, ps[:, u:u + 2, 0:DFF_HALF], ALU.add, ALU.mult))
                    if s >= 2:
                        dve.wait_ge(gated_turned, at(s - 2))
                    nc.vector.scalar_tensor_tensor(
                        gated[:, s % 2].rearrange("p (n f) -> p n f", n=2), act1[:, s % 2].rearrange("p (n f) -> p n f", n=2),
                        0.5, ps[:, u + 2:u + 4, 0:DFF_HALF], ALU.mult, ALU.mult).then_inc(gated_done, 1)

                def final_row(s):
                    u = bank_up(s)
                    dve.wait_ge(down_done, at(s))
                    own.step(nc.vector.tensor_tensor(proc[:, s, :], ps[:, u + 2, 0:D], xr[:, s, :], ALU.add))
                    nc.vector.scalar_tensor_tensor(row[:, s, :], proc[:, s, :], 0.5, xs[:, s, :],
                                                   ALU.mult, ALU.add).then_inc(row_done, 1)

                gate(0)
                gate(1)
                for s in range(NB):
                    final_row(s)
                    if s + 2 < NB:
                        gate(s + 2)
                assert own.n == ROUND_STEPS, own.n

        @block.scalar
        def _(act):
            act.wait_ge(weights_in, WEIGHTS)
            with act.Fori(0, ROUNDS) as i:
                def at(s):
                    return i * NB + s + 1

                act.wait_ge(var_ready, i + 1)
                nc.scalar.activation(sm[:, 4, :], sm[:, 3, :], ACT.Sqrt).then_inc(std_ready, 1)
                act.wait_ge(ms_ready, i + 1)
                nc.scalar.activation(sm[:, 9, :], sm[:, 8, :], ACT.Sqrt).then_inc(rms_ready, 1)
                act.wait_ge(scale_ready, i + 1)
                for s in range(NB):
                    nc.scalar.activation(xh[:, s, :], xs[:, s, :], ACT.Identity, scale=sm[:, 7, s:s + 1],
                                         bias=sm[:, 10, s:s + 1]).then_inc(xh_done, 1)
                for s in range(NB):
                    act.wait_ge(xh_done, at(s))
                    nc.scalar.activation(hn[:, s, :], xh[:, s, :], ACT.Copy, scale=sm[:, 11, s:s + 1]
                                         ).then_inc(hn_done, 1)
                act.wait_ge(h_turned, i + 1)
                for g in range(NC):
                    nc.scalar.activation(hT[:, g].rearrange("p s t -> p (s t)"), ps[:, BANK_H + g, :], ACT.Copy,
                                         scale=gain[:, 0, g:g + 1]).then_inc(hT_done, 1)
                act.wait_ge(qk_done, i + 1)
                for g in range(NC):
                    nc.scalar.copy(qT[:, g].rearrange("p s t -> p (s t)"), ps[:, BANK_Q + g, :]).then_inc(qT_copied, 1)
                act.wait_ge(v_done, i + 1)
                nc.scalar.copy(v[:].rearrange("p (b s) d -> p b (s d)", b=2),
                               ps[:, BANK_V:BANK_V + 2, :]).then_inc(v_copied, 1)
                for s in range(NB):
                    act.wait_ge(shifted_done, at(s))
                    nc.scalar.activation(att[:, s], att[:, s], ACT.Exp, scale=float(FD) ** -0.5).then_inc(exp_done, 1)
                for s in range(NB):
                    for half in range(2):
                        act.wait_ge(probs_turned, (i * NB + s) * 2 + half + 1)
                        if s >= 2 and half == 0:
                            act.wait_ge(pv_done, at(s - 2))
                        nc.scalar.copy(attT[:, s % 2, half * GH:(half + 1) * GH].rearrange("p (b h) t -> p b (h t)", b=2),
                                       ps[:, BANK_PT:BANK_PT + 2, :]).then_inc(probsT_copied, 1)
                act.wait_ge(ms2_ready, i + 1)
                nc.scalar.activation(sm[:, 14, :], sm[:, 13, :], ACT.Sqrt).then_inc(std2_ready, 1)
                act.wait_ge(r2_ready, i + 1)
                for s in range(NB):
                    nc.scalar.activation(hn[:, s, :], xr[:, s, :], ACT.Copy, scale=sm[:, 15, s:s + 1]
                                         ).then_inc(h2_done, 1)
                act.wait_ge(h2_turned, i + 1)
                for g in range(NC):
                    nc.scalar.activation(hT[:, g].rearrange("p s t -> p (s t)"), ps[:, BANK_H2 + g, :], ACT.Copy,
                                         scale=gain[:, 1, g:g + 1]).then_inc(h2T_done, 1)

                def tanh(s):
                    act.wait_ge(up_done, at(s))
                    u = bank_up(s)
                    if s >= 2:
                        act.wait_ge(gated_done, at(s - 2))
                    nc.scalar.activation(sig[:, s % 2].rearrange("p (n f) -> p n f", n=2), ps[:, u:u + 2, 0:DFF_HALF],
                                         ACT.Tanh, scale=0.5).then_inc(tanh_done, 1)

                def copy_gatedT(s):
                    u = bank_up(s)
                    act.wait_ge(gated_turned, at(s))
                    if s >= 2:
                        act.wait_ge(down_done, at(s - 2))
                    nc.scalar.copy(gatedT[:, s % 2, 0:4, :].rearrange("p a t -> p (a t)"), ps[:, u, :])
                    nc.scalar.copy(gatedT[:, s % 2, 4, :], ps[:, u + 1, 0:P])
                    nc.scalar.copy(gatedT[0:DFF - 5 * P, s % 2, 5, :], ps[0:DFF - 5 * P, u + 1, P:2 * P]
                                   ).then_inc(gatedT_done, 1)

                tanh(0)
                tanh(1)
                for s in range(NB):
                    copy_gatedT(s)
                    if s + 2 < NB:
                        tanh(s + 2)

        @block.tensor
        def _(pe):
            pe.wait_ge(weights_in, WEIGHTS)
            pe.wait_ge(consts, 6)
            with pe.Fori(0, ROUNDS) as i:
                def at(s):
                    return i * NB + s + 1

                for s in range(NB):
                    pe.wait_ge(hn_done, at(s))
                    if s == 0:
                        pe.wait_ge(row_done, i * NB)
                    for g in range(NC):
                        last = nc.tensor.transpose(ps[:, BANK_H + g, s * P:(s + 1) * P],
                                                   hn[:, s, g * P:(g + 1) * P], ident[:])
                last.then_inc(h_turned, 1)
                pe.wait_ge(hT_done, i * NC + NC)
                for s in range(NB):
                    for c in range(NC):
                        last = nc.tensor.matmul(ps[:, BANK_V + s // 2, (s % 2) * D:(s % 2 + 1) * D], hT[:, c, s, :],
                                                wqkv[:, c, 2 * D:3 * D], start=(c == 0), stop=(c == NC - 1))
                last.then_inc(v_done, 1)
                for which, bank in ((1, BANK_K), (0, BANK_Q)):
                    for g in range(NC):
                        for c in range(NC):
                            last = nc.tensor.matmul(ps[:, bank + g, :], wqkv[:, c, which * D + g * P:which * D + (g + 1) * P],
                                                    hT[:, c].rearrange("p s t -> p (s t)"), start=(c == 0),
                                                    stop=(c == NC - 1))
                last.then_inc(qk_done, 1)
                pe.wait_ge(qT_copied, i * NC + NC)
                pe.wait_ge(v_copied, i + 1)
                for s in range(NB):
                    pe.wait_ge(spread_done, at(s))
                    if s >= 1:
                        pe.wait_ge(max_done, at(s - 1))
                    for h4 in range(FH // 4):
                        g = h4 // 2
                        last = nc.tensor.matmul(ps[:, BANK_S + h4, :], qT[:, g, s, :],
                                                kspread[:, s, g, (h4 % 2) * 4:(h4 % 2) * 4 + 4].rearrange("p j t -> p (j t)"),
                                                start=True, stop=True)
                    last.then_inc(scores_done, 1)
                for s in range(NB):
                    pe.wait_ge(probs_done, at(s))
                    for half in range(2):
                        if s > 0 or half > 0:
                            pe.wait_ge(probsT_copied, (i * NB + s) * 2 + half)
                        for j in range(GH):
                            last = nc.tensor.transpose(ps[:, BANK_PT + j // 4, (j % 4) * P:(j % 4 + 1) * P],
                                                       att[:, s, half * GH + j, :], ident[:])
                        last.then_inc(probs_turned, 1)
                    for half in range(2):
                        pe.wait_ge(probsT_copied, (i * NB + s) * 2 + half + 1)
                        if s >= 2 and half == 0:
                            pe.wait_ge(oT_done, at(s - 2))
                        for j in (0, 2, 4, 6, 1, 3, 5, 7):
                            h = half * GH + j
                            pair = j // 2
                            base = (half * 2 + j % 2) * P
                            ch = half * P + pair * 2 * FD
                            last = nc.tensor.matmul(ps[pair * 32:pair * 32 + 32, BANK_O + s % 2, base:base + P],
                                                    v[:, s, ch:ch + 2 * FD], attT[:, s % 2, h, :], start=True, stop=True)
                    last.then_inc(pv_done, 1)
                for s in range(NB):
                    pe.wait_ge(oT_done, at(s))
                    for c in range(NC):
                        last = nc.tensor.matmul(ps[:, BANK_W + s, 0:D], oT[:, c, s, :],
                                                wout[:, c, :], start=(c == 0), stop=(c == NC - 1))
                    last.then_inc(proj_done, 1)
                for s in range(NB):
                    pe.wait_ge(h2_done, at(s))
                    for g in range(NC):
                        last = nc.tensor.transpose(ps[:, BANK_H2 + g, s * P:(s + 1) * P],
                                                   hn[:, s, g * P:(g + 1) * P], ident[:])
                last.then_inc(h2_turned, 1)
                pe.wait_ge(h2T_done, i * NC + NC)

                def up(s):
                    u = bank_up(s)
                    if s >= 2:
                        pe.wait_ge(row_done, at(s - 2))
                    for w, bank in ((w1, u), (w2, u + 2)):
                        for n in range(2):
                            for c in range(NC):
                                last = nc.tensor.matmul(ps[:, bank + n, 0:DFF_HALF], hT[:, c, s, :],
                                                        w[:, c, n * DFF_HALF:(n + 1) * DFF_HALF], start=(c == 0),
                                                        stop=(c == NC - 1))
                    last.then_inc(up_done, 1)

                def down(s):
                    u = bank_up(s)
                    pe.wait_ge(gated_done, at(s))
                    for f in range(DFF_TILES):
                        m = min(P, DFF - f * P)
                        last = nc.tensor.transpose(ps[0:m, u + f // 4, (f % 4) * P:(f % 4 + 1) * P],
                                                   gated[:, s % 2, f * P:f * P + m], ident[:])
                    last.then_inc(gated_turned, 1)
                    pe.wait_ge(gatedT_done, at(s))
                    for f in range(DFF_TILES):
                        m = min(P, DFF - f * P)
                        last = nc.tensor.matmul(ps[:, u + 2, 0:D], gatedT[0:m, s % 2, f, :], w3[0:m, f, :],
                                                start=(f == 0), stop=(f == DFF_TILES - 1))
                    last.then_inc(down_done, 1)

                up(0)
                up(1)
                for s in range(NB):
                    down(s)
                    if s + 2 < NB:
                        up(s + 2)


ROUND_STEPS = 48


def project(nc, tag, x, lowrank, biases, v_bias, qk, v_dram):
    with ExitStack() as ctx:
        used = ctx.enter_context(cleared_semaphores(nc))

        def sb(name, shape, dt=F32):
            return ctx.enter_context(nc.sbuf_tensor(f"{tag}_{name}", shape, dt))

        def sem(name):
            handle = nc.alloc_semaphore(f"{tag}_{name}")
            used.append(handle)
            return handle

        NQ = 4
        TQ = T // NQ
        facV = sb("facV", [P, 3, NG, P])
        facU = sb("facU", [P, 3, NG, P])
        w = sb("w", [P, 3, NG, P])
        bias = sb("bias", [P, 2, NG])
        vb = sb("vb", [P, D])
        ones = sb("ones", [P, P])
        ident = sb("ident", [P, P])
        xb = sb("x", [P, 2, T, D])
        stats = sb("stats", [P, T, 6])
        sm = sb("small", [P, 8, T])
        xT = sb("xT", [P, 2, NG, TQ * P])
        hi = sb("hi", [P, 2, 2 * NG, TQ * P], F32R)
        lo = sb("lo", [P, 2, 2 * NG, TQ * P], F32R)
        v = sb("v", [P, 2, TQ, D])
        pT = ctx.enter_context(nc.psum_tensor(f"{tag}_pT", [P, NG, 512], F32))
        pqk = ctx.enter_context(nc.psum_tensor(f"{tag}_pqk", [P, 2 * NG, 512], F32))
        pv = ctx.enter_context(nc.psum_tensor(f"{tag}_pv", [P, 2, 512], F32))

        consts = sem("consts")
        zeroed = sem("zeroed")
        factors_in = sem("factors_in")
        w_done = sem("w_done")
        w_copied = sem("w_copied")
        x_in = [sem(f"x_in{k}") for k in range(2)]
        stats_done = sem("stats_done")
        dve_own = sem("dve_own")
        var_ready = sem("var_ready")
        std_ready = sem("std_ready")
        affine_ready = sem("affine_ready")
        xh_done = sem("xh_done")
        turned = sem("turned")
        xT_copied = sem("xT_copied")
        qk_done = sem("qk_done")
        v_done = sem("v_done")
        hi_done = sem("hi_done")
        lo_done = sem("lo_done")
        v_copied = sem("v_copied")
        hi_out = [sem(f"hi_out{k}") for k in range(2)]
        lo_out = [sem(f"lo_out{k}") for k in range(2)]
        v_out = [sem(f"v_out{k}") for k in range(2)]
        FACTORS = 2 * 3 * H * 16 + 3 * 16
        OWN = 10

        block = ctx.enter_context(nc.Block())

        @block.gpsimd
        def _(pool):
            nc.gpsimd.memset(ones[:], 1.0).then_inc(consts, 1)
            pool.wait_ge(consts, 1)
            nc.gpsimd.affine_select(out=ident[:], in_=ones[:], compare_op=ALU.is_equal, fill=0.0, base=0,
                                    pattern=[[-1, P]], channel_multiplier=1).then_inc(consts, 1)

        @block.sync
        def _(sp):
            sp.wait_ge(zeroed, 2)
            for n, (u, vt) in enumerate(lowrank):
                for h in range(H):
                    r = (h % HG) * DH
                    sp.dma_start(facV[r:r + DH, n, h // HG, r:r + DH], vt[h]).then_inc(factors_in, 16)
                    sp.dma_start(facU[r:r + DH, n, h // HG, r:r + DH], u[h]).then_inc(factors_in, 16)
            for n in range(2):
                sp.dma_start(bias[:, n, :], biases[n]).then_inc(factors_in, 16)
            sp.dma_start(vb[:], v_bias.partition_broadcast(P)).then_inc(factors_in, 16)

            def load(i, k):
                src = x[bass.ds((i * 2 + k) * S, S), :].rearrange("(t p) d -> p t d", p=P)
                sp.dma_start(xb[:, k], src).then_inc(x_in[k], 16)

            def store(i, k, n):
                at = (i * 2 + k) * NQ + n + 1
                tok = slice(n * TQ * P, (n + 1) * TQ * P)
                dst = qk[bass.ds(i * 2 + k, 1)].rearrange("a part g c s -> part c (a g) s")
                sp.wait_ge(hi_done, at * 4)
                sp.dma_start(dst[0, :, :, tok], hi[:, n % 2].bitcast(F32)).then_inc(hi_out[n % 2], 16)
                sp.wait_ge(lo_done, at * 4)
                sp.dma_start(dst[1, :, :, tok], lo[:, n % 2].bitcast(F32)).then_inc(lo_out[n % 2], 16)
                sp.wait_ge(v_copied, at * 2)
                sp.dma_start(v_dram[bass.ds((i * 2 + k) * S + n * TQ * P, TQ * P), :]
                             .rearrange("(t p) d -> p t d", p=P), v[:, n % 2]).then_inc(v_out[n % 2], 16)

            load(0, 0)
            load(0, 1)
            with sp.Fori(0, B // 2 - 1) as i:
                for k in range(2):
                    for n in range(NQ):
                        store(i, k, n)
                    load(i + 1, k)
            for k in range(2):
                for n in range(NQ):
                    store(B // 2 - 1, k, n)
            for s in (*hi_out, *lo_out, *v_out):
                sp.wait_ge(s, B * NQ // 2 * 16)

        @block.vector
        def _(dve):
            nc.vector.memset(facV[:], 0.0).then_inc(zeroed, 1)
            nc.vector.memset(facU[:], 0.0).then_inc(zeroed, 1)
            dve.wait_ge(w_done, 1)
            nc.vector.tensor_copy(w[:, 0:2].rearrange("p n g c -> p (n g c)"), pT[:, 0, :]).then_inc(w_copied, 1)
            nc.vector.tensor_copy(w[:, 2].rearrange("p g c -> p (g c)"), pT[:, 1, 0:NG * P]).then_inc(w_copied, 1)
            with dve.Fori(0, B // 2) as i:
                for k in range(2):
                    b = i * 2 + k
                    own = Chain(dve, dve_own, b * OWN)
                    c = [sm[:, n, :] for n in range(8)]
                    dve.wait_ge(x_in[k], i * 16 + 16)
                    for t in range(T):
                        nc.vector.bn_stats(stats[:, t, :], xb[:, k, t, :]).then_inc(stats_done, 1)
                    dve.wait_ge(stats_done, (b + 1) * T)
                    dve.wait_ge(xh_done, b * T)
                    me, m2e, mo, m2o = (stats[:, :, n] for n in (1, 2, 4, 5))
                    own.step(nc.vector.tensor_tensor(c[0], me, mo, ALU.add))
                    own.step(nc.vector.tensor_tensor(c[1], me, mo, ALU.subtract))
                    own.step(nc.vector.tensor_tensor(c[2], m2e, m2o, ALU.add))
                    own.step(nc.vector.scalar_tensor_tensor(c[1], c[1], 0.25, c[1], ALU.mult, ALU.mult))
                    own.step(nc.vector.tensor_scalar(c[2], c[2], 1.0 / D, LN_EPS, ALU.mult, ALU.add))
                    nc.vector.tensor_tensor(c[3], c[1], c[2], ALU.add).then_inc(var_ready, 1)
                    dve.wait_ge(std_ready, b + 1)
                    own.step(nc.vector.reciprocal(c[5], c[4]))
                    own.step(nc.vector.tensor_tensor(c[6], c[5], c[5], ALU.mult))
                    own.step(nc.vector.tensor_tensor(c[6], c[6], c[3], ALU.mult))
                    own.step(nc.vector.tensor_scalar(c[6], c[6], -0.5, 1.5, ALU.mult, ALU.add))
                    own.step(nc.vector.tensor_tensor(c[6], c[5], c[6], ALU.mult))
                    nc.vector.scalar_tensor_tensor(c[7], c[0], -0.5, c[6], ALU.mult, ALU.mult
                                                   ).then_inc(affine_ready, 1)
                    for n in range(NQ):
                        at = b * NQ + n
                        dve.wait_ge(hi_done, at * 4)
                        if n >= 2:
                            dve.wait_ge(lo_out[n % 2], (i * 2 + k) * 32 + (n // 2) * 16)
                            dve.wait_ge(v_out[n % 2], (i * 2 + k) * 32 + (n // 2) * 16)
                        else:
                            dve.wait_ge(lo_out[n % 2], (i * 2 + k) * 32)
                            dve.wait_ge(v_out[n % 2], (i * 2 + k) * 32)
                        for m in range(2 * NG):
                            dve.wait_ge(hi_done, at * 4 + m + 1)
                            nc.vector.scalar_tensor_tensor(
                                lo[:, n % 2, m], pqk[:, m, :], bias[:, m // NG, m % NG:m % NG + 1],
                                hi[:, n % 2, m].bitcast(F32), ALU.add, ALU.subtract).then_inc(lo_done, 1)
                        dve.wait_ge(v_done, at + 1)
                        for m in range(2):
                            nc.vector.tensor_tensor(v[:, n % 2, 2 * m:2 * m + 2, :],
                                                    pv[:, m, :].rearrange("p (t d) -> p t d", t=2),
                                                    vb[:].unsqueeze(1).to_broadcast([P, 2, D]), ALU.add
                                                    ).then_inc(v_copied, 1)

        @block.scalar
        def _(act):
            act.wait_ge(factors_in, FACTORS)
            with act.Fori(0, B // 2) as i:
                for k in range(2):
                    b = i * 2 + k
                    act.wait_ge(var_ready, b + 1)
                    nc.scalar.activation(sm[:, 4, :], sm[:, 3, :], ACT.Sqrt).then_inc(std_ready, 1)
                    act.wait_ge(affine_ready, b + 1)

                    def normal(n):
                        for t in range(n * TQ, (n + 1) * TQ):
                            nc.scalar.activation(xb[:, k, t, :], xb[:, k, t, :], ACT.Identity,
                                                 scale=sm[:, 6, t:t + 1], bias=sm[:, 7, t:t + 1]).then_inc(xh_done, 1)

                    normal(0)
                    for n in range(NQ):
                        at = b * NQ + n
                        if n + 1 < NQ:
                            normal(n + 1)
                        act.wait_ge(turned, at + 1)
                        for g in range(NG):
                            nc.scalar.copy(xT[:, n % 2, g, :], pT[:, g, :]).then_inc(xT_copied, 1)
                        act.wait_ge(hi_out[n % 2], b * 32 + (n // 2) * 16)
                        for m in range(2 * NG):
                            act.wait_ge(qk_done, at * 4 + m + 1)
                            nc.scalar.activation(hi[:, n % 2, m], pqk[:, m, :], ACT.Identity,
                                                 bias=bias[:, m // NG, m % NG:m % NG + 1]).then_inc(hi_done, 1)

        @block.tensor
        def _(pe):
            pe.wait_ge(consts, 2)
            pe.wait_ge(factors_in, FACTORS)
            for n in range(3):
                for g in range(NG):
                    at = (n * NG + g) * P
                    last = nc.tensor.matmul(pT[:, at // 512, at % 512:at % 512 + P], facV[:, n, g, :],
                                            facU[:, n, g, :], start=True, stop=True)
            last.then_inc(w_done, 1)
            pe.wait_ge(w_copied, 2)
            with pe.Fori(0, B // 2) as i:
                for k in range(2):
                    b = i * 2 + k

                    def turn(n):
                        for t in range(TQ):
                            if t == 0 or n == 0:
                                pe.wait_ge(xh_done, b * T + n * TQ + TQ)
                            for g in range(NG):
                                last = nc.tensor.transpose(pT[:, g, t * P:(t + 1) * P],
                                                           xb[:, k, n * TQ + t, g * P:(g + 1) * P], ident[:])
                        last.then_inc(turned, 1)

                    turn(0)
                    for n in range(NQ):
                        at = b * NQ + n
                        pe.wait_ge(xT_copied, at * NG + NG)
                        if n + 1 < NQ:
                            turn(n + 1)
                        for m in range(2 * NG):
                            pe.wait_ge(lo_done, (at - 1) * 4 + m + 1) if n > 0 else pe.wait_ge(lo_done, at * 4)
                            nc.tensor.matmul(pqk[:, m, :], w[:, m // NG, m % NG, :], xT[:, n % 2, m % NG, :],
                                             start=True, stop=True).then_inc(qk_done, 1)
                        pe.wait_ge(v_copied, at * 2)
                        for t in range(TQ):
                            for g in range(NG):
                                last = nc.tensor.matmul(pv[:, t // 2, (t % 2) * D + g * P:(t % 2) * D + (g + 1) * P],
                                                        xT[:, n % 2, g, t * P:(t + 1) * P], w[:, 2, g, :],
                                                        start=True, stop=True)
                        last.then_inc(v_done, 1)


def attend(nc, tag, qk, v_dram, out):
    UQ = 512
    NU = S // UQ
    NC = S // P
    QT = UQ // P
    TILES = NC * HG
    BU = NG * NU
    STACK = 3 * DH
    RING = 4 * HG
    PV_LAG = 6
    LEAD = 4 * NC // HG
    NQB = 4
    POOL_CHUNKS, DVE_CHUNKS = 11, 4
    RAW = NC - POOL_CHUNKS - DVE_CHUNKS
    SCALE = float(DH) ** -0.5
    with ExitStack() as ctx:
        used = ctx.enter_context(cleared_semaphores(nc))

        def sb(name, shape, dt=F32):
            return ctx.enter_context(nc.sbuf_tensor(f"{tag}_{name}", shape, dt))

        def psum(name, shape):
            return ctx.enter_context(nc.psum_tensor(f"{tag}_{name}", shape, F32))

        def sem(name):
            handle = nc.alloc_semaphore(f"{tag}_{name}")
            used.append(handle)
            return handle

        qs = sb("qs", [STACK + 1, NQB, HG, UQ], F32R)
        ks = sb("ks", [STACK + 1, NG, HG, S], F32R)
        v = sb("v", [P, NG, NC, P])
        probs = sb("probs", [P, RING, UQ])
        pool_sum = sb("pool_sum", [P, 2, HG, UQ])
        dve_sum = sb("dve_sum", [P, 2, HG, UQ])
        part_max = sb("part_max", [P, HG, QT, 2])
        neg_max = sb("neg_max", [P, HG, QT])
        max_row = sb("max_row", [QT, HG, P], F32R)
        ones = sb("ones", [P, P])
        ident = sb("ident", [P, P])
        oT = sb("oT", [P, UQ])
        zT = sb("zT", [P, UQ])
        rz = sb("rz", [P, QT, HG])
        o = sb("o", [P, 2, QT, HG, DH])
        ps_max = psum("ps_max", [P, 2, 2, 512])
        ps_s = psum("ps_s", [P, 2, UQ])
        ps_acc = psum("ps_acc", [P, UQ])
        ps_misc = psum("ps_misc", [P, 512])

        load_turn = sem("load_turn")
        consts = sem("consts")
        ones_row = sem("ones_row")
        q_in = [sem(f"q_in{n}") for n in range(NQB)]
        k_in = [sem(f"k_in{n}") for n in range(NG)]
        v_in = [sem(f"v_in{n}") for n in range(NG)]
        max_scores = sem("max_scores")
        part_max_done = sem("part_max_done")
        neg_max_done = sem("neg_max_done")
        max_turned = sem("max_turned")
        max_row_done = sem("max_row_done")
        max_in = [sem(f"max_in{h}") for h in range(HG)]
        scores = sem("scores")
        exp_done = sem("exp_done")
        pv_done = sem("pv_done")
        pool_added = sem("pool_added")
        dve_added = sem("dve_added")
        z_done = sem("z_done")
        oT_done = sem("oT_done")
        zT_done = sem("zT_done")
        z_turned = sem("z_turned")
        rz_done = sem("rz_done")
        o_turned = sem("o_turned")
        o_done = sem("o_done")
        o_out = [sem(f"o_out{n}") for n in range(2)]

        adds_pool = (POOL_CHUNKS - 1) * HG
        adds_dve = (DVE_CHUNKS - 1) * HG

        block = ctx.enter_context(nc.Block())

        @block.sync
        def _(sp):
            def load_q(b, un):
                g, u, k = un // NU, un % NU, un % NQB
                src = qk[bass.ds(b, 1)].rearrange("a part g (h d) s -> part g d (a h) s", h=HG)
                cols = slice(u * UQ, (u + 1) * UQ)
                for r, part in enumerate((0, 1, 0)):
                    sp.dma_start(qs[r * DH:(r + 1) * DH, k].bitcast(F32), src[part, g, :, :, cols]
                                 ).then_inc(q_in[k], 16)

            def load_kv(b, g):
                src = qk[bass.ds(b, 1)].rearrange("a part g (h d) s -> part g d (a h) s", h=HG)
                for r, part in enumerate((0, 0, 1)):
                    sp.dma_start(ks[r * DH:(r + 1) * DH, g].bitcast(F32), src[part, NG + g]).then_inc(k_in[g], 16)
                sp.dma_start(v[:, g], v_dram[bass.ds(b * S, S), g * P:(g + 1) * P]
                             .rearrange("(c p) d -> p c d", p=P)).then_inc(v_in[g], 16)

            def max_rows(b, un):
                n = b * BU + un + 1
                for h in range(HG):
                    sp.wait_ge(max_row_done, n * HG + h + 1)
                    sp.dma_start(qs[STACK:STACK + 1, (un + 1) % NQB, h, :].bitcast(F32)
                                 .rearrange("a (t q) -> a t q", t=QT),
                                 max_row[:, h, :].bitcast(F32)).then_inc(max_in[h], 16)

            load_q(0, 0)
            load_kv(0, 0)
            load_q(0, 1)
            load_kv(0, 1)
            load_q(0, 2)
            max_rows(0, -1)

            def batch(b, after):
                for un in range(BU):
                    sp.wait_ge(scores, (b * BU + un) * TILES)
                    sp.sem_inc(load_turn, 1)
                    ahead = un + 3
                    load_q(b if ahead < BU else after, ahead % BU)
                    if un == NU:
                        sp.wait_ge(pv_done, (b * BU + un) * TILES)
                        sp.sem_inc(load_turn, 1)
                        load_kv(after, 0)
                    max_rows(b, un)
                sp.wait_ge(pv_done, (b + 1) * BU * TILES)
                sp.sem_inc(load_turn, 1)
                load_kv(after, 1)

            with sp.Fori(0, B - 1) as b:
                batch(b, b + 1)
            batch(B - 1, 0)
            for k in range(NQB):
                units = [u for u in range(B * BU + 3) if u % NQB == k]
                sp.wait_ge(q_in[k], len(units) * 48)
            for g in range(NG):
                sp.wait_ge(k_in[g], (B + 1) * 48)
                sp.wait_ge(v_in[g], (B + 1) * 16)
            for h in range(HG):
                sp.wait_ge(max_in[h], (B * BU + 1) * 16)

        @block.gpsimd
        def _(pool):
            nc.gpsimd.memset(ones[:], 1.0).then_inc(consts, 1)
            pool.wait_ge(consts, 1)
            nc.gpsimd.affine_select(out=ident[:], in_=ones[:], compare_op=ALU.is_equal, fill=0.0, base=0,
                                    pattern=[[-1, P]], channel_multiplier=1).then_inc(consts, 1)
            with pool.Fori(0, B) as b:
                for un in range(BU):
                    unit = b * BU + un
                    acc = pool_sum[:, un % 2]
                    for c in range(1, POOL_CHUNKS):
                        for h in range(HG):
                            j = c * HG + h
                            pool.wait_ge(exp_done, unit * TILES + j + 1)
                            if c == 1:
                                if un >= 2:
                                    pool.wait_ge(z_done, unit - 1)
                                else:
                                    pool.wait_ge(z_done, b * BU)
                                first = probs[:, (j - HG) % RING]
                            else:
                                pool.wait_ge(pool_added, unit * adds_pool + (c - 2) * HG + h + 1)
                                first = acc[:, h]
                            nc.gpsimd.tensor_tensor(acc[:, h], first, probs[:, j % RING], ALU.add
                                                    ).then_inc(pool_added, 1)

        @block.vector
        def _(dve):
            nc.vector.memset(ks[STACK:STACK + 1].bitcast(F32), 1.0).then_inc(ones_row, 1)

            def part_max_of(unit, m):
                h, t, half = m // (2 * QT), m // 2 % QT, m % 2
                if m % (2 * QT) == 0:
                    dve.wait_ge(neg_max_done, (unit - 1) * HG + h + 1) if not isinstance(unit, int) or unit > 0 else None
                dve.wait_ge(max_scores, (unit * TILES // 2 if isinstance(unit, int) else unit * (TILES // 2)) + m + 1)
                nc.vector.reduce_max(part_max[:, h, t, half:half + 1], ps_max[:, m % 2], AX.XY
                                     ).then_inc(part_max_done, 1)
                if m % (2 * QT) == 2 * QT - 1:
                    dve.wait_ge(part_max_done, unit * (TILES // 2) + m + 1)
                    if not isinstance(unit, int) or unit > 0:
                        dve.wait_ge(max_turned, (unit - 1) * HG + h + 1)
                    nc.vector.tensor_reduce(neg_max[:, h], part_max[:, h], AX.X, ALU.max, negate=True
                                            ).then_inc(neg_max_done, 1)

            for m in range(TILES // 2):
                part_max_of(0, m)
            for m in range(LEAD // 2):
                part_max_of(1, m)
            with dve.Fori(0, B) as b:
                for un in range(BU):
                    unit = b * BU + un

                    def add(c, h):
                        j = c * HG + h
                        acc = dve_sum[:, un % 2, h]
                        dve.wait_ge(exp_done, unit * TILES + j + 1)
                        k = c - POOL_CHUNKS - 1
                        if k == 0:
                            if un >= 2:
                                dve.wait_ge(z_done, unit - 1)
                            else:
                                dve.wait_ge(z_done, b * BU)
                            first = probs[:, (j - HG) % RING]
                        else:
                            dve.wait_ge(dve_added, unit * adds_dve + (k - 1) * HG + h + 1)
                            first = acc
                        nc.vector.tensor_tensor(acc, first, probs[:, j % RING], ALU.add).then_inc(dve_added, 1)

                    def invert(prev):
                        dve.wait_ge(z_turned, prev + 1)
                        dve.wait_ge(o_done, prev)
                        nc.vector.reciprocal(rz[:], ps_misc[:].rearrange("p (t h d) -> p t h d", t=QT, h=HG)[:, :, :, 0]
                                             ).then_inc(rz_done, 1)

                    def normalize(prev, k):
                        dve.wait_ge(rz_done, prev + 1)
                        dve.wait_ge(o_turned, prev + 1)
                        if k >= 2:
                            dve.wait_ge(o_out[k % 2], b * BU * 8 + (k // 2) * 16)
                        else:
                            dve.wait_ge(o_out[k % 2], b * BU * 8)
                        nc.vector.tensor_tensor(
                            o[:, k % 2], ps_misc[:].rearrange("p (t h d) -> p t h d", t=QT, h=HG),
                            rz[:].unsqueeze(3).to_broadcast([P, QT, HG, DH]), ALU.mult).then_inc(o_done, 1)

                    for j in range(TILES):
                        if j % 2 == 1:
                            m = (j + LEAD) // 2
                            if m < TILES // 2:
                                part_max_of(unit + 1, m)
                            else:
                                part_max_of(unit + 2, m - TILES // 2)
                        if un > 0 and j == CLOSE_AT + 5:
                            invert(unit - 1)
                        if un > 0 and j == CLOSE_AT + 9:
                            normalize(unit - 1, un - 1)
                        c, h = divmod(j - 4, HG)
                        if POOL_CHUNKS < c < POOL_CHUNKS + DVE_CHUNKS:
                            add(c, h)
                    for j in range(TILES, TILES + 4):
                        c, h = divmod(j - 4, HG)
                        if POOL_CHUNKS < c < POOL_CHUNKS + DVE_CHUNKS:
                            add(c, h)
                invert(b * BU + BU - 1)
                normalize(b * BU + BU - 1, BU - 1)

        @block.scalar
        def _(act):
            def row_of_max(unit, h):
                act.wait_ge(max_turned, unit * HG + h + 1)
                act.wait_ge(max_in[h], unit * 16)
                nc.scalar.copy(max_row[:, h, :], ps_misc[0:QT, 0:P]).then_inc(max_row_done, 1)

            for h in range(HG):
                row_of_max(0, h)
            with act.Fori(0, B) as b:
                for un in range(BU):
                    unit = b * BU + un

                    def free(j):
                        act.wait_ge(pv_done, unit * TILES + j - RING + 1)
                        c, h = divmod(j - RING, HG)
                        if c < 0:
                            if un == 0:
                                act.wait_ge(z_done, unit)
                            elif c + NC >= POOL_CHUNKS + DVE_CHUNKS:
                                act.wait_ge(z_done, unit)
                            elif c + NC >= POOL_CHUNKS:
                                n = max(c + NC - POOL_CHUNKS, 1)
                                act.wait_ge(dve_added, unit * adds_dve + (n - 1 - (DVE_CHUNKS - 1)) * HG + h + 1)
                            else:
                                act.wait_ge(pool_added, unit * adds_pool)
                        elif c < POOL_CHUNKS:
                            act.wait_ge(pool_added, unit * adds_pool + (max(c, 1) - 1) * HG + h + 1)
                        elif c < POOL_CHUNKS + DVE_CHUNKS:
                            act.wait_ge(dve_added, unit * adds_dve + (max(c - POOL_CHUNKS, 1) - 1) * HG + h + 1)

                    def copy_acc(n):
                        act.wait_ge(pv_done, n * TILES)
                        act.wait_ge(o_turned, n - 1)
                        nc.scalar.copy(oT[:], ps_acc[:]).then_inc(oT_done, 1)

                    def copy_z(n):
                        act.wait_ge(z_done, n)
                        act.wait_ge(z_turned, n - 1)
                        nc.scalar.copy(zT[:], ps_misc[:]).then_inc(zT_done, 1)

                    def store(n, k):
                        g, u = k // NU, k % NU
                        act.wait_ge(o_done, n)
                        act.dma_start(out[bass.ds(b * S + u * UQ, UQ), g * P:(g + 1) * P]
                                      .rearrange("(t p) c -> p t c", p=P),
                                      o[:, k % 2].rearrange("p t h d -> p t (h d)")).then_inc(o_out[k % 2], 16)

                    for j in range(TILES):
                        act.wait_ge(scores, unit * TILES + j + 1)
                        if un > 0 or j >= RING:
                            free(j)
                        elif j == 0:
                            act.wait_ge(z_done, unit)
                        nc.scalar.activation(probs[:, j % RING], ps_s[:, j % 2], ACT.Exp, scale=SCALE
                                             ).then_inc(exp_done, 1)
                        if un > 0:
                            if j == PV_LAG:
                                copy_acc(unit)
                            if j == CLOSE_AT + 2:
                                copy_z(unit)
                            if j == CLOSE_AT + 14:
                                store(unit, un - 1)
                        if j in MAX_AT:
                            row_of_max(unit + 1, MAX_AT.index(j))
                copy_acc(b * BU + BU)
                copy_z(b * BU + BU)
                store(b * BU + BU, BU - 1)
            for k in range(2):
                act.wait_ge(o_out[k], B * BU // 2 * 16)

        @block.tensor
        def _(pe):
            def score_for_max(unit, un, m):
                h, t, c = m // (4 * QT), m // 4 % QT, m % 4
                g = un % BU // NU
                if m % 2 == 0:
                    p = unit * (TILES // 2) + m // 2
                    if not (isinstance(unit, int) and p < 2):
                        pe.wait_ge(part_max_done, p - 1)
                last = nc.tensor.matmul(ps_max[:, m // 2 % 2, m % 2], qs[0:STACK, un % NQB, h, t * P:(t + 1) * P],
                                        ks[0:STACK, g, h, c * 512:(c + 1) * 512], start=True, stop=True)
                if m % 2 == 1:
                    last.then_inc(max_scores, 1)

            def turn_max(unit, h, first=False):
                pe.wait_ge(neg_max_done, unit * HG + h + 1)
                nc.tensor.transpose(ps_misc[0:QT, 0:P], neg_max[:, h], ident[:]).then_inc(max_turned, 1)

            pe.wait_ge(consts, 2)
            pe.wait_ge(ones_row, 1)
            pe.wait_ge(q_in[0], 48)
            pe.wait_ge(k_in[0], 48)
            for m in range(TILES):
                score_for_max(0, 0, m)
            pe.wait_ge(q_in[1], 48)
            for h in range(HG):
                if h > 0:
                    pe.wait_ge(max_row_done, h)
                turn_max(0, h)
            for m in range(LEAD):
                score_for_max(1, 1, m)

            with pe.Fori(0, B) as b:
                for un in range(BU):
                    unit = b * BU + un
                    g, u = un // NU, un % NU

                    def pv(n, k, j):
                        c, h = divmod(j, HG)
                        pe.wait_ge(exp_done, n * TILES + j + 1)
                        if j == 0:
                            pe.wait_ge(oT_done, n)
                        nc.tensor.matmul(ps_acc[h * DH:(h + 1) * DH, :], v[:, k // NU, c, h * DH:(h + 1) * DH],
                                         probs[:, j % RING], start=(c == 0), stop=(c == NC - 1)).then_inc(pv_done, 1)

                    def sum_keys(n, k):
                        pe.wait_ge(pool_added, n * adds_pool + adds_pool)
                        pe.wait_ge(dve_added, n * adds_dve + adds_dve)
                        parts = [pool_sum[:, k % 2], dve_sum[:, k % 2]]
                        count = len(parts) + RAW
                        for i in range(count):
                            for h in range(HG):
                                if i < len(parts):
                                    src = parts[i][:, h]
                                else:
                                    src = probs[:, ((NC - RAW + i - len(parts)) * HG + h) % RING]
                                last = nc.tensor.matmul(ps_misc[h * DH:(h + 1) * DH, :], ones[:, 0:DH], src,
                                                        start=(i == 0), stop=(i == count - 1))
                        last.then_inc(z_done, 1)

                    def turn_z(n):
                        pe.wait_ge(zT_done, n)
                        for t in range(QT):
                            last = nc.tensor.transpose(ps_misc[:, t * P:(t + 1) * P], zT[:, t * P:(t + 1) * P], ident[:])
                        last.then_inc(z_turned, 1)

                    def turn_o(n):
                        pe.wait_ge(rz_done, n)
                        pe.wait_ge(oT_done, n)
                        for t in range(QT):
                            last = nc.tensor.transpose(ps_misc[:, t * P:(t + 1) * P], oT[:, t * P:(t + 1) * P], ident[:])
                        last.then_inc(o_turned, 1)

                    if u == 0:
                        pe.wait_ge(v_in[g], b * 16 + 16)
                    pvs = []
                    for j in range(TILES):
                        c, h = divmod(j, HG)
                        if j < HG:
                            pe.wait_ge(max_in[h], unit * 16 + 16)
                        pe.wait_ge(exp_done, unit * TILES + j - 1) if j > 1 or un > 0 else pe.wait_ge(exp_done, unit * TILES)
                        nc.tensor.matmul(ps_s[:, j % 2], ks[:, g, h, c * P:(c + 1) * P], qs[:, un % NQB, h, :],
                                         start=True, stop=True).then_inc(scores, 1)
                        m = j + LEAD
                        if m == TILES:
                            k2 = (un + 2) % NQB
                            n2 = un + 2
                            pe.wait_ge(q_in[k2], (b * (BU // NQB) + n2 // NQB + 1) * 48)
                            if n2 % NU == 0:
                                pe.wait_ge(k_in[n2 // NU % NG], (b + n2 // BU + 1) * 48)
                        if m < TILES:
                            score_for_max(unit + 1, un + 1, m)
                        else:
                            score_for_max(unit + 2, un + 2, m - TILES)
                        if j >= PV_LAG:
                            pv(unit, un, j - PV_LAG)
                        elif un > 0:
                            pv(unit - 1, un - 1, TILES - PV_LAG + j)
                        if un > 0:
                            if j == CLOSE_AT:
                                pe.wait_ge(max_row_done, unit * HG + HG)
                                sum_keys(unit - 1, un - 1)
                            if j == CLOSE_AT + 4:
                                turn_z(unit)
                            if j == CLOSE_AT + 7:
                                turn_o(unit)
                        if j in MAX_AT:
                            i = MAX_AT.index(j)
                            if i == 0:
                                pe.wait_ge(o_done, unit)
                            else:
                                pe.wait_ge(max_row_done, (unit + 1) * HG + i)
                            turn_max(unit + 1, i)
                for j in range(TILES - PV_LAG, TILES):
                    pv(b * BU + BU - 1, BU - 1, j)
                pe.wait_ge(max_row_done, (b * BU + BU) * HG + HG)
                sum_keys(b * BU + BU - 1, BU - 1)
                turn_z(b * BU + BU)
                turn_o(b * BU + BU)


CLOSE_AT = 10
MAX_AT = (26, 30, 36, 54)


def macaron_block(nc, x, qU, qVt, qb, kU, kVt, kb, vU, vVt, vb, w_router, w_qkvT, w_outT, g1, g2, w1T, w2T, w3T,
                  out):
    after_ffn = nc.dram_tensor("after_ffn", [B * S, D], F32).ap()
    attention = nc.dram_tensor("attention", [B * S, D], F32).ap()
    scores = nc.dram_tensor("router_scores", [P, P], F32).ap()
    qk = nc.dram_tensor("qk_parts", [B, 2, 2 * NG, P, S], F32).ap()
    v_dram = nc.dram_tensor("v_tokens", [B * S, D], F32).ap()
    ffn_weights = (w_qkvT, w_outT, g1, g2, w1T, w2T, w3T)
    with nc.sbuf_tensor("picked", [P, B], U32) as picked:
        score_pass(nc, "s1", x, None, w_router, after_ffn, scores)
        pick_tokens(nc, "t1", scores, picked[:])
        routed_ffn(nc, "f1", x, None, picked[:], *ffn_weights, after_ffn)
        project(nc, "pr", after_ffn, [(qU, qVt), (kU, kVt), (vU, vVt)], [qb, kb], vb, qk, v_dram)
        attend(nc, "at", qk, v_dram, attention)
        score_pass(nc, "s2", after_ffn, attention, w_router, out, scores)
        pick_tokens(nc, "t2", scores, picked[:])
        routed_ffn(nc, "f2", after_ffn, attention, picked[:], *ffn_weights, out)


def kernel(L0_attn_x, L0_attn_Uq, L0_attn_Vq, L0_attn_bq, L0_attn_Uk, L0_attn_Vk, L0_attn_bk, L0_attn_Uv, L0_attn_Vv,
           L0_attn_bv, L0_ffn_w_router, L0_ffn_W_qkv, L0_ffn_W_out, L0_ffn_g1, L0_ffn_g2, L0_ffn_W1, L0_ffn_W2,
           L0_ffn_W3):
    import numpy as np
    import concourse.bacc as bacc
    from concourse.bass_utils import run_bass_kernel_spmd

    def columns(a):
        return np.ascontiguousarray(np.asarray(a).reshape(-1, P).T)

    def turned(a):
        return np.ascontiguousarray(np.swapaxes(np.asarray(a), -1, -2))

    arrays = {
        "x": np.ascontiguousarray(np.asarray(L0_attn_x).reshape(B * S, D)),
        "qU": turned(L0_attn_Uq), "qV": np.ascontiguousarray(L0_attn_Vq), "qb": columns(L0_attn_bq),
        "kU": turned(L0_attn_Uk), "kV": np.ascontiguousarray(L0_attn_Vk), "kb": columns(L0_attn_bk),
        "vU": turned(L0_attn_Uv), "vV": np.ascontiguousarray(L0_attn_Vv),
        "vb": np.ascontiguousarray(np.asarray(L0_attn_bv).reshape(D)),
        "w_router": np.ascontiguousarray(L0_ffn_w_router),
        "w_qkvT": turned(L0_ffn_W_qkv), "w_outT": turned(L0_ffn_W_out),
        "g1": columns(L0_ffn_g1), "g2": columns(L0_ffn_g2),
        "w1T": turned(L0_ffn_W1), "w2T": turned(L0_ffn_W2), "w3T": turned(L0_ffn_W3),
    }
    nc = bacc.Bacc("TRN2", target_bir_lowering=False, num_devices=1)
    args = [nc.dram_tensor(f"in_{n}", a.shape, mybir.dt.from_np(a.dtype), kind="ExternalInput").ap()
            for n, a in arrays.items()]
    out = nc.dram_tensor("out", [B * S, D], F32, kind="ExternalOutput").ap()
    macaron_block(nc, *args, out)
    result = run_bass_kernel_spmd(nc, [{f"in_{n}": a for n, a in arrays.items()}], core_ids=[0])
    return result.results[0]["out"].reshape(B, S, D)
```

```python
from contextlib import ExitStack, contextmanager

import concourse.bass as bass
from concourse import mybir

P = 128
F32 = mybir.dt.float32
F32R = mybir.dt.float32r
U32 = mybir.dt.uint32
I32 = mybir.dt.int32
ALU = mybir.AluOpType
ACT = mybir.ActivationFunctionType
AX = mybir.AxisListType

B, S, D = 8, 2048, 256
T = S // P
H, DH = 8, 32
HG = P // DH
NG = H // HG
CAP = 128
FH, FD = 16, 16
DFF = 682
DFF_HALF = DFF // 2
DFF_TILES = (DFF + P - 1) // P
LN_EPS = 1e-5
RMS_EPS = 1e-6
LOWEST = -3.0e38


class Chain:

    def __init__(self, engine, semaphore, base=0):
        self.engine, self.semaphore, self.base, self.n = engine, semaphore, base, 0

    def step(self, instruction):
        self.n += 1
        instruction.then_inc(self.semaphore, 1)
        self.engine.wait_ge(self.semaphore, self.base + self.n)
        return instruction


@contextmanager
def cleared_semaphores(nc):
    used = []
    yield used
    nc.clear_and_free_semaphores(used)
    nc.all_engine_barrier()


def score_pass(nc, tag, x, add, w_router, y, scores):
    adding = add is not None
    with ExitStack() as ctx:
        used = ctx.enter_context(cleared_semaphores(nc))

        def sb(name, shape, dt=F32):
            return ctx.enter_context(nc.sbuf_tensor(f"{tag}_{name}", shape, dt))

        def sem(name):
            handle = nc.alloc_semaphore(f"{tag}_{name}")
            used.append(handle)
            return handle

        xb = sb("x", [P, 2, T, D])
        ab = sb("add", [P, 2, T, D]) if adding else None
        yb = sb("y", [P, 2, T, D])
        w = sb("w", [P, D])
        wsum = sb("wsum", [P, 1])
        junk = sb("junk", [P, 4, D])
        stats = sb("stats", [P, 2, T, 6])
        sm = sb("small", [P, 2, 12, T])
        sall = sb("sall", [P, B, T])
        sT = sb("sT", [P, P])
        ones = sb("ones", [P, P])
        ident = sb("ident", [P, P])
        pt = ctx.enter_context(nc.psum_tensor(f"{tag}_pt", [P, P], F32))

        w_in = sem("w_in")
        x_in = [sem(f"x_in{i}") for i in range(2)]
        a_in = [sem(f"a_in{i}") for i in range(2)]
        added = sem("added")
        dve_own = sem("dve_own")
        var_ready = sem("var_ready")
        std_ready = sem("std_ready")
        affine_ready = sem("affine_ready")
        products_done = sem("products_done")
        stats_done = sem("stats_done")
        y_done = sem("y_done")
        y_out = [sem(f"y_out{i}") for i in range(2)]
        id_ready = sem("id_ready")
        scores_done = sem("scores_done")
        transposed = sem("transposed")
        sT_done = sem("sT_done")
        s_out = sem("s_out")

        block = ctx.enter_context(nc.Block())

        @block.sync
        def _(sp):
            sp.dma_start(w[:], w_router.partition_broadcast(P)).then_inc(w_in, 16)

            def load(i, k):
                b = 2 * i + k
                src = x[bass.ds(b * S, S), :].rearrange("(t p) d -> p t d", p=P)
                sp.dma_start(xb[:, k], src).then_inc(x_in[k], 16)
                if adding:
                    src = add[bass.ds(b * S, S), :].rearrange("(t p) d -> p t d", p=P)
                    sp.dma_start(ab[:, k], src).then_inc(a_in[k], 16)

            for k in range(2):
                load(0, k)
            with sp.Fori(1, B // 2) as i:
                for k in range(2):
                    sp.wait_ge(products_done, ((i - 1) * 2 + k + 1) * T)
                    sp.wait_ge(y_done, (i - 1) * 2 + k + 1)
                    load(i, k)

        @block.gpsimd
        def _(pool):
            nc.gpsimd.memset(ones[:], 1.0).then_inc(id_ready, 1)
            pool.wait_ge(id_ready, 1)
            nc.gpsimd.affine_select(out=ident[:], in_=ones[:], compare_op=ALU.is_equal, fill=0.0, base=0,
                                    pattern=[[-1, P]], channel_multiplier=1).then_inc(id_ready, 1)
            if adding:
                with pool.Fori(0, B // 2) as i:
                    for k in range(2):
                        pool.wait_ge(x_in[k], i * 16 + 16)
                        pool.wait_ge(a_in[k], i * 16 + 16)
                        for q in range(4):
                            t4 = slice(4 * q, 4 * q + 4)
                            last = nc.gpsimd.tensor_tensor(xb[:, k, t4], xb[:, k, t4], ab[:, k, t4], ALU.add)
                            last.then_inc(added, 1)

        @block.vector
        def _(dve):
            dve.wait_ge(w_in, 16)
            own = Chain(dve, dve_own)
            own.step(nc.vector.reduce_sum(wsum[:], w[:], AX.X))
            with dve.Fori(0, B // 2) as i:
                own = Chain(dve, dve_own, i * 28 + 1)
                for k in range(2):
                    if not adding:
                        dve.wait_ge(x_in[k], i * 16 + 16)
                    v = [sm[:, k, n, :] for n in range(12)]
                    for t in range(T):
                        if adding and t % 4 == 0:
                            dve.wait_ge(added, i * 8 + 4 * k + t // 4 + 1)
                        nc.vector.bn_stats(stats[:, k, t, :], xb[:, k, t, :]).then_inc(stats_done, 1)
                        if t >= 4:
                            dve.wait_ge(products_done, (i * 2 + k) * T + t - 3)
                        nc.vector.tensor_tensor_reduce(out=junk[:, t % 4, :], in0=xb[:, k, t, :], in1=w[:], scale=1.0,
                                                       scalar=0.0, op0=ALU.mult, op1=ALU.add,
                                                       accum_out=v[11][:, t:t + 1]).then_inc(products_done, 1)
                    dve.wait_ge(stats_done, (i * 2 + k + 1) * T)
                    dve.wait_ge(products_done, (i * 2 + k + 1) * T)
                    me, m2e, mo, m2o = (stats[:, k, :, n] for n in (1, 2, 4, 5))
                    own.step(nc.vector.tensor_tensor(v[0], me, mo, ALU.add))
                    own.step(nc.vector.tensor_tensor(v[1], me, mo, ALU.subtract))
                    own.step(nc.vector.tensor_tensor(v[2], m2e, m2o, ALU.add))
                    own.step(nc.vector.scalar_tensor_tensor(v[3], v[1], 0.25, v[1], ALU.mult, ALU.mult))
                    own.step(nc.vector.tensor_scalar(v[4], v[2], 1.0 / D, LN_EPS, ALU.mult, ALU.add))
                    nc.vector.tensor_tensor(v[5], v[3], v[4], ALU.add).then_inc(var_ready, 1)
                    dve.wait_ge(std_ready, i * 2 + k + 1)
                    own.step(nc.vector.reciprocal(v[7], v[6]))
                    own.step(nc.vector.tensor_tensor(v[8], v[7], v[7], ALU.mult))
                    own.step(nc.vector.tensor_tensor(v[8], v[8], v[5], ALU.mult))
                    own.step(nc.vector.tensor_scalar(v[8], v[8], -0.5, 1.5, ALU.mult, ALU.add))
                    own.step(nc.vector.tensor_tensor(v[9], v[7], v[8], ALU.mult))
                    own.step(nc.vector.scalar_tensor_tensor(v[10], v[0], 0.5, v[9], ALU.mult, ALU.mult))
                    own.step(nc.vector.tensor_scalar(v[0], v[9], 0.5, 1.0, ALU.mult, ALU.add))
                    nc.vector.tensor_scalar(v[1], v[10], -0.5, None, ALU.mult).then_inc(affine_ready, 1)
                    own.step(nc.vector.tensor_tensor(v[2], v[11], v[9], ALU.mult))
                    own.step(nc.vector.tensor_scalar(v[3], v[10], wsum[:], None, ALU.mult))
                    nc.vector.tensor_tensor(sall[:, bass.ds(i * 2 + k, 1), :].rearrange("p a t -> p (a t)"),
                                            v[2], v[3], ALU.subtract).then_inc(scores_done, 1)

        @block.scalar
        def _(act):
            with act.Fori(0, B // 2) as i:
                for k in range(2):
                    act.wait_ge(var_ready, i * 2 + k + 1)
                    nc.scalar.activation(sm[:, k, 6, :], sm[:, k, 5, :], ACT.Sqrt).then_inc(std_ready, 1)
                    act.wait_ge(affine_ready, i * 2 + k + 1)
                    act.wait_ge(y_out[k], i * 16)
                    for t in range(T):
                        last = nc.scalar.activation(yb[:, k, t, :], xb[:, k, t, :], ACT.Identity,
                                                    scale=sm[:, k, 0, t:t + 1], bias=sm[:, k, 1, t:t + 1])
                    last.then_inc(y_done, 1)
                    act.wait_ge(y_done, i * 2 + k + 1)
                    act.dma_start(y[bass.ds((i * 2 + k) * S, S), :].rearrange("(t p) d -> p t d", p=P),
                                  yb[:, k]).then_inc(y_out[k], 16)
            act.wait_ge(transposed, 1)
            nc.scalar.copy(sT[:], pt[:]).then_inc(sT_done, 1)
            act.wait_ge(sT_done, 1)
            act.dma_start(scores, sT[:]).then_inc(s_out, 16)
            act.wait_ge(s_out, 16)
            for k in range(2):
                act.wait_ge(y_out[k], 16 * B // 2)

        @block.tensor
        def _(pe):
            pe.wait_ge(id_ready, 2)
            pe.wait_ge(scores_done, B)
            nc.tensor.transpose(pt[:], sall[:].rearrange("p b t -> p (b t)"), ident[:]).then_inc(transposed, 1)


def pick_tokens(nc, tag, scores, picked):
    with ExitStack() as ctx:
        used = ctx.enter_context(cleared_semaphores(nc))

        def sb(name, shape, dt=F32):
            return ctx.enter_context(nc.sbuf_tensor(f"{tag}_{name}", shape, dt))

        def sem(name):
            handle = nc.alloc_semaphore(f"{tag}_{name}")
            used.append(handle)
            return handle

        sc = sb("sc", [B, S])
        top = sb("top", [B, CAP])
        index = sb("index", [B, CAP], U32)
        indexf = sb("indexf", [B, CAP])
        ones = sb("ones", [B, B])
        ident = sb("ident", [B, B])
        first_row = sb("first_row", [P, B])
        first_row_i = sb("first_row_i", [P, B], I32)
        pt = ctx.enter_context(nc.psum_tensor(f"{tag}_pt", [P, B], F32))
        loaded = sem("loaded")
        own_done = sem("own")
        consts = sem("consts")
        indices_done = sem("indices_done")
        transposed = sem("transposed")
        picked_done = sem("picked_done")

        block = ctx.enter_context(nc.Block())

        @block.sync
        def _(sp):
            sp.dma_start(sc[:], scores.rearrange("(b t) p -> b (t p)", b=B)).then_inc(loaded, 16)

        @block.gpsimd
        def _(pool):
            nc.gpsimd.memset(ones[:], 1.0).then_inc(consts, 1)
            nc.gpsimd.iota(first_row_i[:], pattern=[[S, B]], base=0, channel_multiplier=0).then_inc(consts, 1)
            pool.wait_ge(consts, 2)
            nc.gpsimd.affine_select(out=ident[:], in_=ones[:], compare_op=ALU.is_equal, fill=0.0, base=0,
                                    pattern=[[-1, B]], channel_multiplier=1).then_inc(consts, 1)
            nc.gpsimd.tensor_copy(first_row[:], first_row_i[:]).then_inc(consts, 1)

        @block.vector
        def _(dve):
            own = Chain(dve, own_done)
            dve.wait_ge(loaded, 16)
            for r in range(CAP // 8):
                eight = slice(8 * r, 8 * r + 8)
                own.step(nc.vector.max(top[:, eight], sc[:]))
                own.step(nc.vector.max_index(index[:, eight], top[:, eight], sc[:]))
                if r < CAP // 8 - 1:
                    own.step(nc.vector.match_replace(sc[:], top[:, eight], sc[:], LOWEST))
            nc.vector.tensor_copy(indexf[:], index[:]).then_inc(indices_done, 1)
            dve.wait_ge(transposed, 1)
            dve.wait_ge(consts, 4)
            nc.vector.tensor_tensor(picked, pt[:], first_row[:], ALU.add).then_inc(picked_done, 1)
            dve.wait_ge(picked_done, 1)

        @block.tensor
        def _(pe):
            pe.wait_ge(consts, 4)
            pe.wait_ge(indices_done, 1)
            nc.tensor.transpose(pt[:], indexf[:], ident[:]).then_inc(transposed, 1)


def routed_ffn(nc, tag, x, add, picked, w_qkvT, w_outT, g1, g2, w1T, w2T, w3T, y):
    adding = add is not None
    NB = 4
    ROUNDS = B // NB
    NC = D // P
    PAIRS = P // (2 * FD)
    GH = P // FD
    with ExitStack() as ctx:
        used = ctx.enter_context(cleared_semaphores(nc))

        def sb(name, shape, dt=F32):
            return ctx.enter_context(nc.sbuf_tensor(f"{tag}_{name}", shape, dt))

        def sem(name):
            handle = nc.alloc_semaphore(f"{tag}_{name}")
            used.append(handle)
            return handle

        wqkv = sb("wqkv", [P, NC, 3 * D])
        wout = sb("wout", [P, NC, D])
        w1 = sb("w1", [P, NC, DFF])
        w2 = sb("w2", [P, NC, DFF])
        w3 = sb("w3", [P, DFF_TILES, D])
        gain = sb("gain", [P, 2, NC])
        ones = sb("ones", [P, P])
        zeros = sb("zeros", [P, P])
        ident = sb("ident", [P, P])
        causal = sb("causal", [P, P])
        head_half = sb("head_half", [P, GH])
        head_of = sb("head_of", [P, GH])
        parity = sb("parity", [P, 2])
        xs = sb("xs", [P, NB, D])
        ads = sb("ads", [P, NB, D]) if adding else None
        chosen = sb("chosen", [P, NB], U32)
        stats = sb("stats", [P, NB, 6])
        sm = sb("small", [P, 16, NB])
        xh = sb("xh", [P, NB, D])
        hn = sb("hn", [P, NB, D])
        hT = sb("hT", [P, NC, NB, P])
        qT = sb("qT", [P, NC, NB, P])
        v = sb("v", [P, NB, D])
        kspread = sb("kspread", [P, NB, NC, GH, P])
        att = sb("att", [P, NB, FH, P])
        rowmax = sb("rowmax", [P, NB, FH])
        rowsum = sb("rowsum", [P, NB, FH])
        attT = sb("attT", [P, 2, FH, P])
        odd = sb("odd", [P, 2, NC, P])
        oT = sb("oT", [P, NC, NB, P])
        xr = sb("xr", [P, NB, D])
        sq = sb("sq", [P, NB, D])
        sig = sb("sig", [P, 2, DFF])
        act1 = sb("act1", [P, 2, DFF])
        gated = sb("gated", [P, 2, DFF])
        gatedT = sb("gatedT", [P, 2, DFF_TILES, P])
        proc = sb("proc", [P, NB, D])
        row = sb("row", [P, NB, D])
        ps = ctx.enter_context(nc.psum_tensor(f"{tag}_ps", [P, 8, 512], F32))

        weights_in = sem("weights_in")
        consts = sem("consts")
        x_in = [sem(f"x_in{s}") for s in range(NB)]
        chosen_done = sem("chosen_done")
        rows_ready = sem("rows_ready")
        dve_own = sem("dve_own")
        var_ready = sem("var_ready")
        std_ready = sem("std_ready")
        rstd_ready = sem("rstd_ready")
        ms_ready = sem("ms_ready")
        rms_ready = sem("rms_ready")
        scale_ready = sem("scale_ready")
        xh_done = sem("xh_done")
        hn_done = sem("hn_done")
        h_turned = sem("h_turned")
        hT_done = sem("hT_done")
        qk_done = sem("qk_done")
        v_done = sem("v_done")
        qT_copied = sem("qT_copied")
        v_copied = sem("v_copied")
        spread_done = sem("spread_done")
        scores_done = sem("scores_done")
        max_done = sem("max_done")
        shifted_done = sem("shifted_done")
        exp_done = sem("exp_done")
        recip_done = sem("recip_done")
        probs_done = sem("probs_done")
        probs_turned = sem("probs_turned")
        probsT_copied = sem("probsT_copied")
        pv_done = sem("pv_done")
        oT_done = sem("oT_done")
        proj_done = sem("proj_done")
        xr_done = sem("xr_done")
        sq_done = sem("sq_done")
        ms2_ready = sem("ms2_ready")
        std2_ready = sem("std2_ready")
        r2_ready = sem("r2_ready")
        h2_done = sem("h2_done")
        h2_turned = sem("h2_turned")
        h2T_done = sem("h2T_done")
        up_done = sem("up_done")
        tanh_done = sem("tanh_done")
        gated_done = sem("gated_done")
        gated_turned = sem("gated_turned")
        gatedT_done = sem("gatedT_done")
        down_done = sem("down_done")
        row_done = sem("row_done")
        row_out = sem("row_out")
        scatter_turn = sem("scatter_turn")
        gather_turn = sem("gather_turn")

        BANK_H = 4
        BANK_K, BANK_Q = 4, 6
        BANK_V = 0
        BANK_S = 0
        BANK_PT = 4
        BANK_O = 6
        BANK_W = 0
        BANK_H2 = 2

        def bank_up(s):
            return 4 * ((s + 1) % 2)

        block = ctx.enter_context(nc.Block())

        @block.sync
        def _(sp):
            sp.dma_start(wqkv[:], w_qkvT.rearrange("(c p) n -> p c n", p=P)).then_inc(weights_in, 16)
            sp.dma_start(wout[:], w_outT.rearrange("(c p) n -> p c n", p=P)).then_inc(weights_in, 16)
            sp.dma_start(w1[:], w1T.rearrange("(c p) n -> p c n", p=P)).then_inc(weights_in, 16)
            sp.dma_start(w2[:], w2T.rearrange("(c p) n -> p c n", p=P)).then_inc(weights_in, 16)
            full = DFF // P
            sp.dma_start(w3[:, 0:full, :], w3T[0:full * P, :].rearrange("(c p) n -> p c n", p=P)
                         ).then_inc(weights_in, 16)
            sp.dma_start(w3[0:DFF - full * P, full, :], w3T[full * P:DFF, :]).then_inc(weights_in, 16)
            sp.dma_start(gain[:, 0, :], g1).then_inc(weights_in, 16)
            sp.dma_start(gain[:, 1, :], g2).then_inc(weights_in, 16)
        WEIGHTS = 8 * 16

        @block.gpsimd
        def _(pool):
            own = Chain(pool, consts)
            own.step(nc.gpsimd.memset(ones[:], 1.0))
            own.step(nc.gpsimd.memset(zeros[:], 0.0))
            nc.gpsimd.affine_select(out=ident[:], in_=ones[:], compare_op=ALU.is_equal, fill=0.0, base=0,
                                    pattern=[[-1, P]], channel_multiplier=1).then_inc(consts, 1)
            nc.gpsimd.affine_select(out=causal[:], in_=zeros[:], compare_op=ALU.is_ge, fill=-1e30, base=0,
                                    pattern=[[-1, P]], channel_multiplier=1).then_inc(consts, 1)
            nc.gpsimd.affine_select(out=head_half[:], in_=ones[:, 0:GH], compare_op=ALU.is_ge, fill=0.0, base=0,
                                    pattern=[[-FD, GH]], channel_multiplier=1).then_inc(consts, 1)
            pool.wait_ge(consts, 5)
            nc.gpsimd.affine_select(out=head_of[:], in_=head_half[:], compare_op=ALU.is_ge, fill=0.0, base=FD - 1,
                                    pattern=[[FD, GH]], channel_multiplier=-1).then_inc(consts, 1)
            with pool.Fori(0, ROUNDS) as i:
                def at(s):
                    return i * NB + s + 1

                pool.wait_ge(row_done, i * NB)
                nc.gpsimd.tensor_copy(chosen[:], picked[:, bass.ds(i * NB, NB)]).then_inc(chosen_done, 1)
                pool.wait_ge(chosen_done, i + 1)
                pool.sem_inc(gather_turn, 1)
                for s in range(NB):
                    index = chosen[:, s:s + 1]
                    nc.gpsimd.indirect_dma_start(
                        out=xs[:, s, :], out_offset=None, in_=x,
                        in_offset=bass.IndirectOffsetOnAxis(ap=index, axis=0)).then_inc(x_in[s], 16)
                    if adding:
                        nc.gpsimd.indirect_dma_start(
                            out=ads[:, s, :], out_offset=None, in_=add,
                            in_offset=bass.IndirectOffsetOnAxis(ap=index, axis=0)).then_inc(x_in[s], 16)
                if adding:
                    for s in range(NB):
                        pool.wait_ge(x_in[s], i * 32 + 32)
                        nc.gpsimd.tensor_tensor(xs[:, s, :], xs[:, s, :], ads[:, s, :],
                                                ALU.add).then_inc(rows_ready, 1)

                def shift(s):
                    pool.wait_ge(max_done, at(s))
                    nc.gpsimd.tensor_tensor(att[:, s], att[:, s], rowmax[:, s].unsqueeze(2).to_broadcast([P, FH, P]),
                                            ALU.subtract).then_inc(shifted_done, 1)

                def normalize(s):
                    pool.wait_ge(recip_done, at(s))
                    nc.gpsimd.tensor_tensor(att[:, s], att[:, s], rowsum[:, s].unsqueeze(2).to_broadcast([P, FH, P]),
                                            ALU.mult).then_inc(probs_done, 1)

                shift(0)
                for s in range(1, NB):
                    shift(s)
                    normalize(s - 1)
                normalize(NB - 1)
                for s in range(NB):
                    pool.wait_ge(row_done, at(s))
                    pool.sem_inc(scatter_turn, 1)
                    index = chosen[:, s:s + 1]
                    nc.gpsimd.indirect_dma_start(
                        out=y, out_offset=bass.IndirectOffsetOnAxis(ap=index, axis=0), in_=row[:, s, :],
                        in_offset=None).then_inc(row_out, 16)
                    pool.wait_ge(row_out, at(s) * 16)

        @block.vector
        def _(dve):
            dve.wait_ge(consts, 6)
            own = Chain(dve, dve_own)
            own.step(nc.vector.tensor_reduce(parity[:], head_of[:].rearrange("p (a two) -> p two a", two=2),
                                             AX.X, ALU.add))
            dve.wait_ge(weights_in, WEIGHTS)
            with dve.Fori(0, ROUNDS) as i:
                own = Chain(dve, dve_own, i * ROUND_STEPS + 1)

                def at(s):
                    return i * NB + s + 1

                def c(n):
                    return sm[:, n, :]

                def newton(r, var, scratch, out, done):
                    own.step(nc.vector.tensor_tensor(c(scratch), c(r), c(r), ALU.mult))
                    own.step(nc.vector.tensor_tensor(c(scratch), c(scratch), c(var), ALU.mult))
                    own.step(nc.vector.tensor_scalar(c(scratch), c(scratch), -0.5, 1.5, ALU.mult, ALU.add))
                    nc.vector.tensor_tensor(c(out), c(r), c(scratch), ALU.mult).then_inc(done, 1)
                    dve.wait_ge(done, i + 1)

                for s in range(NB):
                    if adding:
                        dve.wait_ge(rows_ready, at(s))
                    else:
                        dve.wait_ge(x_in[s], i * 16 + 16)
                    last = nc.vector.bn_stats(stats[:, s, :], xs[:, s, :])
                    own.step(last)
                me, m2e, mo, m2o = (stats[:, :, n] for n in (1, 2, 4, 5))
                own.step(nc.vector.tensor_tensor(c(0), me, mo, ALU.add))
                own.step(nc.vector.tensor_tensor(c(1), me, mo, ALU.subtract))
                own.step(nc.vector.tensor_tensor(c(2), m2e, m2o, ALU.add))
                own.step(nc.vector.scalar_tensor_tensor(c(1), c(1), 0.25, c(1), ALU.mult, ALU.mult))
                own.step(nc.vector.scalar_tensor_tensor(c(2), c(2), 1.0 / D, c(1), ALU.mult, ALU.add))
                nc.vector.tensor_scalar(c(3), c(2), LN_EPS, None, ALU.add).then_inc(var_ready, 1)
                dve.wait_ge(std_ready, i + 1)
                own.step(nc.vector.reciprocal(c(5), c(4)))
                newton(5, 3, 6, 7, rstd_ready)
                own.step(nc.vector.tensor_tensor(c(8), c(2), c(7), ALU.mult))
                own.step(nc.vector.tensor_tensor(c(8), c(8), c(7), ALU.mult))
                own.step(nc.vector.scalar_tensor_tensor(c(10), c(0), -0.5, c(7), ALU.mult, ALU.mult))
                nc.vector.tensor_scalar(c(8), c(8), RMS_EPS, None, ALU.add).then_inc(ms_ready, 1)
                dve.wait_ge(rms_ready, i + 1)
                own.step(nc.vector.reciprocal(c(5), c(9)))
                newton(5, 8, 6, 11, scale_ready)

                for s in range(NB):
                    for g in range(NC):
                        if s == 0 and g == 0:
                            dve.wait_ge(qk_done, i + 1)
                        last = nc.vector.tensor_tensor(
                            kspread[:, s, g],
                            ps[:, BANK_K + g, s * P:(s + 1) * P].unsqueeze(1).to_broadcast([P, GH, P]),
                            head_of[:].unsqueeze(2).to_broadcast([P, GH, P]), ALU.mult)
                    last.then_inc(spread_done, 1)
                for s in range(NB):
                    dve.wait_ge(scores_done, at(s))
                    own.step(nc.vector.tensor_tensor(
                        att[:, s], ps[:, BANK_S:BANK_S + 4, :].rearrange("p b (h k) -> p (b h) k", k=P),
                        causal[:].unsqueeze(1).to_broadcast([P, FH, P]), ALU.add))
                    nc.vector.reduce_max(rowmax[:, s], att[:, s], AX.X).then_inc(max_done, 1)
                for s in range(NB):
                    dve.wait_ge(exp_done, at(s))
                    own.step(nc.vector.reduce_sum(rowsum[:, s], att[:, s], AX.X))
                    nc.vector.reciprocal(rowsum[:, s], rowsum[:, s]).then_inc(recip_done, 1)
                for s in range(NB):
                    o = ps[:, BANK_O + s % 2, :].rearrange("p (g two t) -> p two g t", g=NC, two=2)
                    dve.wait_ge(pv_done, at(s))
                    own.step(nc.vector.tensor_scalar(odd[:, s % 2], o[:, 1], parity[:, 1:2], None, ALU.mult))
                    nc.vector.scalar_tensor_tensor(oT[:, :, s, :], o[:, 0], parity[:, 0:1], odd[:, s % 2],
                                                   ALU.mult, ALU.add).then_inc(oT_done, 1)
                for s in range(NB):
                    dve.wait_ge(proj_done, at(s))
                    nc.vector.tensor_tensor(xr[:, s, :], ps[:, BANK_W + s, 0:D], xh[:, s, :],
                                            ALU.add).then_inc(xr_done, 1)
                    dve.wait_ge(xr_done, at(s))
                    own.step(nc.vector.tensor_tensor_reduce(out=sq[:, s, :], in0=xr[:, s, :], in1=xr[:, s, :],
                                                            scale=1.0, scalar=0.0, op0=ALU.mult, op1=ALU.add,
                                                            accum_out=sm[:, 12, s:s + 1]))
                nc.vector.tensor_scalar(c(13), c(12), 1.0 / D, RMS_EPS, ALU.mult, ALU.add).then_inc(ms2_ready, 1)
                dve.wait_ge(std2_ready, i + 1)
                own.step(nc.vector.reciprocal(c(5), c(14)))
                newton(5, 13, 6, 15, r2_ready)
                def gate(s):
                    u = bank_up(s)
                    dve.wait_ge(tanh_done, at(s))
                    own.step(nc.vector.scalar_tensor_tensor(
                        act1[:, s % 2].rearrange("p (n f) -> p n f", n=2), sig[:, s % 2].rearrange("p (n f) -> p n f", n=2),
                        1.0, ps[:, u:u + 2, 0:DFF_HALF], ALU.add, ALU.mult))
                    if s >= 2:
                        dve.wait_ge(gated_turned, at(s - 2))
                    nc.vector.scalar_tensor_tensor(
                        gated[:, s % 2].rearrange("p (n f) -> p n f", n=2), act1[:, s % 2].rearrange("p (n f) -> p n f", n=2),
                        0.5, ps[:, u + 2:u + 4, 0:DFF_HALF], ALU.mult, ALU.mult).then_inc(gated_done, 1)

                def final_row(s):
                    u = bank_up(s)
                    dve.wait_ge(down_done, at(s))
                    own.step(nc.vector.tensor_tensor(proc[:, s, :], ps[:, u + 2, 0:D], xr[:, s, :], ALU.add))
                    nc.vector.scalar_tensor_tensor(row[:, s, :], proc[:, s, :], 0.5, xs[:, s, :],
                                                   ALU.mult, ALU.add).then_inc(row_done, 1)

                gate(0)
                gate(1)
                for s in range(NB):
                    final_row(s)
                    if s + 2 < NB:
                        gate(s + 2)
                assert own.n == ROUND_STEPS, own.n

        @block.scalar
        def _(act):
            act.wait_ge(weights_in, WEIGHTS)
            with act.Fori(0, ROUNDS) as i:
                def at(s):
                    return i * NB + s + 1

                act.wait_ge(var_ready, i + 1)
                nc.scalar.activation(sm[:, 4, :], sm[:, 3, :], ACT.Sqrt).then_inc(std_ready, 1)
                act.wait_ge(ms_ready, i + 1)
                nc.scalar.activation(sm[:, 9, :], sm[:, 8, :], ACT.Sqrt).then_inc(rms_ready, 1)
                act.wait_ge(scale_ready, i + 1)
                for s in range(NB):
                    nc.scalar.activation(xh[:, s, :], xs[:, s, :], ACT.Identity, scale=sm[:, 7, s:s + 1],
                                         bias=sm[:, 10, s:s + 1]).then_inc(xh_done, 1)
                for s in range(NB):
                    act.wait_ge(xh_done, at(s))
                    nc.scalar.activation(hn[:, s, :], xh[:, s, :], ACT.Copy, scale=sm[:, 11, s:s + 1]
                                         ).then_inc(hn_done, 1)
                act.wait_ge(h_turned, i + 1)
                for g in range(NC):
                    nc.scalar.activation(hT[:, g].rearrange("p s t -> p (s t)"), ps[:, BANK_H + g, :], ACT.Copy,
                                         scale=gain[:, 0, g:g + 1]).then_inc(hT_done, 1)
                act.wait_ge(qk_done, i + 1)
                for g in range(NC):
                    nc.scalar.copy(qT[:, g].rearrange("p s t -> p (s t)"), ps[:, BANK_Q + g, :]).then_inc(qT_copied, 1)
                act.wait_ge(v_done, i + 1)
                nc.scalar.copy(v[:].rearrange("p (b s) d -> p b (s d)", b=2),
                               ps[:, BANK_V:BANK_V + 2, :]).then_inc(v_copied, 1)
                for s in range(NB):
                    act.wait_ge(shifted_done, at(s))
                    nc.scalar.activation(att[:, s], att[:, s], ACT.Exp, scale=float(FD) ** -0.5).then_inc(exp_done, 1)
                for s in range(NB):
                    for half in range(2):
                        act.wait_ge(probs_turned, (i * NB + s) * 2 + half + 1)
                        if s >= 2 and half == 0:
                            act.wait_ge(pv_done, at(s - 2))
                        nc.scalar.copy(attT[:, s % 2, half * GH:(half + 1) * GH].rearrange("p (b h) t -> p b (h t)", b=2),
                                       ps[:, BANK_PT:BANK_PT + 2, :]).then_inc(probsT_copied, 1)
                act.wait_ge(ms2_ready, i + 1)
                nc.scalar.activation(sm[:, 14, :], sm[:, 13, :], ACT.Sqrt).then_inc(std2_ready, 1)
                act.wait_ge(r2_ready, i + 1)
                for s in range(NB):
                    nc.scalar.activation(hn[:, s, :], xr[:, s, :], ACT.Copy, scale=sm[:, 15, s:s + 1]
                                         ).then_inc(h2_done, 1)
                act.wait_ge(h2_turned, i + 1)
                for g in range(NC):
                    nc.scalar.activation(hT[:, g].rearrange("p s t -> p (s t)"), ps[:, BANK_H2 + g, :], ACT.Copy,
                                         scale=gain[:, 1, g:g + 1]).then_inc(h2T_done, 1)

                def tanh(s):
                    act.wait_ge(up_done, at(s))
                    u = bank_up(s)
                    if s >= 2:
                        act.wait_ge(gated_done, at(s - 2))
                    nc.scalar.activation(sig[:, s % 2].rearrange("p (n f) -> p n f", n=2), ps[:, u:u + 2, 0:DFF_HALF],
                                         ACT.Tanh, scale=0.5).then_inc(tanh_done, 1)

                def copy_gatedT(s):
                    u = bank_up(s)
                    act.wait_ge(gated_turned, at(s))
                    if s >= 2:
                        act.wait_ge(down_done, at(s - 2))
                    nc.scalar.copy(gatedT[:, s % 2, 0:4, :].rearrange("p a t -> p (a t)"), ps[:, u, :])
                    nc.scalar.copy(gatedT[:, s % 2, 4, :], ps[:, u + 1, 0:P])
                    nc.scalar.copy(gatedT[0:DFF - 5 * P, s % 2, 5, :], ps[0:DFF - 5 * P, u + 1, P:2 * P]
                                   ).then_inc(gatedT_done, 1)

                tanh(0)
                tanh(1)
                for s in range(NB):
                    copy_gatedT(s)
                    if s + 2 < NB:
                        tanh(s + 2)

        @block.tensor
        def _(pe):
            pe.wait_ge(weights_in, WEIGHTS)
            pe.wait_ge(consts, 6)
            with pe.Fori(0, ROUNDS) as i:
                def at(s):
                    return i * NB + s + 1

                for s in range(NB):
                    pe.wait_ge(hn_done, at(s))
                    if s == 0:
                        pe.wait_ge(row_done, i * NB)
                    for g in range(NC):
                        last = nc.tensor.transpose(ps[:, BANK_H + g, s * P:(s + 1) * P],
                                                   hn[:, s, g * P:(g + 1) * P], ident[:])
                last.then_inc(h_turned, 1)
                pe.wait_ge(hT_done, i * NC + NC)
                for s in range(NB):
                    for c in range(NC):
                        last = nc.tensor.matmul(ps[:, BANK_V + s // 2, (s % 2) * D:(s % 2 + 1) * D], hT[:, c, s, :],
                                                wqkv[:, c, 2 * D:3 * D], start=(c == 0), stop=(c == NC - 1))
                last.then_inc(v_done, 1)
                for which, bank in ((1, BANK_K), (0, BANK_Q)):
                    for g in range(NC):
                        for c in range(NC):
                            last = nc.tensor.matmul(ps[:, bank + g, :], wqkv[:, c, which * D + g * P:which * D + (g + 1) * P],
                                                    hT[:, c].rearrange("p s t -> p (s t)"), start=(c == 0),
                                                    stop=(c == NC - 1))
                last.then_inc(qk_done, 1)
                pe.wait_ge(qT_copied, i * NC + NC)
                pe.wait_ge(v_copied, i + 1)
                for s in range(NB):
                    pe.wait_ge(spread_done, at(s))
                    if s >= 1:
                        pe.wait_ge(max_done, at(s - 1))
                    for h4 in range(FH // 4):
                        g = h4 // 2
                        last = nc.tensor.matmul(ps[:, BANK_S + h4, :], qT[:, g, s, :],
                                                kspread[:, s, g, (h4 % 2) * 4:(h4 % 2) * 4 + 4].rearrange("p j t -> p (j t)"),
                                                start=True, stop=True)
                    last.then_inc(scores_done, 1)
                for s in range(NB):
                    pe.wait_ge(probs_done, at(s))
                    for half in range(2):
                        if s > 0 or half > 0:
                            pe.wait_ge(probsT_copied, (i * NB + s) * 2 + half)
                        for j in range(GH):
                            last = nc.tensor.transpose(ps[:, BANK_PT + j // 4, (j % 4) * P:(j % 4 + 1) * P],
                                                       att[:, s, half * GH + j, :], ident[:])
                        last.then_inc(probs_turned, 1)
                    for half in range(2):
                        pe.wait_ge(probsT_copied, (i * NB + s) * 2 + half + 1)
                        if s >= 2 and half == 0:
                            pe.wait_ge(oT_done, at(s - 2))
                        for j in (0, 2, 4, 6, 1, 3, 5, 7):
                            h = half * GH + j
                            pair = j // 2
                            base = (half * 2 + j % 2) * P
                            ch = half * P + pair * 2 * FD
                            last = nc.tensor.matmul(ps[pair * 32:pair * 32 + 32, BANK_O + s % 2, base:base + P],
                                                    v[:, s, ch:ch + 2 * FD], attT[:, s % 2, h, :], start=True, stop=True)
                    last.then_inc(pv_done, 1)
                for s in range(NB):
                    pe.wait_ge(oT_done, at(s))
                    for c in range(NC):
                        last = nc.tensor.matmul(ps[:, BANK_W + s, 0:D], oT[:, c, s, :],
                                                wout[:, c, :], start=(c == 0), stop=(c == NC - 1))
                    last.then_inc(proj_done, 1)
                for s in range(NB):
                    pe.wait_ge(h2_done, at(s))
                    for g in range(NC):
                        last = nc.tensor.transpose(ps[:, BANK_H2 + g, s * P:(s + 1) * P],
                                                   hn[:, s, g * P:(g + 1) * P], ident[:])
                last.then_inc(h2_turned, 1)
                pe.wait_ge(h2T_done, i * NC + NC)

                def up(s):
                    u = bank_up(s)
                    if s >= 2:
                        pe.wait_ge(row_done, at(s - 2))
                    for w, bank in ((w1, u), (w2, u + 2)):
                        for n in range(2):
                            for c in range(NC):
                                last = nc.tensor.matmul(ps[:, bank + n, 0:DFF_HALF], hT[:, c, s, :],
                                                        w[:, c, n * DFF_HALF:(n + 1) * DFF_HALF], start=(c == 0),
                                                        stop=(c == NC - 1))
                    last.then_inc(up_done, 1)

                def down(s):
                    u = bank_up(s)
                    pe.wait_ge(gated_done, at(s))
                    for f in range(DFF_TILES):
                        m = min(P, DFF - f * P)
                        last = nc.tensor.transpose(ps[0:m, u + f // 4, (f % 4) * P:(f % 4 + 1) * P],
                                                   gated[:, s % 2, f * P:f * P + m], ident[:])
                    last.then_inc(gated_turned, 1)
                    pe.wait_ge(gatedT_done, at(s))
                    for f in range(DFF_TILES):
                        m = min(P, DFF - f * P)
                        last = nc.tensor.matmul(ps[:, u + 2, 0:D], gatedT[0:m, s % 2, f, :], w3[0:m, f, :],
                                                start=(f == 0), stop=(f == DFF_TILES - 1))
                    last.then_inc(down_done, 1)

                up(0)
                up(1)
                for s in range(NB):
                    down(s)
                    if s + 2 < NB:
                        up(s + 2)


ROUND_STEPS = 48


def project(nc, tag, x, lowrank, biases, v_bias, qk, v_dram):
    with ExitStack() as ctx:
        used = ctx.enter_context(cleared_semaphores(nc))

        def sb(name, shape, dt=F32):
            return ctx.enter_context(nc.sbuf_tensor(f"{tag}_{name}", shape, dt))

        def sem(name):
            handle = nc.alloc_semaphore(f"{tag}_{name}")
            used.append(handle)
            return handle

        NQ = 4
        TQ = T // NQ
        facV = sb("facV", [P, 3, NG, P])
        facU = sb("facU", [P, 3, NG, P])
        w = sb("w", [P, 3, NG, P])
        bias = sb("bias", [P, 2, NG])
        vb = sb("vb", [P, D])
        ones = sb("ones", [P, P])
        ident = sb("ident", [P, P])
        xb = sb("x", [P, 2, T, D])
        stats = sb("stats", [P, T, 6])
        sm = sb("small", [P, 8, T])
        xT = sb("xT", [P, 2, NG, TQ * P])
        hi = sb("hi", [P, 2, 2 * NG, TQ * P], F32R)
        lo = sb("lo", [P, 2, 2 * NG, TQ * P], F32R)
        v = sb("v", [P, 2, TQ, D])
        pT = ctx.enter_context(nc.psum_tensor(f"{tag}_pT", [P, NG, 512], F32))
        pqk = ctx.enter_context(nc.psum_tensor(f"{tag}_pqk", [P, 2 * NG, 512], F32))
        pv = ctx.enter_context(nc.psum_tensor(f"{tag}_pv", [P, 2, 512], F32))

        consts = sem("consts")
        zeroed = sem("zeroed")
        factors_in = sem("factors_in")
        w_done = sem("w_done")
        w_copied = sem("w_copied")
        x_in = [sem(f"x_in{k}") for k in range(2)]
        stats_done = sem("stats_done")
        dve_own = sem("dve_own")
        var_ready = sem("var_ready")
        std_ready = sem("std_ready")
        affine_ready = sem("affine_ready")
        xh_done = sem("xh_done")
        turned = sem("turned")
        xT_copied = sem("xT_copied")
        qk_done = sem("qk_done")
        v_done = sem("v_done")
        hi_done = sem("hi_done")
        lo_done = sem("lo_done")
        v_copied = sem("v_copied")
        hi_out = [sem(f"hi_out{k}") for k in range(2)]
        lo_out = [sem(f"lo_out{k}") for k in range(2)]
        v_out = [sem(f"v_out{k}") for k in range(2)]
        FACTORS = 2 * 3 * H * 16 + 3 * 16
        OWN = 10

        block = ctx.enter_context(nc.Block())

        @block.gpsimd
        def _(pool):
            nc.gpsimd.memset(ones[:], 1.0).then_inc(consts, 1)
            pool.wait_ge(consts, 1)
            nc.gpsimd.affine_select(out=ident[:], in_=ones[:], compare_op=ALU.is_equal, fill=0.0, base=0,
                                    pattern=[[-1, P]], channel_multiplier=1).then_inc(consts, 1)

        @block.sync
        def _(sp):
            sp.wait_ge(zeroed, 2)
            for n, (u, vt) in enumerate(lowrank):
                for h in range(H):
                    r = (h % HG) * DH
                    sp.dma_start(facV[r:r + DH, n, h // HG, r:r + DH], vt[h]).then_inc(factors_in, 16)
                    sp.dma_start(facU[r:r + DH, n, h // HG, r:r + DH], u[h]).then_inc(factors_in, 16)
            for n in range(2):
                sp.dma_start(bias[:, n, :], biases[n]).then_inc(factors_in, 16)
            sp.dma_start(vb[:], v_bias.partition_broadcast(P)).then_inc(factors_in, 16)

            def load(i, k):
                src = x[bass.ds((i * 2 + k) * S, S), :].rearrange("(t p) d -> p t d", p=P)
                sp.dma_start(xb[:, k], src).then_inc(x_in[k], 16)

            def store(i, k, n):
                at = (i * 2 + k) * NQ + n + 1
                tok = slice(n * TQ * P, (n + 1) * TQ * P)
                dst = qk[bass.ds(i * 2 + k, 1)].rearrange("a part g c s -> part c (a g) s")
                sp.wait_ge(hi_done, at * 4)
                sp.dma_start(dst[0, :, :, tok], hi[:, n % 2].bitcast(F32)).then_inc(hi_out[n % 2], 16)
                sp.wait_ge(lo_done, at * 4)
                sp.dma_start(dst[1, :, :, tok], lo[:, n % 2].bitcast(F32)).then_inc(lo_out[n % 2], 16)
                sp.wait_ge(v_copied, at * 2)
                sp.dma_start(v_dram[bass.ds((i * 2 + k) * S + n * TQ * P, TQ * P), :]
                             .rearrange("(t p) d -> p t d", p=P), v[:, n % 2]).then_inc(v_out[n % 2], 16)

            load(0, 0)
            load(0, 1)
            with sp.Fori(0, B // 2 - 1) as i:
                for k in range(2):
                    for n in range(NQ):
                        store(i, k, n)
                    load(i + 1, k)
            for k in range(2):
                for n in range(NQ):
                    store(B // 2 - 1, k, n)
            for s in (*hi_out, *lo_out, *v_out):
                sp.wait_ge(s, B * NQ // 2 * 16)

        @block.vector
        def _(dve):
            nc.vector.memset(facV[:], 0.0).then_inc(zeroed, 1)
            nc.vector.memset(facU[:], 0.0).then_inc(zeroed, 1)
            dve.wait_ge(w_done, 1)
            nc.vector.tensor_copy(w[:, 0:2].rearrange("p n g c -> p (n g c)"), pT[:, 0, :]).then_inc(w_copied, 1)
            nc.vector.tensor_copy(w[:, 2].rearrange("p g c -> p (g c)"), pT[:, 1, 0:NG * P]).then_inc(w_copied, 1)
            with dve.Fori(0, B // 2) as i:
                for k in range(2):
                    b = i * 2 + k
                    own = Chain(dve, dve_own, b * OWN)
                    c = [sm[:, n, :] for n in range(8)]
                    dve.wait_ge(x_in[k], i * 16 + 16)
                    for t in range(T):
                        nc.vector.bn_stats(stats[:, t, :], xb[:, k, t, :]).then_inc(stats_done, 1)
                    dve.wait_ge(stats_done, (b + 1) * T)
                    dve.wait_ge(xh_done, b * T)
                    me, m2e, mo, m2o = (stats[:, :, n] for n in (1, 2, 4, 5))
                    own.step(nc.vector.tensor_tensor(c[0], me, mo, ALU.add))
                    own.step(nc.vector.tensor_tensor(c[1], me, mo, ALU.subtract))
                    own.step(nc.vector.tensor_tensor(c[2], m2e, m2o, ALU.add))
                    own.step(nc.vector.scalar_tensor_tensor(c[1], c[1], 0.25, c[1], ALU.mult, ALU.mult))
                    own.step(nc.vector.tensor_scalar(c[2], c[2], 1.0 / D, LN_EPS, ALU.mult, ALU.add))
                    nc.vector.tensor_tensor(c[3], c[1], c[2], ALU.add).then_inc(var_ready, 1)
                    dve.wait_ge(std_ready, b + 1)
                    own.step(nc.vector.reciprocal(c[5], c[4]))
                    own.step(nc.vector.tensor_tensor(c[6], c[5], c[5], ALU.mult))
                    own.step(nc.vector.tensor_tensor(c[6], c[6], c[3], ALU.mult))
                    own.step(nc.vector.tensor_scalar(c[6], c[6], -0.5, 1.5, ALU.mult, ALU.add))
                    own.step(nc.vector.tensor_tensor(c[6], c[5], c[6], ALU.mult))
                    nc.vector.scalar_tensor_tensor(c[7], c[0], -0.5, c[6], ALU.mult, ALU.mult
                                                   ).then_inc(affine_ready, 1)
                    for n in range(NQ):
                        at = b * NQ + n
                        dve.wait_ge(hi_done, at * 4)
                        if n >= 2:
                            dve.wait_ge(lo_out[n % 2], (i * 2 + k) * 32 + (n // 2) * 16)
                            dve.wait_ge(v_out[n % 2], (i * 2 + k) * 32 + (n // 2) * 16)
                        else:
                            dve.wait_ge(lo_out[n % 2], (i * 2 + k) * 32)
                            dve.wait_ge(v_out[n % 2], (i * 2 + k) * 32)
                        for m in range(2 * NG):
                            dve.wait_ge(hi_done, at * 4 + m + 1)
                            nc.vector.scalar_tensor_tensor(
                                lo[:, n % 2, m], pqk[:, m, :], bias[:, m // NG, m % NG:m % NG + 1],
                                hi[:, n % 2, m].bitcast(F32), ALU.add, ALU.subtract).then_inc(lo_done, 1)
                        dve.wait_ge(v_done, at + 1)
                        for m in range(2):
                            nc.vector.tensor_tensor(v[:, n % 2, 2 * m:2 * m + 2, :],
                                                    pv[:, m, :].rearrange("p (t d) -> p t d", t=2),
                                                    vb[:].unsqueeze(1).to_broadcast([P, 2, D]), ALU.add
                                                    ).then_inc(v_copied, 1)

        @block.scalar
        def _(act):
            act.wait_ge(factors_in, FACTORS)
            with act.Fori(0, B // 2) as i:
                for k in range(2):
                    b = i * 2 + k
                    act.wait_ge(var_ready, b + 1)
                    nc.scalar.activation(sm[:, 4, :], sm[:, 3, :], ACT.Sqrt).then_inc(std_ready, 1)
                    act.wait_ge(affine_ready, b + 1)

                    def normal(n):
                        for t in range(n * TQ, (n + 1) * TQ):
                            nc.scalar.activation(xb[:, k, t, :], xb[:, k, t, :], ACT.Identity,
                                                 scale=sm[:, 6, t:t + 1], bias=sm[:, 7, t:t + 1]).then_inc(xh_done, 1)

                    normal(0)
                    for n in range(NQ):
                        at = b * NQ + n
                        if n + 1 < NQ:
                            normal(n + 1)
                        act.wait_ge(turned, at + 1)
                        for g in range(NG):
                            nc.scalar.copy(xT[:, n % 2, g, :], pT[:, g, :]).then_inc(xT_copied, 1)
                        act.wait_ge(hi_out[n % 2], b * 32 + (n // 2) * 16)
                        for m in range(2 * NG):
                            act.wait_ge(qk_done, at * 4 + m + 1)
                            nc.scalar.activation(hi[:, n % 2, m], pqk[:, m, :], ACT.Identity,
                                                 bias=bias[:, m // NG, m % NG:m % NG + 1]).then_inc(hi_done, 1)

        @block.tensor
        def _(pe):
            pe.wait_ge(consts, 2)
            pe.wait_ge(factors_in, FACTORS)
            for n in range(3):
                for g in range(NG):
                    at = (n * NG + g) * P
                    last = nc.tensor.matmul(pT[:, at // 512, at % 512:at % 512 + P], facV[:, n, g, :],
                                            facU[:, n, g, :], start=True, stop=True)
            last.then_inc(w_done, 1)
            pe.wait_ge(w_copied, 2)
            with pe.Fori(0, B // 2) as i:
                for k in range(2):
                    b = i * 2 + k

                    def turn(n):
                        for t in range(TQ):
                            if t == 0 or n == 0:
                                pe.wait_ge(xh_done, b * T + n * TQ + TQ)
                            for g in range(NG):
                                last = nc.tensor.transpose(pT[:, g, t * P:(t + 1) * P],
                                                           xb[:, k, n * TQ + t, g * P:(g + 1) * P], ident[:])
                        last.then_inc(turned, 1)

                    turn(0)
                    for n in range(NQ):
                        at = b * NQ + n
                        pe.wait_ge(xT_copied, at * NG + NG)
                        if n + 1 < NQ:
                            turn(n + 1)
                        for m in range(2 * NG):
                            pe.wait_ge(lo_done, (at - 1) * 4 + m + 1) if n > 0 else pe.wait_ge(lo_done, at * 4)
                            nc.tensor.matmul(pqk[:, m, :], w[:, m // NG, m % NG, :], xT[:, n % 2, m % NG, :],
                                             start=True, stop=True).then_inc(qk_done, 1)
                        pe.wait_ge(v_copied, at * 2)
                        for t in range(TQ):
                            for g in range(NG):
                                last = nc.tensor.matmul(pv[:, t // 2, (t % 2) * D + g * P:(t % 2) * D + (g + 1) * P],
                                                        xT[:, n % 2, g, t * P:(t + 1) * P], w[:, 2, g, :],
                                                        start=True, stop=True)
                        last.then_inc(v_done, 1)


def attend(nc, tag, qk, v_dram, out):
    UQ = 512
    NU = S // UQ
    NC = S // P
    QT = UQ // P
    TILES = NC * HG
    BU = NG * NU
    STACK = 3 * DH
    RING = 8 * HG
    PV_LAG = 6
    LEAD = 4 * NC // HG
    NQB = 4
    raw_chunks = range(NC - RAW, NC)
    dve_tiles = [j for j in range((NC - RAW) * HG) if (j // HG + j % HG) % DVE_SHARE == 0]
    pool_tiles = [j for j in range((NC - RAW) * HG) if j not in dve_tiles]

    def additions(tiles):
        found, first, last = {}, {}, {}
        for j in tiles:
            h = j % HG
            if h not in first:
                first[h] = j
            else:
                found[j] = (None if h in last else first[h], len(found), last.get(h))
                last[h] = len(found) - 1
        return found

    def used_by(adds, j):
        if j in adds:
            return adds[j][1] + 1
        return next(n for first, n, _ in adds.values() if first == j) + 1

    pool_adds, dve_adds = additions(pool_tiles), additions(dve_tiles)
    SCALE = float(DH) ** -0.5
    with ExitStack() as ctx:
        used = ctx.enter_context(cleared_semaphores(nc))

        def sb(name, shape, dt=F32):
            return ctx.enter_context(nc.sbuf_tensor(f"{tag}_{name}", shape, dt))

        def psum(name, shape):
            return ctx.enter_context(nc.psum_tensor(f"{tag}_{name}", shape, F32))

        def sem(name):
            handle = nc.alloc_semaphore(f"{tag}_{name}")
            used.append(handle)
            return handle

        qs = sb("qs", [STACK + 1, NQB, HG, UQ], F32R)
        ks = sb("ks", [STACK + 1, NG, HG, S], F32R)
        v = sb("v", [P, NG, NC, P])
        probs = sb("probs", [P, RING, UQ])
        pool_sum = sb("pool_sum", [P, HG, UQ])
        dve_sum = sb("dve_sum", [P, HG, UQ])
        part_max = sb("part_max", [P, HG, QT, 2])
        neg_max = sb("neg_max", [P, HG, QT])
        max_row = sb("max_row", [QT, HG, P], F32R)
        ones = sb("ones", [P, P])
        ident = sb("ident", [P, P])
        oT = sb("oT", [P, UQ])
        zT = sb("zT", [P, UQ])
        rz = sb("rz", [P, QT, HG])
        o = sb("o", [P, 2, QT, HG, DH])
        ps_max = psum("ps_max", [P, 2, 2, 512])
        ps_s = psum("ps_s", [P, 2, UQ])
        ps_acc = psum("ps_acc", [P, UQ])
        ps_misc = psum("ps_misc", [P, 512])

        load_turn = sem("load_turn")
        consts = sem("consts")
        ones_row = sem("ones_row")
        q_in = [sem(f"q_in{n}") for n in range(NQB)]
        k_in = [sem(f"k_in{n}") for n in range(NG)]
        v_in = [sem(f"v_in{n}") for n in range(NG)]
        max_scores = sem("max_scores")
        part_max_done = sem("part_max_done")
        neg_max_done = sem("neg_max_done")
        max_turned = sem("max_turned")
        max_row_done = sem("max_row_done")
        max_in = [sem(f"max_in{h}") for h in range(HG)]
        scores = sem("scores")
        exp_done = sem("exp_done")
        pv_done = sem("pv_done")
        pool_added = sem("pool_added")
        dve_added = sem("dve_added")
        z_done = sem("z_done")
        oT_done = sem("oT_done")
        zT_done = sem("zT_done")
        z_turned = sem("z_turned")
        rz_done = sem("rz_done")
        o_turned = sem("o_turned")
        o_done = sem("o_done")
        o_out = [sem(f"o_out{n}") for n in range(2)]

        adds_pool, adds_dve = len(pool_adds), len(dve_adds)

        block = ctx.enter_context(nc.Block())

        @block.sync
        def _(sp):
            def load_q(b, un):
                g, u, k = un // NU, un % NU, un % NQB
                src = qk[bass.ds(b, 1)].rearrange("a part g (h d) s -> part g d (a h) s", h=HG)
                cols = slice(u * UQ, (u + 1) * UQ)
                for r, part in enumerate((0, 1, 0)):
                    sp.dma_start(qs[r * DH:(r + 1) * DH, k].bitcast(F32), src[part, g, :, :, cols]
                                 ).then_inc(q_in[k], 16)

            def load_kv(b, g):
                src = qk[bass.ds(b, 1)].rearrange("a part g (h d) s -> part g d (a h) s", h=HG)
                for r, part in enumerate((0, 0, 1)):
                    sp.dma_start(ks[r * DH:(r + 1) * DH, g].bitcast(F32), src[part, NG + g]).then_inc(k_in[g], 16)
                sp.dma_start(v[:, g], v_dram[bass.ds(b * S, S), g * P:(g + 1) * P]
                             .rearrange("(c p) d -> p c d", p=P)).then_inc(v_in[g], 16)

            def max_rows(b, un):
                n = b * BU + un + 1
                for h in range(HG):
                    sp.wait_ge(max_row_done, n * HG + h + 1)
                    sp.dma_start(qs[STACK:STACK + 1, (un + 1) % NQB, h, :].bitcast(F32)
                                 .rearrange("a (t q) -> a t q", t=QT),
                                 max_row[:, h, :].bitcast(F32)).then_inc(max_in[h], 16)

            load_q(0, 0)
            load_kv(0, 0)
            load_q(0, 1)
            load_kv(0, 1)
            load_q(0, 2)
            max_rows(0, -1)

            def batch(b, last=False):
                for un in range(BU):
                    if un + 3 < BU or not last:
                        sp.wait_ge(scores, (b * BU + un) * TILES)
                        sp.sem_inc(load_turn, 1)
                        load_q(b + (un + 3) // BU, (un + 3) % BU)
                    if un == NU and not last:
                        sp.wait_ge(pv_done, (b * BU + un) * TILES)
                        sp.sem_inc(load_turn, 1)
                        load_kv(b + 1, 0)
                    if un + 1 < BU or not last:
                        max_rows(b, un)
                if not last:
                    sp.wait_ge(pv_done, (b + 1) * BU * TILES)
                    sp.sem_inc(load_turn, 1)
                    load_kv(b + 1, 1)

            batch(0)
            with sp.Fori(1, B - 1) as b:
                batch(b)
            batch(B - 1, last=True)

        @block.gpsimd
        def _(pool):
            nc.gpsimd.memset(ones[:], 1.0).then_inc(consts, 1)
            pool.wait_ge(consts, 1)
            nc.gpsimd.affine_select(out=ident[:], in_=ones[:], compare_op=ALU.is_equal, fill=0.0, base=0,
                                    pattern=[[-1, P]], channel_multiplier=1).then_inc(consts, 1)
            pool.wait_ge(consts, 2)
            for g in range(NG):
                nc.gpsimd.memset(ks[STACK:STACK + 1, g].bitcast(F32), 1.0).then_inc(ones_row, 1)
                pool.wait_ge(ones_row, g + 1)

            def batch(b, first_batch=False):
                for un in range(BU):
                    unit = b * BU + un
                    for j, (first, n, before) in pool_adds.items():
                        pool.wait_ge(exp_done, unit * TILES + j + 1)
                        acc = pool_sum[:, j % HG]
                        if first is None:
                            pool.wait_ge(pool_added, unit * adds_pool + before + 1)
                            a = acc
                        else:
                            if un > 0 or not first_batch:
                                pool.wait_ge(z_done, unit)
                            a = probs[:, first % RING]
                        nc.gpsimd.tensor_tensor(acc, a, probs[:, j % RING], ALU.add).then_inc(pool_added, 1)

            batch(0, first_batch=True)
            with pool.Fori(1, B) as b:
                batch(b)

        @block.vector
        def _(dve):
            def part_max_of(unit, m, first_unit=False):
                h, t, half = m // (2 * QT), m // 2 % QT, m % 2
                if m % (2 * QT) == 0 and not first_unit:
                    dve.wait_ge(neg_max_done, (unit - 1) * HG + h + 1)
                dve.wait_ge(max_scores, unit * (TILES // 2) + m + 1)
                nc.vector.reduce_max(part_max[:, h, t, half:half + 1], ps_max[:, m % 2], AX.XY
                                     ).then_inc(part_max_done, 1)
                if m % (2 * QT) == 2 * QT - 1:
                    dve.wait_ge(part_max_done, unit * (TILES // 2) + m + 1)
                    if not first_unit:
                        dve.wait_ge(max_turned, (unit - 1) * HG + h + 1)
                    nc.vector.tensor_reduce(neg_max[:, h], part_max[:, h], AX.X, ALU.max, negate=True
                                            ).then_inc(neg_max_done, 1)

            for m in range(TILES // 2):
                part_max_of(0, m, first_unit=True)
            for m in range(LEAD // 2):
                part_max_of(1, m)

            def batch(b, first_batch=False, last=False):
                for un in range(BU):
                    unit = b * BU + un
                    carry = un > 0 or not first_batch

                    def add(j):
                        first, n, before = dve_adds[j]
                        dve.wait_ge(exp_done, unit * TILES + j + 1)
                        acc = dve_sum[:, j % HG]
                        if first is None:
                            dve.wait_ge(dve_added, unit * adds_dve + before + 1)
                            a = acc
                        else:
                            if un > 0 or not first_batch:
                                dve.wait_ge(z_done, unit)
                            a = probs[:, first % RING]
                        nc.vector.tensor_tensor(acc, a, probs[:, j % RING], ALU.add).then_inc(dve_added, 1)

                    def invert(prev):
                        dve.wait_ge(z_turned, prev + 1)
                        dve.wait_ge(o_done, prev)
                        nc.vector.reciprocal(rz[:], ps_misc[:].rearrange("p (t h d) -> p t h d", t=QT, h=HG)[:, :, :, 0]
                                             ).then_inc(rz_done, 1)

                    def normalize(prev, un_close):
                        k = (un_close - 1) % BU
                        dve.wait_ge(rz_done, prev + 1)
                        dve.wait_ge(o_turned, prev + 1)
                        if un_close > 2 or not first_batch:
                            dve.wait_ge(o_out[k % 2], (b * (BU // 2) + (un_close - 1) // 2) * 16)
                        nc.vector.tensor_tensor(
                            o[:, k % 2], ps_misc[:].rearrange("p (t h d) -> p t h d", t=QT, h=HG),
                            rz[:].unsqueeze(3).to_broadcast([P, QT, HG, DH]), ALU.mult).then_inc(o_done, 1)

                    for j in range(TILES):
                        if j % 2 == 1:
                            m = (j + LEAD) // 2
                            if un + 1 + m // (TILES // 2) < BU or not last:
                                part_max_of(unit + 1 + m // (TILES // 2), m % (TILES // 2))
                        if carry and j == CLOSE_AT + 5:
                            invert(unit - 1)
                        if carry and j == CLOSE_AT + 9:
                            normalize(unit - 1, un)
                        if j - ADD_LAG in dve_adds:
                            add(j - ADD_LAG)
                    for j in range(TILES, TILES + ADD_LAG):
                        if j - ADD_LAG in dve_adds:
                            add(j - ADD_LAG)
                if last:
                    invert(b * BU + BU - 1)
                    normalize(b * BU + BU - 1, BU)

            batch(0, first_batch=True)
            with dve.Fori(1, B - 1) as b:
                batch(b)
            batch(B - 1, last=True)

        @block.scalar
        def _(act):
            def row_of_max(unit, h, first_unit=False):
                act.wait_ge(max_turned, unit * HG + h + 1)
                if not first_unit:
                    act.wait_ge(max_in[h], unit * 16)
                nc.scalar.copy(max_row[:, h, :], ps_misc[0:QT, 0:P]).then_inc(max_row_done, 1)

            for h in range(HG):
                row_of_max(0, h, first_unit=True)

            def batch(b, first_batch=False, last=False):
                for un in range(BU):
                    unit = b * BU + un
                    carry = un > 0 or not first_batch

                    def free(j):
                        act.wait_ge(pv_done, unit * TILES + j - RING + 1)
                        before = 1 if j < RING else 0
                        k = (j - RING) % TILES
                        if k in pool_tiles:
                            act.wait_ge(pool_added, (unit - before) * adds_pool + used_by(pool_adds, k))
                        elif k in dve_tiles:
                            act.wait_ge(dve_added, (unit - before) * adds_dve + used_by(dve_adds, k))
                        else:
                            act.wait_ge(z_done, unit + 1 - before)

                    def copy_acc(n):
                        act.wait_ge(pv_done, n * TILES)
                        if un > 1 or not first_batch:
                            act.wait_ge(o_turned, n - 1)
                        nc.scalar.copy(oT[:], ps_acc[:]).then_inc(oT_done, 1)

                    def copy_z(n):
                        act.wait_ge(z_done, n)
                        if un > 1 or not first_batch:
                            act.wait_ge(z_turned, n - 1)
                        nc.scalar.copy(zT[:], ps_misc[:]).then_inc(zT_done, 1)

                    def store(n, un_close):
                        k = (un_close - 1) % BU
                        g, u = k // NU, k % NU
                        act.wait_ge(o_done, n)
                        act.dma_start(out[bass.ds((b + (un_close - 1) // BU) * S + u * UQ, UQ), g * P:(g + 1) * P]
                                      .rearrange("(t p) c -> p t c", p=P),
                                      o[:, k % 2].rearrange("p t h d -> p t (h d)")).then_inc(o_out[k % 2], 16)

                    for j in range(TILES):
                        act.wait_ge(scores, unit * TILES + j + 1)
                        if carry or j >= RING:
                            free(j)
                        nc.scalar.activation(probs[:, j % RING], ps_s[:, j % 2], ACT.Exp, scale=SCALE
                                             ).then_inc(exp_done, 1)
                        if carry:
                            if j == PV_LAG:
                                copy_acc(unit)
                            if j == CLOSE_AT + 2:
                                copy_z(unit)
                            if j == CLOSE_AT + 14:
                                store(unit, un)
                        if j in MAX_AT and (un + 1 < BU or not last):
                            row_of_max(unit + 1, MAX_AT.index(j))
                if last:
                    copy_acc(b * BU + BU)
                    copy_z(b * BU + BU)
                    store(b * BU + BU, BU)

            batch(0, first_batch=True)
            with act.Fori(1, B - 1) as b:
                batch(b)
            batch(B - 1, last=True)
            for k in range(2):
                act.wait_ge(o_out[k], B * BU // 2 * 16)

        @block.tensor
        def _(pe):
            def score_for_max(unit, un, m, first_unit=False):
                h, t, c = m // (4 * QT), m // 4 % QT, m % 4
                g = un % BU // NU
                if m % 2 == 0 and (m >= 4 or not first_unit):
                    pe.wait_ge(part_max_done, unit * (TILES // 2) + m // 2 - 1)
                last = nc.tensor.matmul(ps_max[:, m // 2 % 2, m % 2], qs[0:STACK, un % NQB, h, t * P:(t + 1) * P],
                                        ks[0:STACK, g, h, c * 512:(c + 1) * 512], start=True, stop=True)
                if m % 2 == 1:
                    last.then_inc(max_scores, 1)

            def turn_max(unit, h):
                pe.wait_ge(neg_max_done, unit * HG + h + 1)
                nc.tensor.transpose(ps_misc[0:QT, 0:P], neg_max[:, h], ident[:]).then_inc(max_turned, 1)

            pe.wait_ge(consts, 2)
            pe.wait_ge(q_in[0], 48)
            pe.wait_ge(k_in[0], 48)
            for m in range(TILES):
                score_for_max(0, 0, m, first_unit=True)
            pe.wait_ge(q_in[1], 48)
            for h in range(HG):
                if h > 0:
                    pe.wait_ge(max_row_done, h)
                turn_max(0, h)
            for m in range(LEAD):
                score_for_max(1, 1, m)

            pe.wait_ge(ones_row, NG)

            def batch(b, first_batch=False, last=False):
                for un in range(BU):
                    unit = b * BU + un
                    carry = un > 0 or not first_batch
                    g, u = un // NU, un % NU

                    def pv(n, k, j):
                        c, h = divmod(j, HG)
                        pe.wait_ge(exp_done, n * TILES + j + 1)
                        if j == 0 and (k > 0 or not first_batch):
                            pe.wait_ge(oT_done, n)
                        nc.tensor.matmul(ps_acc[h * DH:(h + 1) * DH, :], v[:, k // NU, c, h * DH:(h + 1) * DH],
                                         probs[:, j % RING], start=(c == 0), stop=(c == NC - 1)).then_inc(pv_done, 1)

                    def sum_keys(n):
                        pe.wait_ge(pool_added, n * adds_pool + adds_pool)
                        pe.wait_ge(dve_added, n * adds_dve + adds_dve)
                        parts = [pool_sum, dve_sum]
                        count = len(parts) + len(raw_chunks)
                        for i in range(count):
                            for h in range(HG):
                                if i < len(parts):
                                    src = parts[i][:, h]
                                else:
                                    src = probs[:, (raw_chunks[i - len(parts)] * HG + h) % RING]
                                last = nc.tensor.matmul(ps_misc[h * DH:(h + 1) * DH, :], ones[:, 0:DH], src,
                                                        start=(i == 0), stop=(i == count - 1))
                        last.then_inc(z_done, 1)

                    def turn_z(n):
                        pe.wait_ge(zT_done, n)
                        for t in range(QT):
                            last = nc.tensor.transpose(ps_misc[:, t * P:(t + 1) * P], zT[:, t * P:(t + 1) * P], ident[:])
                        last.then_inc(z_turned, 1)

                    def turn_o(n):
                        pe.wait_ge(rz_done, n)
                        pe.wait_ge(oT_done, n)
                        for t in range(QT):
                            last = nc.tensor.transpose(ps_misc[:, t * P:(t + 1) * P], oT[:, t * P:(t + 1) * P], ident[:])
                        last.then_inc(o_turned, 1)

                    if u == 0:
                        pe.wait_ge(v_in[g], b * 16 + 16)
                    pvs = []
                    for j in range(TILES):
                        c, h = divmod(j, HG)
                        if j < HG:
                            pe.wait_ge(max_in[h], unit * 16 + 16)
                        if j > 1 or carry:
                            pe.wait_ge(exp_done, unit * TILES + j - 1)
                        nc.tensor.matmul(ps_s[:, j % 2], ks[:, g, h, c * P:(c + 1) * P], qs[:, un % NQB, h, :],
                                         start=True, stop=True).then_inc(scores, 1)
                        m = j + LEAD
                        ahead = un + 1 + m // TILES
                        if ahead < BU or not last:
                            if m == TILES:
                                pe.wait_ge(q_in[ahead % NQB], (b * (BU // NQB) + ahead // NQB + 1) * 48)
                                if ahead % NU == 0:
                                    pe.wait_ge(k_in[ahead // NU % NG], (b + ahead // BU + 1) * 48)
                            score_for_max(unit + ahead - un, ahead, m % TILES)
                        if j >= PV_LAG:
                            pv(unit, un, j - PV_LAG)
                        elif carry:
                            pv(unit - 1, (un - 1) % BU, TILES - PV_LAG + j)
                        if carry:
                            if j == CLOSE_AT:
                                pe.wait_ge(max_row_done, unit * HG + HG)
                                sum_keys(unit - 1)
                            if j == CLOSE_AT + 4:
                                turn_z(unit)
                            if j == CLOSE_AT + 7:
                                turn_o(unit)
                        if j in MAX_AT and (un + 1 < BU or not last):
                            i = MAX_AT.index(j)
                            if i == 0 and carry:
                                pe.wait_ge(o_done, unit)
                            elif i > 0:
                                pe.wait_ge(max_row_done, (unit + 1) * HG + i)
                            turn_max(unit + 1, i)
                if last:
                    for j in range(TILES - PV_LAG, TILES):
                        pv(b * BU + BU - 1, BU - 1, j)
                    sum_keys(b * BU + BU - 1)
                    turn_z(b * BU + BU)
                    turn_o(b * BU + BU)

            batch(0, first_batch=True)
            with pe.Fori(1, B - 1) as b:
                batch(b)
            batch(B - 1, last=True)


RAW, DVE_SHARE = 2, 4
ADD_LAG = 4
CLOSE_AT = 8
MAX_AT = (24, 31, 40, 56)


def macaron_block(nc, x, qU, qVt, qb, kU, kVt, kb, vU, vVt, vb, w_router, w_qkvT, w_outT, g1, g2, w1T, w2T, w3T,
                  out):
    after_ffn = nc.dram_tensor("after_ffn", [B * S, D], F32).ap()
    attention = nc.dram_tensor("attention", [B * S, D], F32).ap()
    scores = nc.dram_tensor("router_scores", [P, P], F32).ap()
    qk = nc.dram_tensor("qk_parts", [B, 2, 2 * NG, P, S], F32).ap()
    v_dram = nc.dram_tensor("v_tokens", [B * S, D], F32).ap()
    ffn_weights = (w_qkvT, w_outT, g1, g2, w1T, w2T, w3T)
    with nc.sbuf_tensor("picked", [P, B], U32) as picked:
        score_pass(nc, "s1", x, None, w_router, after_ffn, scores)
        pick_tokens(nc, "t1", scores, picked[:])
        routed_ffn(nc, "f1", x, None, picked[:], *ffn_weights, after_ffn)
        project(nc, "pr", after_ffn, [(qU, qVt), (kU, kVt), (vU, vVt)], [qb, kb], vb, qk, v_dram)
        attend(nc, "at", qk, v_dram, attention)
        score_pass(nc, "s2", after_ffn, attention, w_router, out, scores)
        pick_tokens(nc, "t2", scores, picked[:])
        routed_ffn(nc, "f2", after_ffn, attention, picked[:], *ffn_weights, out)


def kernel(L0_attn_x, L0_attn_Uq, L0_attn_Vq, L0_attn_bq, L0_attn_Uk, L0_attn_Vk, L0_attn_bk, L0_attn_Uv, L0_attn_Vv,
           L0_attn_bv, L0_ffn_w_router, L0_ffn_W_qkv, L0_ffn_W_out, L0_ffn_g1, L0_ffn_g2, L0_ffn_W1, L0_ffn_W2,
           L0_ffn_W3):
    import numpy as np
    import concourse.bacc as bacc
    from concourse.bass_utils import run_bass_kernel_spmd

    def columns(a):
        return np.ascontiguousarray(np.asarray(a).reshape(-1, P).T)

    def turned(a):
        return np.ascontiguousarray(np.swapaxes(np.asarray(a), -1, -2))

    arrays = {
        "x": np.ascontiguousarray(np.asarray(L0_attn_x).reshape(B * S, D)),
        "qU": turned(L0_attn_Uq), "qV": np.ascontiguousarray(L0_attn_Vq), "qb": columns(L0_attn_bq),
        "kU": turned(L0_attn_Uk), "kV": np.ascontiguousarray(L0_attn_Vk), "kb": columns(L0_attn_bk),
        "vU": turned(L0_attn_Uv), "vV": np.ascontiguousarray(L0_attn_Vv),
        "vb": np.ascontiguousarray(np.asarray(L0_attn_bv).reshape(D)),
        "w_router": np.ascontiguousarray(L0_ffn_w_router),
        "w_qkvT": turned(L0_ffn_W_qkv), "w_outT": turned(L0_ffn_W_out),
        "g1": columns(L0_ffn_g1), "g2": columns(L0_ffn_g2),
        "w1T": turned(L0_ffn_W1), "w2T": turned(L0_ffn_W2), "w3T": turned(L0_ffn_W3),
    }
    nc = bacc.Bacc("TRN2", target_bir_lowering=False, num_devices=1)
    args = [nc.dram_tensor(f"in_{n}", a.shape, mybir.dt.from_np(a.dtype), kind="ExternalInput").ap()
            for n, a in arrays.items()]
    out = nc.dram_tensor("out", [B * S, D], F32, kind="ExternalOutput").ap()
    macaron_block(nc, *args, out)
    result = run_bass_kernel_spmd(nc, [{f"in_{n}": a for n, a in arrays.items()}], core_ids=[0])
    return result.results[0]["out"].reshape(B, S, D)
```

```python
from contextlib import ExitStack, contextmanager

import concourse.bass as bass
from concourse import mybir

P = 128
F32 = mybir.dt.float32
F32R = mybir.dt.float32r
U32 = mybir.dt.uint32
I32 = mybir.dt.int32
ALU = mybir.AluOpType
ACT = mybir.ActivationFunctionType
AX = mybir.AxisListType

B, S, D = 8, 2048, 256
T = S // P
H, DH = 8, 32
HG = P // DH
NG = H // HG
CAP = 128
FH, FD = 16, 16
DFF = 682
DFF_HALF = DFF // 2
DFF_TILES = (DFF + P - 1) // P
LN_EPS = 1e-5
RMS_EPS = 1e-6
LOWEST = -3.0e38


class Chain:

    def __init__(self, engine, semaphore, base=0):
        self.engine, self.semaphore, self.base, self.n = engine, semaphore, base, 0

    def step(self, instruction):
        self.n += 1
        instruction.then_inc(self.semaphore, 1)
        self.engine.wait_ge(self.semaphore, self.base + self.n)
        return instruction


@contextmanager
def cleared_semaphores(nc):
    used = []
    yield used
    nc.clear_and_free_semaphores(used)
    nc.all_engine_barrier()


def score_pass(nc, tag, x, add, w_router, y, scores):
    adding = add is not None
    TG = T // 2
    GROUPS = B * T // TG
    NBUF = 4
    ROWS = TG * P
    OWN = 14
    with ExitStack() as ctx:
        used = ctx.enter_context(cleared_semaphores(nc))

        def sb(name, shape, dt=F32):
            return ctx.enter_context(nc.sbuf_tensor(f"{tag}_{name}", shape, dt))

        def sem(name):
            handle = nc.alloc_semaphore(f"{tag}_{name}")
            used.append(handle)
            return handle

        xb = sb("x", [P, NBUF, TG, D])
        ab = sb("add", [P, NBUF, TG, D]) if adding else None
        yb = sb("y", [P, NBUF, TG, D])
        w = sb("w", [P, D])
        wsum = sb("wsum", [P, 1])
        junk = sb("junk", [P, 4, D])
        stats = sb("stats", [P, NBUF, TG, 6])
        sm = sb("small", [P, NBUF, 12, TG])
        sall = sb("sall", [P, GROUPS, TG])
        sT = sb("sT", [P, P])
        ones = sb("ones", [P, P])
        ident = sb("ident", [P, P])
        pt = ctx.enter_context(nc.psum_tensor(f"{tag}_pt", [P, P], F32))

        w_in = sem("w_in")
        x_in = [sem(f"x_in{i}") for i in range(NBUF)]
        a_in = [sem(f"a_in{i}") for i in range(NBUF)]
        added = sem("added")
        dve_own = sem("dve_own")
        var_ready = sem("var_ready")
        std_ready = sem("std_ready")
        affine_ready = sem("affine_ready")
        products_done = sem("products_done")
        stats_done = sem("stats_done")
        y_done = sem("y_done")
        y_out = [sem(f"y_out{i}") for i in range(NBUF)]
        id_ready = sem("id_ready")
        scores_done = sem("scores_done")
        transposed = sem("transposed")
        sT_done = sem("sT_done")
        s_out = sem("s_out")

        block = ctx.enter_context(nc.Block())

        @block.sync
        def _(sp):
            sp.dma_start(w[:], w_router.partition_broadcast(P)).then_inc(w_in, 16)

            def load(i, k):
                b = NBUF * i + k
                src = x[bass.ds(b * ROWS, ROWS), :].rearrange("(t p) d -> p t d", p=P)
                sp.dma_start(xb[:, k], src).then_inc(x_in[k], 16)
                if adding:
                    src = add[bass.ds(b * ROWS, ROWS), :].rearrange("(t p) d -> p t d", p=P)
                    sp.dma_start(ab[:, k], src).then_inc(a_in[k], 16)

            for k in range(NBUF):
                load(0, k)
            with sp.Fori(1, GROUPS // NBUF) as i:
                for k in range(NBUF):
                    sp.wait_ge(products_done, ((i - 1) * NBUF + k + 1) * TG)
                    sp.wait_ge(y_done, (i - 1) * NBUF + k + 1)
                    load(i, k)

        @block.gpsimd
        def _(pool):
            nc.gpsimd.memset(ones[:], 1.0).then_inc(id_ready, 1)
            pool.wait_ge(id_ready, 1)
            nc.gpsimd.affine_select(out=ident[:], in_=ones[:], compare_op=ALU.is_equal, fill=0.0, base=0,
                                    pattern=[[-1, P]], channel_multiplier=1).then_inc(id_ready, 1)
            if adding:
                with pool.Fori(0, GROUPS // NBUF) as i:
                    for k in range(NBUF):
                        pool.wait_ge(x_in[k], i * 16 + 16)
                        pool.wait_ge(a_in[k], i * 16 + 16)
                        for q in range(TG // 4):
                            t4 = slice(4 * q, 4 * q + 4)
                            last = nc.gpsimd.tensor_tensor(xb[:, k, t4], xb[:, k, t4], ab[:, k, t4], ALU.add)
                            last.then_inc(added, 1)

        @block.vector
        def _(dve):
            dve.wait_ge(w_in, 16)
            own = Chain(dve, dve_own)
            own.step(nc.vector.reduce_sum(wsum[:], w[:], AX.X))
            with dve.Fori(0, GROUPS // NBUF) as i:
                own = Chain(dve, dve_own, i * NBUF * OWN + 1)
                for k in range(NBUF):
                    if not adding:
                        dve.wait_ge(x_in[k], i * 16 + 16)
                    v = [sm[:, k, n, :] for n in range(12)]
                    for t in range(TG):
                        if adding and t % 4 == 0:
                            dve.wait_ge(added, (i * NBUF + k) * (TG // 4) + t // 4 + 1)
                        nc.vector.bn_stats(stats[:, k, t, :], xb[:, k, t, :]).then_inc(stats_done, 1)
                        if t >= 4:
                            dve.wait_ge(products_done, (i * NBUF + k) * TG + t - 3)
                        nc.vector.tensor_tensor_reduce(out=junk[:, t % 4, :], in0=xb[:, k, t, :], in1=w[:], scale=1.0,
                                                       scalar=0.0, op0=ALU.mult, op1=ALU.add,
                                                       accum_out=v[11][:, t:t + 1]).then_inc(products_done, 1)
                    dve.wait_ge(stats_done, (i * NBUF + k + 1) * TG)
                    dve.wait_ge(products_done, (i * NBUF + k + 1) * TG)
                    me, m2e, mo, m2o = (stats[:, k, :, n] for n in (1, 2, 4, 5))
                    own.step(nc.vector.tensor_tensor(v[0], me, mo, ALU.add))
                    own.step(nc.vector.tensor_tensor(v[1], me, mo, ALU.subtract))
                    own.step(nc.vector.tensor_tensor(v[2], m2e, m2o, ALU.add))
                    own.step(nc.vector.scalar_tensor_tensor(v[3], v[1], 0.25, v[1], ALU.mult, ALU.mult))
                    own.step(nc.vector.tensor_scalar(v[4], v[2], 1.0 / D, LN_EPS, ALU.mult, ALU.add))
                    nc.vector.tensor_tensor(v[5], v[3], v[4], ALU.add).then_inc(var_ready, 1)
                    dve.wait_ge(std_ready, i * NBUF + k + 1)
                    own.step(nc.vector.reciprocal(v[7], v[6]))
                    own.step(nc.vector.tensor_tensor(v[8], v[7], v[7], ALU.mult))
                    own.step(nc.vector.tensor_tensor(v[8], v[8], v[5], ALU.mult))
                    own.step(nc.vector.tensor_scalar(v[8], v[8], -0.5, 1.5, ALU.mult, ALU.add))
                    own.step(nc.vector.tensor_tensor(v[9], v[7], v[8], ALU.mult))
                    own.step(nc.vector.scalar_tensor_tensor(v[10], v[0], 0.5, v[9], ALU.mult, ALU.mult))
                    own.step(nc.vector.tensor_scalar(v[0], v[9], 0.5, 1.0, ALU.mult, ALU.add))
                    nc.vector.tensor_scalar(v[1], v[10], -0.5, None, ALU.mult).then_inc(affine_ready, 1)
                    own.step(nc.vector.tensor_tensor(v[2], v[11], v[9], ALU.mult))
                    own.step(nc.vector.tensor_scalar(v[3], v[10], wsum[:], None, ALU.mult))
                    nc.vector.tensor_tensor(sall[:, bass.ds(i * NBUF + k, 1), :].rearrange("p a t -> p (a t)"),
                                            v[2], v[3], ALU.subtract).then_inc(scores_done, 1)

        @block.scalar
        def _(act):
            with act.Fori(0, GROUPS // NBUF) as i:
                for k in range(NBUF):
                    act.wait_ge(var_ready, i * NBUF + k + 1)
                    nc.scalar.activation(sm[:, k, 6, :], sm[:, k, 5, :], ACT.Sqrt).then_inc(std_ready, 1)
                    act.wait_ge(affine_ready, i * NBUF + k + 1)
                    act.wait_ge(y_out[k], i * 16)
                    for t in range(TG):
                        last = nc.scalar.activation(yb[:, k, t, :], xb[:, k, t, :], ACT.Identity,
                                                    scale=sm[:, k, 0, t:t + 1], bias=sm[:, k, 1, t:t + 1])
                    last.then_inc(y_done, 1)
                    act.wait_ge(y_done, i * NBUF + k + 1)
                    act.dma_start(y[bass.ds((i * NBUF + k) * ROWS, ROWS), :].rearrange("(t p) d -> p t d", p=P),
                                  yb[:, k]).then_inc(y_out[k], 16)
            act.wait_ge(transposed, 1)
            nc.scalar.copy(sT[:], pt[:]).then_inc(sT_done, 1)
            act.wait_ge(sT_done, 1)
            act.dma_start(scores, sT[:]).then_inc(s_out, 16)
            act.wait_ge(s_out, 16)
            for k in range(NBUF):
                act.wait_ge(y_out[k], 16 * GROUPS // NBUF)

        @block.tensor
        def _(pe):
            pe.wait_ge(id_ready, 2)
            pe.wait_ge(scores_done, GROUPS)
            nc.tensor.transpose(pt[:], sall[:].rearrange("p b t -> p (b t)"), ident[:]).then_inc(transposed, 1)


def pick_tokens(nc, tag, scores, picked):
    QUARTERS = 4
    Q = B * QUARTERS
    L = S // QUARTERS
    with ExitStack() as ctx:
        used = ctx.enter_context(cleared_semaphores(nc))

        def sb(name, shape, dt=F32):
            return ctx.enter_context(nc.sbuf_tensor(f"{tag}_{name}", shape, dt))

        def sem(name):
            handle = nc.alloc_semaphore(f"{tag}_{name}")
            used.append(handle)
            return handle

        sc = sb("sc", [Q, L])
        top = sb("top", [Q, CAP])
        index = sb("index", [Q, CAP], U32)
        indexf = sb("indexf", [Q, CAP])
        ones = sb("ones", [Q, Q])
        ident = sb("ident", [Q, Q])
        ints = sb("ints", [P, 2 * Q + CAP], I32)
        floats = sb("floats", [P, 2 * Q + CAP])
        first_row = floats[:, 0:Q]
        place = floats[:, Q:2 * Q]
        wanted = floats[:, 2 * Q:2 * Q + CAP]
        all_top = sb("all_top", [P, Q, CAP])
        topT = sb("topT", [P, Q])
        rowT = sb("rowT", [P, Q])
        junk = sb("junk", [P, 4, (QUARTERS - 1) * CAP])
        before = sb("before", [P, 2, Q])
        rank = sb("rank", [P, Q])
        is_rank = sb("is_rank", [P, Q, CAP])
        top_dram = nc.dram_tensor(f"{tag}_top_lists", [Q * CAP], F32).ap()
        pt = ctx.enter_context(nc.psum_tensor(f"{tag}_pt", [P, 2, Q], F32))
        prow = ctx.enter_context(nc.psum_tensor(f"{tag}_prow", [P, B], F32))
        loaded = sem("loaded")
        own_done = sem("own")
        consts = sem("consts")
        tops_done = sem("tops_done")
        top_out = sem("top_out")
        all_top_in = sem("all_top_in")
        indices_done = sem("indices_done")
        zeroed = sem("zeroed")
        transposed = sem("transposed")
        counted = sem("counted")
        rows_done = sem("rows_done")
        is_rank_done = sem("is_rank_done")
        ordered = sem("ordered")
        picked_done = sem("picked_done")

        block = ctx.enter_context(nc.Block())

        @block.sync
        def _(sp):
            sp.dma_start(sc[:], scores.rearrange("(q t) p -> q (t p)", q=Q)).then_inc(loaded, 16)
            sp.wait_ge(tops_done, 1)
            sp.dma_start(top_dram.rearrange("(q c) -> q c", q=Q), top[:]).then_inc(top_out, 16)
            sp.wait_ge(top_out, 16)
            sp.dma_start(all_top[:].rearrange("p q c -> p (q c)"), top_dram.partition_broadcast(P)
                         ).then_inc(all_top_in, 16)

        @block.gpsimd
        def _(pool):
            nc.gpsimd.memset(ones[:], 1.0).then_inc(consts, 1)
            nc.gpsimd.iota(ints[:, 0:Q], pattern=[[L, Q]], base=0, channel_multiplier=0).then_inc(consts, 1)
            nc.gpsimd.iota(ints[:, Q:2 * Q], pattern=[[0, Q]], base=0, channel_multiplier=1).then_inc(consts, 1)
            nc.gpsimd.iota(ints[:, 2 * Q:2 * Q + CAP], pattern=[[1, CAP]], base=0, channel_multiplier=0
                           ).then_inc(consts, 1)
            pool.wait_ge(consts, 4)
            nc.gpsimd.affine_select(out=ident[:], in_=ones[:], compare_op=ALU.is_equal, fill=0.0, base=0,
                                    pattern=[[-1, Q]], channel_multiplier=1).then_inc(consts, 1)
            nc.gpsimd.tensor_copy(floats[:], ints[:]).then_inc(consts, 1)
        CONSTS = 6

        @block.vector
        def _(dve):
            nc.vector.memset(before[:], 0.0).then_inc(zeroed, 1)
            own = Chain(dve, own_done)
            dve.wait_ge(loaded, 16)
            for r in range(CAP // 8):
                eight = slice(8 * r, 8 * r + 8)
                own.step(nc.vector.max(top[:, eight], sc[:]))
                if r == CAP // 8 - 1:
                    dve.sem_inc(tops_done, 1)
                own.step(nc.vector.max_index(index[:, eight], top[:, eight], sc[:]))
                if r < CAP // 8 - 1:
                    own.step(nc.vector.match_replace(sc[:], top[:, eight], sc[:], LOWEST))
            nc.vector.tensor_copy(indexf[:], index[:]).then_inc(indices_done, 1)
            dve.wait_ge(transposed, 1)
            dve.wait_ge(consts, CONSTS)
            own.step(nc.vector.tensor_copy(topT[:], pt[:, 0, :]))
            nc.vector.tensor_tensor(rowT[:], pt[:, 1, :], first_row, ALU.add).then_inc(rows_done, 1)
            dve.wait_ge(all_top_in, 16)
            dve.wait_ge(zeroed, 1)
            n = 0
            for b in range(B):
                first, end = b * QUARTERS, (b + 1) * QUARTERS
                for q in range(first, end):
                    for side, lists, op in ((0, (first, q), ALU.is_ge), (1, (q + 1, end), ALU.is_gt)):
                        if lists[0] == lists[1]:
                            continue
                        if n >= 4:
                            dve.wait_ge(counted, n - 3)
                        nc.vector.tensor_scalar(
                            junk[:, n % 4, 0:(lists[1] - lists[0]) * CAP],
                            all_top[:, lists[0]:lists[1], :].rearrange("p q c -> p (q c)"), topT[:, q:q + 1], None,
                            op, ALU.add, accum_out=before[:, side, q:q + 1]).then_inc(counted, 1)
                        n += 1
                dve.wait_ge(counted, n)
                own.step(nc.vector.tensor_tensor(rank[:, first:end], before[:, 0, first:end],
                                                 before[:, 1, first:end], ALU.add))
                own.step(nc.vector.tensor_tensor(rank[:, first:end], rank[:, first:end], place[:, first:end], ALU.add))
                nc.vector.tensor_tensor(is_rank[:, first:end, :],
                                        wanted.unsqueeze(1).to_broadcast([P, QUARTERS, CAP]),
                                        rank[:, first:end].unsqueeze(2).to_broadcast([P, QUARTERS, CAP]),
                                        ALU.is_equal).then_inc(is_rank_done, 1)
            dve.wait_ge(ordered, 1)
            nc.vector.tensor_copy(picked, prow[:]).then_inc(picked_done, 1)
            dve.wait_ge(picked_done, 1)

        @block.tensor
        def _(pe):
            pe.wait_ge(consts, CONSTS)
            pe.wait_ge(tops_done, 1)
            pe.wait_ge(indices_done, 1)
            nc.tensor.transpose(pt[:, 0, :], top[:], ident[:])
            nc.tensor.transpose(pt[:, 1, :], indexf[:], ident[:]).then_inc(transposed, 1)
            pe.wait_ge(rows_done, 1)
            for b in range(B):
                pe.wait_ge(is_rank_done, b + 1)
                for j in range(QUARTERS):
                    q = b * QUARTERS + j
                    last = nc.tensor.matmul(prow[:, b:b + 1], is_rank[:, q, :], rowT[:, q:q + 1], start=(j == 0),
                                            stop=(j == QUARTERS - 1))
            last.then_inc(ordered, 1)


def routed_ffn(nc, tag, x, add, picked, w_qkvT, w_outT, g1, g2, w1T, w2T, w3T, y):
    adding = add is not None
    NB = 4
    ROUNDS = B // NB
    NC = D // P
    GH = P // FD
    ATT_SCALE = float(FD) ** -0.5
    DVE_HEADS = 6
    with ExitStack() as ctx:
        used = ctx.enter_context(cleared_semaphores(nc))

        def sb(name, shape, dt=F32):
            return ctx.enter_context(nc.sbuf_tensor(f"{tag}_{name}", shape, dt))

        def sem(name):
            handle = nc.alloc_semaphore(f"{tag}_{name}")
            used.append(handle)
            return handle

        wqkv = sb("wqkv", [P, NC, 3 * D])
        wout = sb("wout", [P, NC, D])
        w1 = sb("w1", [P, NC, DFF])
        w2 = sb("w2", [P, NC, DFF])
        w3 = sb("w3", [P, DFF_TILES, D])
        gain = sb("gain", [P, 2, NC])
        ones = sb("ones", [P, P])
        zeros = sb("zeros", [P, P])
        ident = sb("ident", [P, P])
        causal = sb("causal", [P, P])
        head_half = sb("head_half", [P, GH])
        head_of = sb("head_of", [P, GH])
        parity = sb("parity", [P, 2])
        xs = sb("xs", [P, B, D])
        ads = sb("ads", [P, B, D]) if adding else None
        stats = sb("stats", [P, B, 6])
        sm = sb("small", [P, ROUNDS, 16, NB])
        xh = sb("xh", [P, B, D])
        hn = sb("hn", [P, B, D])
        hT = sb("hT", [P, NC, NB, P])
        qT = sb("qT", [P, NC, NB, P])
        v = sb("v", [P, NB, D])
        kspread = sb("kspread", [P, NB, NC, GH, P])
        att = sb("att", [P, NB, FH, P])
        rowmax = sb("rowmax", [P, NB, FH])
        rowsum = sb("rowsum", [P, NB, FH])
        attT = sb("attT", [P, 2, FH, P])
        odd = sb("odd", [P, 2, NC, P])
        oT = sb("oT", [P, NC, NB, P])
        xr = sb("xr", [P, NB, D])
        sq = sb("sq", [P, NB, D])
        sig = sb("sig", [P, 2, DFF])
        act1 = sb("act1", [P, 2, DFF])
        gated = sb("gated", [P, 2, DFF])
        gatedT = sb("gatedT", [P, 2, DFF_TILES, P])
        proc = sb("proc", [P, NB, D])
        row = sb("row", [P, NB, D])
        ps = ctx.enter_context(nc.psum_tensor(f"{tag}_ps", [P, 8, 512], F32))

        weights_in = sem("weights_in")
        consts = sem("consts")
        x_in = [sem(f"x_in{b}") for b in range(B)]
        rows_ready = sem("rows_ready")
        dve_own = sem("dve_own")
        var_ready = sem("var_ready")
        std_ready = sem("std_ready")
        rstd_ready = sem("rstd_ready")
        ms_ready = sem("ms_ready")
        rms_ready = sem("rms_ready")
        scale_ready = sem("scale_ready")
        xh_done = sem("xh_done")
        hn_done = sem("hn_done")
        h_turned = sem("h_turned")
        hT_done = sem("hT_done")
        qk_done = sem("qk_done")
        v_done = sem("v_done")
        qT_copied = sem("qT_copied")
        v_copied = sem("v_copied")
        spread_done = sem("spread_done")
        scores_done = sem("scores_done")
        max_done = sem("max_done")
        masked_done = sem("masked_done")
        exp_done = sem("exp_done")
        recip_done = sem("recip_done")
        dve_probs_done = sem("dve_probs_done")
        pool_probs_done = sem("pool_probs_done")
        probs_turned = sem("probs_turned")
        probsT_copied = sem("probsT_copied")
        pv_done = sem("pv_done")
        oT_done = sem("oT_done")
        proj_done = sem("proj_done")
        xr_done = sem("xr_done")
        ms2_ready = sem("ms2_ready")
        std2_ready = sem("std2_ready")
        r2_ready = sem("r2_ready")
        h2_done = sem("h2_done")
        h2_turned = sem("h2_turned")
        h2T_done = sem("h2T_done")
        up_done = sem("up_done")
        tanh_done = sem("tanh_done")
        gated_done = sem("gated_done")
        gated_turned = sem("gated_turned")
        gatedT_done = sem("gatedT_done")
        down_done = sem("down_done")
        row_done = sem("row_done")
        row_out = sem("row_out")
        stats_done = sem("stats_done")

        BANK_H = 4
        BANK_K, BANK_Q = 4, 6
        BANK_V = 0
        BANK_S = 0
        BANK_PT = 4
        BANK_O = 6
        BANK_W = 0
        BANK_H2 = 2

        def bank_up(s):
            return 4 * ((s + 1) % 2)

        block = ctx.enter_context(nc.Block())

        @block.sync
        def _(sp):
            sp.dma_start(wqkv[:], w_qkvT.rearrange("(c p) n -> p c n", p=P)).then_inc(weights_in, 16)
            sp.dma_start(wout[:], w_outT.rearrange("(c p) n -> p c n", p=P)).then_inc(weights_in, 16)
            sp.dma_start(w1[:], w1T.rearrange("(c p) n -> p c n", p=P)).then_inc(weights_in, 16)
            sp.dma_start(w2[:], w2T.rearrange("(c p) n -> p c n", p=P)).then_inc(weights_in, 16)
            full = DFF // P
            sp.dma_start(w3[:, 0:full, :], w3T[0:full * P, :].rearrange("(c p) n -> p c n", p=P)
                         ).then_inc(weights_in, 16)
            sp.dma_start(w3[0:DFF - full * P, full, :], w3T[full * P:DFF, :]).then_inc(weights_in, 16)
            sp.dma_start(gain[:, 0, :], g1).then_inc(weights_in, 16)
            sp.dma_start(gain[:, 1, :], g2).then_inc(weights_in, 16)
        WEIGHTS = 8 * 16

        @block.gpsimd
        def _(pool):
            own = Chain(pool, consts)
            own.step(nc.gpsimd.memset(ones[:], 1.0))
            own.step(nc.gpsimd.memset(zeros[:], 0.0))
            nc.gpsimd.affine_select(out=ident[:], in_=ones[:], compare_op=ALU.is_equal, fill=0.0, base=0,
                                    pattern=[[-1, P]], channel_multiplier=1).then_inc(consts, 1)
            nc.gpsimd.affine_select(out=causal[:], in_=zeros[:], compare_op=ALU.is_ge, fill=-1e30, base=0,
                                    pattern=[[-1, P]], channel_multiplier=1).then_inc(consts, 1)
            nc.gpsimd.affine_select(out=head_half[:], in_=ones[:, 0:GH], compare_op=ALU.is_ge, fill=0.0, base=0,
                                    pattern=[[-FD, GH]], channel_multiplier=1).then_inc(consts, 1)
            pool.wait_ge(consts, 5)
            nc.gpsimd.affine_select(out=head_of[:], in_=head_half[:], compare_op=ALU.is_ge, fill=0.0, base=FD - 1,
                                    pattern=[[FD, GH]], channel_multiplier=-1).then_inc(consts, 1)
            for i in range(ROUNDS):
                for b in range(i * NB, i * NB + NB):
                    rows = bass.IndirectOffsetOnAxis(ap=picked[:, b:b + 1], axis=0)
                    nc.gpsimd.indirect_dma_start(out=xs[:, b, :], out_offset=None, in_=x, in_offset=rows
                                                 ).then_inc(x_in[b], 16)
                    if adding:
                        nc.gpsimd.indirect_dma_start(out=ads[:, b, :], out_offset=None, in_=add, in_offset=rows
                                                     ).then_inc(x_in[b], 16)
                for b in range(i * NB, i * NB + NB):
                    if adding:
                        pool.wait_ge(x_in[b], 32)
                        nc.gpsimd.tensor_tensor(xs[:, b, :], xs[:, b, :], ads[:, b, :], ALU.add
                                                ).then_inc(rows_ready, 1)

            for i in range(ROUNDS):
                def at(s):
                    return i * NB + s + 1

                for s in range(NB):
                    pool.wait_ge(recip_done, at(s))
                    nc.gpsimd.tensor_tensor(
                        att[:, s, DVE_HEADS:FH], att[:, s, DVE_HEADS:FH],
                        rowsum[:, s, DVE_HEADS:FH].unsqueeze(2).to_broadcast([P, FH - DVE_HEADS, P]),
                        ALU.mult).then_inc(pool_probs_done, 1)
                for s in range(NB):
                    pool.wait_ge(row_done, at(s))
                    nc.gpsimd.indirect_dma_start(
                        out=y, out_offset=bass.IndirectOffsetOnAxis(ap=picked[:, at(s) - 1:at(s)], axis=0),
                        in_=row[:, s, :], in_offset=None).then_inc(row_out, 16)
            pool.wait_ge(row_out, B * 16)

        @block.vector
        def _(dve):
            dve.wait_ge(consts, 6)
            own = Chain(dve, dve_own)
            own.step(nc.vector.tensor_reduce(parity[:], head_of[:].rearrange("p (a two) -> p two a", two=2),
                                             AX.X, ALU.add))
            dve.wait_ge(weights_in, WEIGHTS)

            def c(i, n):
                return sm[:, i, n, :]

            def newton(i, r, var, scratch, out, done):
                own.step(nc.vector.tensor_tensor(c(i, scratch), c(i, r), c(i, r), ALU.mult))
                own.step(nc.vector.tensor_tensor(c(i, scratch), c(i, scratch), c(i, var), ALU.mult))
                own.step(nc.vector.tensor_scalar(c(i, scratch), c(i, scratch), -0.5, 1.5, ALU.mult, ALU.add))
                nc.vector.tensor_tensor(c(i, out), c(i, r), c(i, scratch), ALU.mult).then_inc(done, 1)
                dve.wait_ge(done, i + 1)

            for i in range(ROUNDS):
                now = slice(i * NB, (i + 1) * NB)
                for s in range(NB):
                    if adding:
                        dve.wait_ge(rows_ready, i * NB + s + 1)
                    else:
                        dve.wait_ge(x_in[i * NB + s], 16)
                    nc.vector.bn_stats(stats[:, i * NB + s, :], xs[:, i * NB + s, :]).then_inc(stats_done, 1)
                dve.wait_ge(stats_done, (i + 1) * NB)
                me, m2e, mo, m2o = (stats[:, now, n] for n in (1, 2, 4, 5))
                own.step(nc.vector.tensor_tensor(c(i, 0), me, mo, ALU.add))
                own.step(nc.vector.tensor_tensor(c(i, 1), me, mo, ALU.subtract))
                own.step(nc.vector.tensor_tensor(c(i, 2), m2e, m2o, ALU.add))
                own.step(nc.vector.scalar_tensor_tensor(c(i, 1), c(i, 1), 0.25, c(i, 1), ALU.mult, ALU.mult))
                own.step(nc.vector.scalar_tensor_tensor(c(i, 2), c(i, 2), 1.0 / D, c(i, 1), ALU.mult, ALU.add))
                nc.vector.tensor_scalar(c(i, 3), c(i, 2), LN_EPS, None, ALU.add).then_inc(var_ready, 1)
                dve.wait_ge(std_ready, i + 1)
                own.step(nc.vector.reciprocal(c(i, 5), c(i, 4)))
                newton(i, 5, 3, 6, 7, rstd_ready)
                own.step(nc.vector.tensor_tensor(c(i, 8), c(i, 2), c(i, 7), ALU.mult))
                own.step(nc.vector.tensor_tensor(c(i, 8), c(i, 8), c(i, 7), ALU.mult))
                own.step(nc.vector.scalar_tensor_tensor(c(i, 10), c(i, 0), -0.5, c(i, 7), ALU.mult, ALU.mult))
                nc.vector.tensor_scalar(c(i, 8), c(i, 8), RMS_EPS, None, ALU.add).then_inc(ms_ready, 1)
                dve.wait_ge(rms_ready, i + 1)
                own.step(nc.vector.reciprocal(c(i, 5), c(i, 9)))
                newton(i, 5, 8, 6, 11, scale_ready)

            for i in range(ROUNDS):
                def at(s):
                    return i * NB + s + 1

                for s in range(NB):
                    for g in range(NC):
                        if s == 0 and g == 0:
                            dve.wait_ge(qk_done, i + 1)
                        last = nc.vector.tensor_tensor(
                            kspread[:, s, g],
                            ps[:, BANK_K + g, s * P:(s + 1) * P].unsqueeze(1).to_broadcast([P, GH, P]),
                            head_of[:].unsqueeze(2).to_broadcast([P, GH, P]), ALU.mult)
                    last.then_inc(spread_done, 1)
                def mask(s):
                    dve.wait_ge(scores_done, at(s))
                    nc.vector.tensor_tensor(
                        att[:, s], ps[:, BANK_S:BANK_S + 4, :].rearrange("p b (h k) -> p (b h) k", k=P),
                        causal[:].unsqueeze(1).to_broadcast([P, FH, P]), ALU.add).then_inc(masked_done, 1)
                    dve.wait_ge(masked_done, at(s))
                    own.step(nc.vector.tensor_reduce(rowmax[:, s], att[:, s], AX.X, ALU.max, negate=True))
                    nc.vector.tensor_scalar(rowmax[:, s], rowmax[:, s], ATT_SCALE, None, ALU.mult).then_inc(max_done, 1)

                def normalize(s):
                    dve.wait_ge(exp_done, at(s))
                    nc.vector.reciprocal(rowsum[:, s], rowsum[:, s]).then_inc(recip_done, 1)
                    dve.wait_ge(recip_done, at(s))
                    nc.vector.tensor_tensor(
                        att[:, s, 0:DVE_HEADS], att[:, s, 0:DVE_HEADS],
                        rowsum[:, s, 0:DVE_HEADS].unsqueeze(2).to_broadcast([P, DVE_HEADS, P]),
                        ALU.mult).then_inc(dve_probs_done, 1)

                mask(0)
                mask(1)
                for s in range(NB):
                    normalize(s)
                    if s + 2 < NB:
                        mask(s + 2)
                for s in range(NB):
                    o = ps[:, BANK_O + s % 2, :].rearrange("p (g two t) -> p two g t", g=NC, two=2)
                    dve.wait_ge(pv_done, at(s))
                    own.step(nc.vector.tensor_scalar(odd[:, s % 2], o[:, 1], parity[:, 1:2], None, ALU.mult))
                    nc.vector.scalar_tensor_tensor(oT[:, :, s, :], o[:, 0], parity[:, 0:1], odd[:, s % 2],
                                                   ALU.mult, ALU.add).then_inc(oT_done, 1)
                for s in range(NB):
                    dve.wait_ge(proj_done, at(s))
                    nc.vector.tensor_tensor(xr[:, s, :], ps[:, BANK_W + s, 0:D], xh[:, at(s) - 1, :],
                                            ALU.add).then_inc(xr_done, 1)
                    dve.wait_ge(xr_done, at(s))
                    own.step(nc.vector.tensor_tensor_reduce(out=sq[:, s, :], in0=xr[:, s, :], in1=xr[:, s, :],
                                                            scale=1.0, scalar=0.0, op0=ALU.mult, op1=ALU.add,
                                                            accum_out=sm[:, i, 12, s:s + 1]))
                nc.vector.tensor_scalar(c(i, 13), c(i, 12), 1.0 / D, RMS_EPS, ALU.mult, ALU.add).then_inc(ms2_ready, 1)
                dve.wait_ge(std2_ready, i + 1)
                own.step(nc.vector.reciprocal(c(i, 5), c(i, 14)))
                newton(i, 5, 13, 6, 15, r2_ready)

                def gate(s):
                    u = bank_up(s)
                    dve.wait_ge(tanh_done, at(s))
                    own.step(nc.vector.scalar_tensor_tensor(
                        act1[:, s % 2].rearrange("p (n f) -> p n f", n=2), sig[:, s % 2].rearrange("p (n f) -> p n f", n=2),
                        1.0, ps[:, u:u + 2, 0:DFF_HALF], ALU.add, ALU.mult))
                    if s >= 2:
                        dve.wait_ge(gated_turned, at(s - 2))
                    nc.vector.scalar_tensor_tensor(
                        gated[:, s % 2].rearrange("p (n f) -> p n f", n=2), act1[:, s % 2].rearrange("p (n f) -> p n f", n=2),
                        0.5, ps[:, u + 2:u + 4, 0:DFF_HALF], ALU.mult, ALU.mult).then_inc(gated_done, 1)

                def final_row(s):
                    u = bank_up(s)
                    dve.wait_ge(down_done, at(s))
                    own.step(nc.vector.tensor_tensor(proc[:, s, :], ps[:, u + 2, 0:D], xr[:, s, :], ALU.add))
                    if i > 0:
                        dve.wait_ge(row_out, i * NB * 16)
                    nc.vector.scalar_tensor_tensor(row[:, s, :], proc[:, s, :], 0.5, xs[:, at(s) - 1, :],
                                                   ALU.mult, ALU.add).then_inc(row_done, 1)

                gate(0)
                gate(1)
                for s in range(NB):
                    final_row(s)
                    if s + 2 < NB:
                        gate(s + 2)

        @block.scalar
        def _(act):
            act.wait_ge(weights_in, WEIGHTS)
            def norms(i):
                act.wait_ge(var_ready, i + 1)
                nc.scalar.activation(sm[:, i, 4, :], sm[:, i, 3, :], ACT.Sqrt).then_inc(std_ready, 1)
                act.wait_ge(ms_ready, i + 1)
                nc.scalar.activation(sm[:, i, 9, :], sm[:, i, 8, :], ACT.Sqrt).then_inc(rms_ready, 1)
                act.wait_ge(scale_ready, i + 1)
                for s in range(NB):
                    nc.scalar.activation(xh[:, i * NB + s, :], xs[:, i * NB + s, :], ACT.Identity, scale=sm[:, i, 7, s:s + 1],
                                         bias=sm[:, i, 10, s:s + 1]).then_inc(xh_done, 1)
                for s in range(NB):
                    act.wait_ge(xh_done, i * NB + s + 1)
                    nc.scalar.activation(hn[:, i * NB + s, :], xh[:, i * NB + s, :], ACT.Copy, scale=sm[:, i, 11, s:s + 1]
                                         ).then_inc(hn_done, 1)

            norms(0)

            for i in range(ROUNDS):
                def at(s):
                    return i * NB + s + 1

                act.wait_ge(h_turned, i + 1)
                for g in range(NC):
                    nc.scalar.activation(hT[:, g].rearrange("p s t -> p (s t)"), ps[:, BANK_H + g, :], ACT.Copy,
                                         scale=gain[:, 0, g:g + 1]).then_inc(hT_done, 1)
                if i + 1 < ROUNDS:
                    norms(i + 1)
                act.wait_ge(qk_done, i + 1)
                for g in range(NC):
                    nc.scalar.copy(qT[:, g].rearrange("p s t -> p (s t)"), ps[:, BANK_Q + g, :]).then_inc(qT_copied, 1)
                act.wait_ge(v_done, i + 1)
                nc.scalar.copy(v[:].rearrange("p (b s) d -> p b (s d)", b=2),
                               ps[:, BANK_V:BANK_V + 2, :]).then_inc(v_copied, 1)
                for s in range(NB):
                    act.wait_ge(max_done, at(s))
                    for h in range(FH):
                        last = nc.scalar.activation(att[:, s, h], att[:, s, h], ACT.Exp, scale=ATT_SCALE,
                                                    bias=rowmax[:, s, h:h + 1], accum_out=rowsum[:, s, h:h + 1])
                    last.then_inc(exp_done, 1)
                for s in range(NB):
                    for half in range(2):
                        act.wait_ge(probs_turned, (i * NB + s) * 2 + half + 1)
                        if s >= 2 and half == 0:
                            act.wait_ge(pv_done, at(s - 2))
                        nc.scalar.copy(attT[:, s % 2, half * GH:(half + 1) * GH].rearrange("p (b h) t -> p b (h t)", b=2),
                                       ps[:, BANK_PT:BANK_PT + 2, :]).then_inc(probsT_copied, 1)
                act.wait_ge(ms2_ready, i + 1)
                nc.scalar.activation(sm[:, i, 14, :], sm[:, i, 13, :], ACT.Sqrt).then_inc(std2_ready, 1)
                act.wait_ge(r2_ready, i + 1)
                for s in range(NB):
                    nc.scalar.activation(hn[:, at(s) - 1, :], xr[:, s, :], ACT.Copy, scale=sm[:, i, 15, s:s + 1]
                                         ).then_inc(h2_done, 1)
                act.wait_ge(h2_turned, i + 1)
                for g in range(NC):
                    nc.scalar.activation(hT[:, g].rearrange("p s t -> p (s t)"), ps[:, BANK_H2 + g, :], ACT.Copy,
                                         scale=gain[:, 1, g:g + 1]).then_inc(h2T_done, 1)

                def tanh(s):
                    act.wait_ge(up_done, at(s))
                    u = bank_up(s)
                    if s >= 2:
                        act.wait_ge(gated_done, at(s - 2))
                    nc.scalar.activation(sig[:, s % 2].rearrange("p (n f) -> p n f", n=2), ps[:, u:u + 2, 0:DFF_HALF],
                                         ACT.Tanh, scale=0.5).then_inc(tanh_done, 1)

                def copy_gatedT(s):
                    u = bank_up(s)
                    act.wait_ge(gated_turned, at(s))
                    if s >= 2:
                        act.wait_ge(down_done, at(s - 2))
                    nc.scalar.copy(gatedT[:, s % 2, 0:4, :].rearrange("p a t -> p (a t)"), ps[:, u, :])
                    nc.scalar.copy(gatedT[:, s % 2, 4, :], ps[:, u + 1, 0:P])
                    nc.scalar.copy(gatedT[0:DFF - 5 * P, s % 2, 5, :], ps[0:DFF - 5 * P, u + 1, P:2 * P]
                                   ).then_inc(gatedT_done, 1)

                tanh(0)
                tanh(1)
                for s in range(NB):
                    copy_gatedT(s)
                    if s + 2 < NB:
                        tanh(s + 2)

        @block.tensor
        def _(pe):
            pe.wait_ge(weights_in, WEIGHTS)
            pe.wait_ge(consts, 6)
            for i in range(ROUNDS):
                def at(s):
                    return i * NB + s + 1

                for s in range(NB):
                    pe.wait_ge(hn_done, at(s))
                    if s == 0 and i > 0:
                        pe.wait_ge(row_done, i * NB - 1)
                    for g in range(NC):
                        last = nc.tensor.transpose(ps[:, BANK_H + g, s * P:(s + 1) * P],
                                                   hn[:, at(s) - 1, g * P:(g + 1) * P], ident[:])
                last.then_inc(h_turned, 1)
                pe.wait_ge(hT_done, i * NC + NC)
                for which, bank in ((1, BANK_K), (0, BANK_Q)):
                    for g in range(NC):
                        for c in range(NC):
                            last = nc.tensor.matmul(ps[:, bank + g, :], wqkv[:, c, which * D + g * P:which * D + (g + 1) * P],
                                                    hT[:, c].rearrange("p s t -> p (s t)"), start=(c == 0),
                                                    stop=(c == NC - 1))
                last.then_inc(qk_done, 1)
                if i > 0:
                    pe.wait_ge(row_done, i * NB)
                for s in range(NB):
                    for c in range(NC):
                        last = nc.tensor.matmul(ps[:, BANK_V + s // 2, (s % 2) * D:(s % 2 + 1) * D], hT[:, c, s, :],
                                                wqkv[:, c, 2 * D:3 * D], start=(c == 0), stop=(c == NC - 1))
                last.then_inc(v_done, 1)
                pe.wait_ge(qT_copied, i * NC + NC)
                pe.wait_ge(v_copied, i + 1)
                for s in range(NB):
                    pe.wait_ge(spread_done, at(s))
                    if s >= 1:
                        pe.wait_ge(masked_done, at(s - 1))
                    for h4 in range(FH // 4):
                        g = h4 // 2
                        last = nc.tensor.matmul(ps[:, BANK_S + h4, :], qT[:, g, s, :],
                                                kspread[:, s, g, (h4 % 2) * 4:(h4 % 2) * 4 + 4].rearrange("p j t -> p (j t)"),
                                                start=True, stop=True)
                    last.then_inc(scores_done, 1)
                for s in range(NB):
                    pe.wait_ge(dve_probs_done, at(s))
                    pe.wait_ge(pool_probs_done, at(s))
                    for half in range(2):
                        if s > 0 or half > 0:
                            pe.wait_ge(probsT_copied, (i * NB + s) * 2 + half)
                        for j in range(GH):
                            last = nc.tensor.transpose(ps[:, BANK_PT + j // 4, (j % 4) * P:(j % 4 + 1) * P],
                                                       att[:, s, half * GH + j, :], ident[:])
                        last.then_inc(probs_turned, 1)
                    for half in range(2):
                        pe.wait_ge(probsT_copied, (i * NB + s) * 2 + half + 1)
                        if s >= 2 and half == 0:
                            pe.wait_ge(oT_done, at(s - 2))
                        for j in (0, 2, 4, 6, 1, 3, 5, 7):
                            h = half * GH + j
                            pair = j // 2
                            base = (half * 2 + j % 2) * P
                            ch = half * P + pair * 2 * FD
                            last = nc.tensor.matmul(ps[pair * 32:pair * 32 + 32, BANK_O + s % 2, base:base + P],
                                                    v[:, s, ch:ch + 2 * FD], attT[:, s % 2, h, :], start=True, stop=True)
                    last.then_inc(pv_done, 1)
                for s in range(NB):
                    pe.wait_ge(oT_done, at(s))
                    for c in range(NC):
                        last = nc.tensor.matmul(ps[:, BANK_W + s, 0:D], oT[:, c, s, :],
                                                wout[:, c, :], start=(c == 0), stop=(c == NC - 1))
                    last.then_inc(proj_done, 1)
                for s in range(NB):
                    pe.wait_ge(h2_done, at(s))
                    for g in range(NC):
                        last = nc.tensor.transpose(ps[:, BANK_H2 + g, s * P:(s + 1) * P],
                                                   hn[:, at(s) - 1, g * P:(g + 1) * P], ident[:])
                last.then_inc(h2_turned, 1)
                pe.wait_ge(h2T_done, i * NC + NC)

                def up(s):
                    u = bank_up(s)
                    if s >= 2:
                        pe.wait_ge(row_done, at(s - 2))
                    for w, bank in ((w1, u), (w2, u + 2)):
                        for n in range(2):
                            for c in range(NC):
                                last = nc.tensor.matmul(ps[:, bank + n, 0:DFF_HALF], hT[:, c, s, :],
                                                        w[:, c, n * DFF_HALF:(n + 1) * DFF_HALF], start=(c == 0),
                                                        stop=(c == NC - 1))
                    last.then_inc(up_done, 1)

                def down(s):
                    u = bank_up(s)
                    pe.wait_ge(gated_done, at(s))
                    for f in range(DFF_TILES):
                        m = min(P, DFF - f * P)
                        last = nc.tensor.transpose(ps[0:m, u + f // 4, (f % 4) * P:(f % 4 + 1) * P],
                                                   gated[:, s % 2, f * P:f * P + m], ident[:])
                    last.then_inc(gated_turned, 1)
                    pe.wait_ge(gatedT_done, at(s))
                    for f in range(DFF_TILES):
                        m = min(P, DFF - f * P)
                        last = nc.tensor.matmul(ps[:, u + 2, 0:D], gatedT[0:m, s % 2, f, :], w3[0:m, f, :],
                                                start=(f == 0), stop=(f == DFF_TILES - 1))
                    last.then_inc(down_done, 1)

                up(0)
                up(1)
                for s in range(NB):
                    down(s)
                    if s + 2 < NB:
                        up(s + 2)


def project(nc, tag, x, lowrank, biases, v_bias, qk, v_dram):
    with ExitStack() as ctx:
        used = ctx.enter_context(cleared_semaphores(nc))

        def sb(name, shape, dt=F32):
            return ctx.enter_context(nc.sbuf_tensor(f"{tag}_{name}", shape, dt))

        def sem(name):
            handle = nc.alloc_semaphore(f"{tag}_{name}")
            used.append(handle)
            return handle

        NQ = 4
        TQ = T // NQ
        facV = sb("facV", [P, 3, NG, P])
        facU = sb("facU", [P, 3, NG, P])
        w = sb("w", [P, 3, NG, P])
        bias = sb("bias", [P, 2, NG])
        vb = sb("vb", [P, D])
        ones = sb("ones", [P, P])
        ident = sb("ident", [P, P])
        xb = sb("x", [P, 2, T, D])
        stats = sb("stats", [P, 2, T, 6])
        sm = sb("small", [P, 2, 8, T])
        xT = sb("xT", [P, 2, NG, TQ * P])
        hi = sb("hi", [P, 2, 2 * NG, TQ * P], F32R)
        lo = sb("lo", [P, 2, 2 * NG, TQ * P], F32R)
        v = sb("v", [P, 2, TQ, D])
        pT = ctx.enter_context(nc.psum_tensor(f"{tag}_pT", [P, NG, 512], F32))
        pqk = ctx.enter_context(nc.psum_tensor(f"{tag}_pqk", [P, 2 * NG, 512], F32))
        pv = ctx.enter_context(nc.psum_tensor(f"{tag}_pv", [P, 2, 512], F32))

        consts = sem("consts")
        zeroed = sem("zeroed")
        factors_in = sem("factors_in")
        w_done = sem("w_done")
        w_copied = sem("w_copied")
        x_in = [sem(f"x_in{k}") for k in range(2)]
        stats_done = sem("stats_done")
        dve_own = sem("dve_own")
        var_ready = sem("var_ready")
        std_ready = sem("std_ready")
        affine_ready = sem("affine_ready")
        xh_done = sem("xh_done")
        turned = sem("turned")
        xT_copied = sem("xT_copied")
        qk_done = sem("qk_done")
        v_done = sem("v_done")
        hi_done = sem("hi_done")
        lo_done = sem("lo_done")
        v_copied = sem("v_copied")
        hi_out = [sem(f"hi_out{k}") for k in range(2)]
        lo_out = [sem(f"lo_out{k}") for k in range(2)]
        v_out = [sem(f"v_out{k}") for k in range(2)]
        FACTORS = 2 * 3 * H * 16 + 3 * 16
        OWN = 10

        block = ctx.enter_context(nc.Block())

        @block.gpsimd
        def _(pool):
            nc.gpsimd.memset(ones[:], 1.0).then_inc(consts, 1)
            pool.wait_ge(consts, 1)
            nc.gpsimd.affine_select(out=ident[:], in_=ones[:], compare_op=ALU.is_equal, fill=0.0, base=0,
                                    pattern=[[-1, P]], channel_multiplier=1).then_inc(consts, 1)

        @block.sync
        def _(sp):
            sp.wait_ge(zeroed, 2)
            for n, (u, vt) in enumerate(lowrank):
                for h in range(H):
                    r = (h % HG) * DH
                    sp.dma_start(facV[r:r + DH, n, h // HG, r:r + DH], vt[h]).then_inc(factors_in, 16)
                    sp.dma_start(facU[r:r + DH, n, h // HG, r:r + DH], u[h]).then_inc(factors_in, 16)
            for n in range(2):
                sp.dma_start(bias[:, n, :], biases[n]).then_inc(factors_in, 16)
            sp.dma_start(vb[:], v_bias.partition_broadcast(P)).then_inc(factors_in, 16)

            def load(i, k):
                src = x[bass.ds((i * 2 + k) * S, S), :].rearrange("(t p) d -> p t d", p=P)
                sp.dma_start(xb[:, k], src).then_inc(x_in[k], 16)

            def store(i, k, n):
                at = (i * 2 + k) * NQ + n + 1
                tok = slice(n * TQ * P, (n + 1) * TQ * P)
                dst = qk[bass.ds(i * 2 + k, 1)].rearrange("a part g c s -> part c (a g) s")
                sp.wait_ge(hi_done, at * 4)
                sp.dma_start(dst[0, :, :, tok], hi[:, n % 2].bitcast(F32)).then_inc(hi_out[n % 2], 16)
                sp.wait_ge(lo_done, at * 4)
                sp.dma_start(dst[1, :, :, tok], lo[:, n % 2].bitcast(F32)).then_inc(lo_out[n % 2], 16)
                sp.wait_ge(v_copied, at * 2)
                sp.dma_start(v_dram[bass.ds((i * 2 + k) * S + n * TQ * P, TQ * P), :]
                             .rearrange("(t p) d -> p t d", p=P), v[:, n % 2]).then_inc(v_out[n % 2], 16)

            load(0, 0)
            load(0, 1)
            with sp.Fori(0, B // 2 - 1) as i:
                for k in range(2):
                    for n in range(NQ):
                        store(i, k, n)
                    load(i + 1, k)
            for k in range(2):
                for n in range(NQ):
                    store(B // 2 - 1, k, n)
            for s in (*hi_out, *lo_out, *v_out):
                sp.wait_ge(s, B * NQ // 2 * 16)

        @block.vector
        def _(dve):
            nc.vector.memset(facV[:], 0.0).then_inc(zeroed, 1)
            nc.vector.memset(facU[:], 0.0).then_inc(zeroed, 1)
            dve.wait_ge(w_done, 1)
            nc.vector.tensor_copy(w[:, 0:2].rearrange("p n g c -> p (n g c)"), pT[:, 0, :]).then_inc(w_copied, 1)
            nc.vector.tensor_copy(w[:, 2].rearrange("p g c -> p (g c)"), pT[:, 1, 0:NG * P]).then_inc(w_copied, 1)

            def statistics(k, loads, tiles):
                dve.wait_ge(x_in[k], loads * 16)
                for t in tiles:
                    nc.vector.bn_stats(stats[:, k, t, :], xb[:, k, t, :]).then_inc(stats_done, 1)

            def variances(b, k, first_batch=False):
                own = Chain(dve, dve_own, b * OWN)
                c = [sm[:, k, n, :] for n in range(8)]
                dve.wait_ge(stats_done, (b + 1) * T)
                if not first_batch:
                    dve.wait_ge(xh_done, (b - 1) * T)
                me, m2e, mo, m2o = (stats[:, k, :, n] for n in (1, 2, 4, 5))
                own.step(nc.vector.tensor_tensor(c[0], me, mo, ALU.add))
                own.step(nc.vector.tensor_tensor(c[1], me, mo, ALU.subtract))
                own.step(nc.vector.tensor_tensor(c[2], m2e, m2o, ALU.add))
                own.step(nc.vector.scalar_tensor_tensor(c[1], c[1], 0.25, c[1], ALU.mult, ALU.mult))
                own.step(nc.vector.tensor_scalar(c[2], c[2], 1.0 / D, LN_EPS, ALU.mult, ALU.add))
                nc.vector.tensor_tensor(c[3], c[1], c[2], ALU.add).then_inc(var_ready, 1)

            def scales(b, k):
                own = Chain(dve, dve_own, b * OWN + 5)
                c = [sm[:, k, n, :] for n in range(8)]
                dve.wait_ge(std_ready, b + 1)
                own.step(nc.vector.reciprocal(c[5], c[4]))
                own.step(nc.vector.tensor_tensor(c[6], c[5], c[5], ALU.mult))
                own.step(nc.vector.tensor_tensor(c[6], c[6], c[3], ALU.mult))
                own.step(nc.vector.tensor_scalar(c[6], c[6], -0.5, 1.5, ALU.mult, ALU.add))
                own.step(nc.vector.tensor_tensor(c[6], c[5], c[6], ALU.mult))
                nc.vector.scalar_tensor_tensor(c[7], c[0], -0.5, c[6], ALU.mult, ALU.mult
                                               ).then_inc(affine_ready, 1)

            statistics(0, 1, range(T))
            variances(0, 0, first_batch=True)
            scales(0, 0)

            def pair(i, last_pair=False):
                for k in range(2):
                    b = i * 2 + k
                    for n in range(NQ):
                        at = b * NQ + n
                        dve.wait_ge(hi_done, at * 4)
                        if n >= 2:
                            dve.wait_ge(lo_out[n % 2], (i * 2 + k) * 32 + (n // 2) * 16)
                            dve.wait_ge(v_out[n % 2], (i * 2 + k) * 32 + (n // 2) * 16)
                        else:
                            dve.wait_ge(lo_out[n % 2], (i * 2 + k) * 32)
                            dve.wait_ge(v_out[n % 2], (i * 2 + k) * 32)
                        for m in range(2 * NG):
                            dve.wait_ge(hi_done, at * 4 + m + 1)
                            nc.vector.scalar_tensor_tensor(
                                lo[:, n % 2, m], pqk[:, m, :], bias[:, m // NG, m % NG:m % NG + 1],
                                hi[:, n % 2, m].bitcast(F32), ALU.add, ALU.subtract).then_inc(lo_done, 1)
                        dve.wait_ge(v_done, at + 1)
                        for m in range(2):
                            nc.vector.tensor_tensor(v[:, n % 2, 2 * m:2 * m + 2, :],
                                                    pv[:, m, :].rearrange("p (t d) -> p t d", t=2),
                                                    vb[:].unsqueeze(1).to_broadcast([P, 2, D]), ALU.add
                                                    ).then_inc(v_copied, 1)
                        if k == 0 or not last_pair:
                            if n < 2:
                                statistics(1 - k, i + 1 + k, range(n * T // 2, (n + 1) * T // 2))
                            if n == 1:
                                variances(b + 1, 1 - k)
                            if n == 2:
                                scales(b + 1, 1 - k)

            with dve.Fori(0, B // 2 - 1) as i:
                pair(i)
            pair(B // 2 - 1, last_pair=True)

        @block.scalar
        def _(act):
            act.wait_ge(factors_in, FACTORS)

            def roots(b, k):
                act.wait_ge(var_ready, b + 1)
                nc.scalar.activation(sm[:, k, 4, :], sm[:, k, 3, :], ACT.Sqrt).then_inc(std_ready, 1)

            def normal(b, k, n):
                if n == 0:
                    act.wait_ge(affine_ready, b + 1)
                for t in range(n * TQ, (n + 1) * TQ):
                    nc.scalar.activation(xb[:, k, t, :], xb[:, k, t, :], ACT.Identity,
                                         scale=sm[:, k, 6, t:t + 1], bias=sm[:, k, 7, t:t + 1]).then_inc(xh_done, 1)

            roots(0, 0)
            normal(0, 0, 0)

            def pair(i, last_pair=False):
                for k in range(2):
                    b = i * 2 + k
                    for n in range(NQ):
                        at = b * NQ + n
                        act.wait_ge(turned, at + 1)
                        for g in range(NG):
                            nc.scalar.copy(xT[:, n % 2, g, :], pT[:, g, :]).then_inc(xT_copied, 1)
                        if n + 1 < NQ:
                            normal(b, k, n + 1)
                        elif k == 0 or not last_pair:
                            normal(b + 1, 1 - k, 0)
                        act.wait_ge(hi_out[n % 2], b * 32 + (n // 2) * 16)
                        for m in range(2 * NG):
                            act.wait_ge(qk_done, at * 4 + m + 1)
                            nc.scalar.activation(hi[:, n % 2, m], pqk[:, m, :], ACT.Identity,
                                                 bias=bias[:, m // NG, m % NG:m % NG + 1]).then_inc(hi_done, 1)
                        if n == 2 and (k == 0 or not last_pair):
                            roots(b + 1, 1 - k)

            with act.Fori(0, B // 2 - 1) as i:
                pair(i)
            pair(B // 2 - 1, last_pair=True)

        @block.tensor
        def _(pe):
            pe.wait_ge(consts, 2)
            pe.wait_ge(factors_in, FACTORS)
            for n in range(3):
                for g in range(NG):
                    at = (n * NG + g) * P
                    last = nc.tensor.matmul(pT[:, at // 512, at % 512:at % 512 + P], facV[:, n, g, :],
                                            facU[:, n, g, :], start=True, stop=True)
            last.then_inc(w_done, 1)
            pe.wait_ge(w_copied, 2)
            def turn(b, k, n):
                for t in range(TQ):
                    if t == 0 or n == 0:
                        pe.wait_ge(xh_done, b * T + n * TQ + TQ)
                    for g in range(NG):
                        last = nc.tensor.transpose(pT[:, g, t * P:(t + 1) * P],
                                                   xb[:, k, n * TQ + t, g * P:(g + 1) * P], ident[:])
                last.then_inc(turned, 1)

            turn(0, 0, 0)

            def pair(i, last_pair=False):
                for k in range(2):
                    b = i * 2 + k

                    for n in range(NQ):
                        at = b * NQ + n
                        pe.wait_ge(xT_copied, at * NG + NG)
                        for m in range(2 * NG):
                            pe.wait_ge(lo_done, (at - 1) * 4 + m + 1) if n > 0 else pe.wait_ge(lo_done, at * 4)
                            nc.tensor.matmul(pqk[:, m, :], w[:, m // NG, m % NG, :], xT[:, n % 2, m % NG, :],
                                             start=True, stop=True).then_inc(qk_done, 1)
                        if n + 1 < NQ:
                            turn(b, k, n + 1)
                        elif k == 0 or not last_pair:
                            turn(b + 1, 1 - k, 0)
                        pe.wait_ge(v_copied, at * 2)
                        for t in range(TQ):
                            for g in range(NG):
                                last = nc.tensor.matmul(pv[:, t // 2, (t % 2) * D + g * P:(t % 2) * D + (g + 1) * P],
                                                        xT[:, n % 2, g, t * P:(t + 1) * P], w[:, 2, g, :],
                                                        start=True, stop=True)
                        last.then_inc(v_done, 1)

            with pe.Fori(0, B // 2 - 1) as i:
                pair(i)
            pair(B // 2 - 1, last_pair=True)


RAW, DVE_SHARE = 1, 4
ADD_LAG = 5
COPY_O_AT = 3
CLOSE_AT = 5
COPY_Z_AT = 10
TURN_Z_AT = (12, 13)
INVERT_AT = 14
TURN_O_AT = (15, 16)
NORMALIZE_AT = 18
STORE_AT = 24
MAX_AT = (24, 31, 40, 56)


def attend(nc, tag, qk, v_dram, out):
    UQ = 512
    NU = S // UQ
    NC = S // P
    QT = UQ // P
    TILES = NC * HG
    BU = NG * NU
    STACK = 3 * DH
    RING = 8 * HG
    PV_LAG = 9
    MAX_STEP = 1
    PV_GROUP = 2
    PV_TAIL = (TILES - PV_LAG) // PV_GROUP * PV_GROUP
    LEAD = TILES // 4
    NQB = 4
    raw_chunks = range(NC - RAW, NC)
    PARTS = RAW + 2
    dve_tiles = [j for j in range((NC - RAW) * HG) if (j // HG + j % HG) % DVE_SHARE == 0]
    pool_tiles = [j for j in range((NC - RAW) * HG) if j not in dve_tiles]

    def additions(tiles):
        found, first, last = {}, {}, {}
        for j in tiles:
            h = j % HG
            if h not in first:
                first[h] = j
            else:
                found[j] = (None if h in last else first[h], len(found), last.get(h))
                last[h] = len(found) - 1
        return found

    def used_by(adds, j):
        if j in adds:
            return adds[j][1] + 1
        return next(n for first, n, _ in adds.values() if first == j) + 1

    pool_adds, dve_adds = additions(pool_tiles), additions(dve_tiles)
    SCALE = float(DH) ** -0.5
    with ExitStack() as ctx:
        used = ctx.enter_context(cleared_semaphores(nc))

        def sb(name, shape, dt=F32):
            return ctx.enter_context(nc.sbuf_tensor(f"{tag}_{name}", shape, dt))

        def psum(name, shape):
            return ctx.enter_context(nc.psum_tensor(f"{tag}_{name}", shape, F32))

        def sem(name):
            handle = nc.alloc_semaphore(f"{tag}_{name}")
            used.append(handle)
            return handle

        qs = sb("qs", [STACK + 1, NQB, HG, UQ], F32R)
        ks = sb("ks", [STACK + 1, NG, HG, S], F32R)
        v = sb("v", [P, NG, NC, P])
        probs = sb("probs", [P, RING, UQ])
        pool_sum = sb("pool_sum", [P, HG, UQ])
        dve_sum = sb("dve_sum", [P, HG, UQ])
        part_max = sb("part_max", [P, HG, QT, 2])
        neg_max = sb("neg_max", [P, HG, QT])
        max_row = sb("max_row", [QT, HG, P], F32R)
        ones = sb("ones", [P, P])
        ident = sb("ident", [P, P])
        oT = sb("oT", [P, UQ])
        zT = sb("zT", [P, UQ])
        rz = sb("rz", [P, QT, HG])
        o = sb("o", [P, 2, QT, HG, DH])
        ps_max = psum("ps_max", [P, 2, 2, 512])
        ps_s = psum("ps_s", [P, 2, UQ])
        ps_acc = psum("ps_acc", [P, UQ])
        ps_misc = psum("ps_misc", [P, 512])

        load_turn = sem("load_turn")
        consts = sem("consts")
        ones_row = sem("ones_row")
        q_in = [sem(f"q_in{n}") for n in range(NQB)]
        k_in = [sem(f"k_in{n}") for n in range(NG)]
        v_in = [sem(f"v_in{n}") for n in range(NG)]
        max_scores = sem("max_scores")
        part_max_done = sem("part_max_done")
        neg_max_done = sem("neg_max_done")
        max_turned = sem("max_turned")
        max_row_done = sem("max_row_done")
        max_in = [sem(f"max_in{h}") for h in range(HG)]
        scores = sem("scores")
        exp_done = sem("exp_done")
        pv_done = sem("pv_done")
        pool_added = sem("pool_added")
        dve_added = sem("dve_added")
        z_done = sem("z_done")
        oT_done = sem("oT_done")
        zT_done = sem("zT_done")
        z_turned = sem("z_turned")
        rz_done = sem("rz_done")
        o_turned = sem("o_turned")
        o_done = sem("o_done")
        o_out = [sem(f"o_out{n}") for n in range(2)]

        adds_pool, adds_dve = len(pool_adds), len(dve_adds)

        block = ctx.enter_context(nc.Block())

        @block.sync
        def _(sp):
            def load_q(b, un):
                g, u, k = un // NU, un % NU, un % NQB
                src = qk[bass.ds(b, 1)].rearrange("a part g (h d) s -> part g d (a h) s", h=HG)
                cols = slice(u * UQ, (u + 1) * UQ)
                for r, part in enumerate((0, 1, 0)):
                    sp.dma_start(qs[r * DH:(r + 1) * DH, k].bitcast(F32), src[part, g, :, :, cols]
                                 ).then_inc(q_in[k], 16)

            def load_kv(b, g):
                src = qk[bass.ds(b, 1)].rearrange("a part g (h d) s -> part g d (a h) s", h=HG)
                for r, part in enumerate((0, 0, 1)):
                    sp.dma_start(ks[r * DH:(r + 1) * DH, g].bitcast(F32), src[part, NG + g]).then_inc(k_in[g], 16)
                sp.dma_start(v[:, g], v_dram[bass.ds(b * S, S), g * P:(g + 1) * P]
                             .rearrange("(c p) d -> p c d", p=P)).then_inc(v_in[g], 16)

            def max_rows(b, un):
                n = b * BU + un + 1
                for h in range(HG):
                    sp.wait_ge(max_row_done, n * HG + h + 1)
                    sp.dma_start(qs[STACK:STACK + 1, (un + 1) % NQB, h, :].bitcast(F32)
                                 .rearrange("a (t q) -> a t q", t=QT),
                                 max_row[:, h, :].bitcast(F32)).then_inc(max_in[h], 16)

            load_q(0, 0)
            load_kv(0, 0)
            load_q(0, 1)
            load_kv(0, 1)
            load_q(0, 2)
            max_rows(0, -1)

            def batch(b, last=False):
                for un in range(BU):
                    if un + 3 < BU or not last:
                        sp.wait_ge(scores, (b * BU + un) * TILES)
                        sp.sem_inc(load_turn, 1)
                        load_q(b + (un + 3) // BU, (un + 3) % BU)
                    if un == NU and not last:
                        sp.wait_ge(pv_done, (b * BU + un) * TILES)
                        sp.sem_inc(load_turn, 1)
                        load_kv(b + 1, 0)
                    if un + 1 < BU or not last:
                        max_rows(b, un)
                if not last:
                    sp.wait_ge(pv_done, (b + 1) * BU * TILES)
                    sp.sem_inc(load_turn, 1)
                    load_kv(b + 1, 1)

            batch(0)
            with sp.Fori(1, B - 1) as b:
                batch(b)
            batch(B - 1, last=True)

        @block.gpsimd
        def _(pool):
            nc.gpsimd.memset(ones[:], 1.0).then_inc(consts, 1)
            pool.wait_ge(consts, 1)
            nc.gpsimd.affine_select(out=ident[:], in_=ones[:], compare_op=ALU.is_equal, fill=0.0, base=0,
                                    pattern=[[-1, P]], channel_multiplier=1).then_inc(consts, 1)
            pool.wait_ge(consts, 2)
            for g in range(NG):
                nc.gpsimd.memset(ks[STACK:STACK + 1, g].bitcast(F32), 1.0).then_inc(ones_row, 1)
                pool.wait_ge(ones_row, g + 1)

            def batch(b, first_batch=False):
                for un in range(BU):
                    unit = b * BU + un
                    for j, (first, n, before) in pool_adds.items():
                        pool.wait_ge(exp_done, unit * TILES + j + 1)
                        acc = pool_sum[:, j % HG]
                        if first is None:
                            pool.wait_ge(pool_added, unit * adds_pool + before + 1)
                            a = acc
                        else:
                            if un > 0 or not first_batch:
                                pool.wait_ge(z_done, unit)
                            a = probs[:, first % RING]
                        nc.gpsimd.tensor_tensor(acc, a, probs[:, j % RING], ALU.add).then_inc(pool_added, 1)

            batch(0, first_batch=True)
            with pool.Fori(1, B) as b:
                batch(b)

        @block.vector
        def _(dve):
            def part_max_of(unit, m, first_unit=False):
                h, t, half = m // (2 * QT), m // 2 % QT, m % 2
                if m % (2 * QT) == 0 and not first_unit:
                    dve.wait_ge(neg_max_done, (unit - 1) * HG + h + 1)
                dve.wait_ge(max_scores, unit * (TILES // 2) + m + 1)
                nc.vector.reduce_max(part_max[:, h, t, half:half + 1], ps_max[:, m % 2], AX.XY
                                     ).then_inc(part_max_done, 1)
                if m % (2 * QT) == 2 * QT - 1:
                    dve.wait_ge(part_max_done, unit * (TILES // 2) + m + 1)
                    if not first_unit:
                        dve.wait_ge(max_turned, (unit - 1) * HG + h + 1)
                    nc.vector.tensor_reduce(neg_max[:, h], part_max[:, h], AX.X, ALU.max, negate=True
                                            ).then_inc(neg_max_done, 1)

            for m in range(TILES // 2):
                part_max_of(0, m, first_unit=True)
            for m in range(LEAD // 2):
                part_max_of(1, m)

            def batch(b, first_batch=False, last=False):
                for un in range(BU):
                    unit = b * BU + un
                    carry = un > 0 or not first_batch

                    def add(j):
                        first, n, before = dve_adds[j]
                        dve.wait_ge(exp_done, unit * TILES + j + 1)
                        acc = dve_sum[:, j % HG]
                        if first is None:
                            dve.wait_ge(dve_added, unit * adds_dve + before + 1)
                            a = acc
                        else:
                            if un > 0 or not first_batch:
                                dve.wait_ge(z_done, unit)
                            a = probs[:, first % RING]
                        nc.vector.tensor_tensor(acc, a, probs[:, j % RING], ALU.add).then_inc(dve_added, 1)

                    def invert(prev):
                        dve.wait_ge(z_turned, prev + 1)
                        dve.wait_ge(o_done, prev)
                        nc.vector.reciprocal(rz[:], ps_misc[:].rearrange("p (t h d) -> p t h d", t=QT, h=HG)[:, :, :, 0]
                                             ).then_inc(rz_done, 1)

                    def normalize(prev, un_close):
                        k = (un_close - 1) % BU
                        dve.wait_ge(rz_done, prev + 1)
                        dve.wait_ge(o_turned, prev + 1)
                        if un_close > 2 or not first_batch:
                            dve.wait_ge(o_out[k % 2], (b * (BU // 2) + (un_close - 1) // 2) * 16)
                        nc.vector.tensor_tensor(
                            o[:, k % 2], ps_misc[:].rearrange("p (t h d) -> p t h d", t=QT, h=HG),
                            rz[:].unsqueeze(3).to_broadcast([P, QT, HG, DH]), ALU.mult).then_inc(o_done, 1)

                    for j in range(TILES):
                        if j % 2 == 1:
                            m = (j + LEAD) // 2
                            if un + 1 + m // (TILES // 2) < BU or not last:
                                part_max_of(unit + 1 + m // (TILES // 2), m % (TILES // 2))
                        if carry and j == INVERT_AT:
                            invert(unit - 1)
                        if carry and j == NORMALIZE_AT:
                            normalize(unit - 1, un)
                        if j - ADD_LAG in dve_adds:
                            add(j - ADD_LAG)
                    for j in range(TILES, TILES + ADD_LAG):
                        if j - ADD_LAG in dve_adds:
                            add(j - ADD_LAG)
                if last:
                    invert(b * BU + BU - 1)
                    normalize(b * BU + BU - 1, BU)

            batch(0, first_batch=True)
            with dve.Fori(1, B - 1) as b:
                batch(b)
            batch(B - 1, last=True)

        @block.scalar
        def _(act):
            def row_of_max(unit, h, first_unit=False):
                act.wait_ge(max_turned, unit * HG + h + 1)
                if not first_unit:
                    act.wait_ge(max_in[h], unit * 16)
                nc.scalar.copy(max_row[:, h, :], ps_misc[0:QT, 0:P]).then_inc(max_row_done, 1)

            for h in range(HG):
                row_of_max(0, h, first_unit=True)

            def batch(b, first_batch=False, last=False):
                for un in range(BU):
                    unit = b * BU + un
                    carry = un > 0 or not first_batch

                    def free(j):
                        act.wait_ge(pv_done, unit * TILES + j - RING + 1)
                        before = 1 if j < RING else 0
                        k = (j - RING) % TILES
                        if k in pool_tiles:
                            act.wait_ge(pool_added, (unit - before) * adds_pool + used_by(pool_adds, k))
                        elif k in dve_tiles:
                            act.wait_ge(dve_added, (unit - before) * adds_dve + used_by(dve_adds, k))
                        else:
                            act.wait_ge(z_done, unit + 1 - before)

                    def copy_acc(n):
                        act.wait_ge(pv_done, n * TILES)
                        if un > 1 or not first_batch:
                            act.wait_ge(o_turned, n - 1)
                        nc.scalar.copy(oT[:], ps_acc[:]).then_inc(oT_done, 1)

                    def copy_z(n):
                        act.wait_ge(z_done, n)
                        if un > 1 or not first_batch:
                            act.wait_ge(z_turned, n - 1)
                        nc.scalar.copy(zT[:], ps_misc[:]).then_inc(zT_done, 1)

                    def store(n, un_close):
                        k = (un_close - 1) % BU
                        g, u = k // NU, k % NU
                        act.wait_ge(o_done, n)
                        act.dma_start(out[bass.ds((b + (un_close - 1) // BU) * S + u * UQ, UQ), g * P:(g + 1) * P]
                                      .rearrange("(t p) c -> p t c", p=P),
                                      o[:, k % 2].rearrange("p t h d -> p t (h d)")).then_inc(o_out[k % 2], 16)

                    for j in range(TILES):
                        act.wait_ge(scores, unit * TILES + j + 1)
                        if carry or j >= RING:
                            free(j)
                        nc.scalar.activation(probs[:, j % RING], ps_s[:, j % 2], ACT.Exp, scale=SCALE
                                             ).then_inc(exp_done, 1)
                        if carry:
                            if j == COPY_O_AT:
                                copy_acc(unit)
                            if j == COPY_Z_AT:
                                copy_z(unit)
                            if j == STORE_AT:
                                store(unit, un)
                        if j in MAX_AT and (un + 1 < BU or not last):
                            row_of_max(unit + 1, MAX_AT.index(j))
                if last:
                    copy_acc(b * BU + BU)
                    copy_z(b * BU + BU)
                    store(b * BU + BU, BU)

            batch(0, first_batch=True)
            with act.Fori(1, B - 1) as b:
                batch(b)
            batch(B - 1, last=True)
            for k in range(2):
                act.wait_ge(o_out[k], B * BU // 2 * 16)

        @block.tensor
        def _(pe):
            def score_for_max(unit, un, m, first_unit=False):
                h, t, c = m // (4 * QT), m // 4 % QT, m % 4
                g = un % BU // NU
                if m % 2 == 0 and (m >= 4 or not first_unit):
                    pe.wait_ge(part_max_done, unit * (TILES // 2) + m // 2 - 1)
                last = nc.tensor.matmul(ps_max[:, m // 2 % 2, m % 2], qs[0:STACK, un % NQB, h, t * P:(t + 1) * P],
                                        ks[0:STACK, g, h, c * 512:(c + 1) * 512], start=True, stop=True)
                if m % 2 == 1:
                    last.then_inc(max_scores, 1)

            def turn_max(unit, h):
                pe.wait_ge(neg_max_done, unit * HG + h + 1)
                nc.tensor.transpose(ps_misc[0:QT, 0:P], neg_max[:, h], ident[:]).then_inc(max_turned, 1)

            pe.wait_ge(consts, 2)
            pe.wait_ge(q_in[0], 48)
            pe.wait_ge(k_in[0], 48)
            for m in range(TILES):
                score_for_max(0, 0, m, first_unit=True)
            pe.wait_ge(q_in[1], 48)
            for h in range(HG):
                if h > 0:
                    pe.wait_ge(max_row_done, h)
                turn_max(0, h)
            for m in range(LEAD):
                score_for_max(1, 1, m)

            pe.wait_ge(ones_row, NG)

            def batch(b, first_batch=False, last=False):
                for un in range(BU):
                    unit = b * BU + un
                    carry = un > 0 or not first_batch
                    g, u = un // NU, un % NU

                    def pv(n, k, j):
                        c, h = divmod(j, HG)
                        pe.wait_ge(exp_done, n * TILES + j + 1)
                        if j == 0 and (k > 0 or not first_batch):
                            pe.wait_ge(oT_done, n)
                        nc.tensor.matmul(ps_acc[h * DH:(h + 1) * DH, :], v[:, k // NU, c, h * DH:(h + 1) * DH],
                                         probs[:, j % RING], start=(c == 0), stop=(c == NC - 1)).then_inc(pv_done, 1)

                    def sum_keys(n, part):
                        if part < len(raw_chunks):
                            source = [probs[:, (raw_chunks[part] * HG + h) % RING] for h in range(HG)]
                        elif part == len(raw_chunks):
                            pe.wait_ge(dve_added, n * adds_dve + adds_dve)
                            source = [dve_sum[:, h] for h in range(HG)]
                        else:
                            pe.wait_ge(pool_added, n * adds_pool + adds_pool)
                            source = [pool_sum[:, h] for h in range(HG)]
                        for h in range(HG):
                            last = nc.tensor.matmul(ps_misc[h * DH:(h + 1) * DH, :], ones[:, 0:DH], source[h],
                                                    start=(part == 0), stop=(part == PARTS - 1))
                        if part == PARTS - 1:
                            last.then_inc(z_done, 1)

                    def turn_z(n, half):
                        pe.wait_ge(zT_done, n)
                        for t in range(half * QT // 2, (half + 1) * QT // 2):
                            last = nc.tensor.transpose(ps_misc[:, t * P:(t + 1) * P], zT[:, t * P:(t + 1) * P], ident[:])
                        if half == 1:
                            last.then_inc(z_turned, 1)

                    def turn_o(n, half):
                        pe.wait_ge(rz_done, n)
                        pe.wait_ge(oT_done, n)
                        for t in range(half * QT // 2, (half + 1) * QT // 2):
                            last = nc.tensor.transpose(ps_misc[:, t * P:(t + 1) * P], oT[:, t * P:(t + 1) * P], ident[:])
                        if half == 1:
                            last.then_inc(o_turned, 1)

                    if u == 0:
                        pe.wait_ge(v_in[g], b * 16 + 16)
                    for j in range(TILES):
                        c, h = divmod(j, HG)
                        if j < HG:
                            pe.wait_ge(max_in[h], unit * 16 + 16)
                        if j > 1 or carry:
                            pe.wait_ge(exp_done, unit * TILES + j - 1)
                        nc.tensor.matmul(ps_s[:, j % 2], ks[:, g, h, c * P:(c + 1) * P], qs[:, un % NQB, h, :],
                                         start=True, stop=True).then_inc(scores, 1)
                        m = j + LEAD
                        ahead = un + 1 + m // TILES
                        if m % 2 == MAX_STEP and (ahead < BU or not last):
                            if m // 2 * 2 == TILES:
                                pe.wait_ge(q_in[ahead % NQB], (b * (BU // NQB) + ahead // NQB + 1) * 48)
                                if ahead % NU == 0:
                                    pe.wait_ge(k_in[ahead // NU % NG], (b + ahead // BU + 1) * 48)
                            for n in range(m // 2 * 2, m // 2 * 2 + 2):
                                score_for_max(unit + ahead - un, ahead, n % TILES)
                        if j >= PV_LAG and (j - PV_LAG) % PV_GROUP == PV_GROUP - 1:
                            for t in range(j - PV_LAG - PV_GROUP + 1, j - PV_LAG + 1):
                                pv(unit, un, t)
                        elif carry and j < (TILES - PV_TAIL) // 2:
                            for t in range(PV_TAIL + 2 * j, PV_TAIL + 2 * j + 2):
                                pv(unit - 1, (un - 1) % BU, t)
                        if carry:
                            if j == CLOSE_AT:
                                pe.wait_ge(max_row_done, unit * HG + HG)
                            if CLOSE_AT <= j < CLOSE_AT + PARTS:
                                sum_keys(unit - 1, j - CLOSE_AT)
                            if j in TURN_Z_AT:
                                turn_z(unit, TURN_Z_AT.index(j))
                            if j in TURN_O_AT:
                                turn_o(unit, TURN_O_AT.index(j))
                        if j in MAX_AT and (un + 1 < BU or not last):
                            i = MAX_AT.index(j)
                            if i == 0 and carry:
                                pe.wait_ge(o_done, unit)
                            elif i > 0:
                                pe.wait_ge(max_row_done, (unit + 1) * HG + i)
                            turn_max(unit + 1, i)
                if last:
                    for j in range(PV_TAIL, TILES):
                        pv(b * BU + BU - 1, BU - 1, j)
                    for part in range(PARTS):
                        sum_keys(b * BU + BU - 1, part)
                    for half in range(2):
                        turn_z(b * BU + BU, half)
                    for half in range(2):
                        turn_o(b * BU + BU, half)

            batch(0, first_batch=True)
            with pe.Fori(1, B - 1) as b:
                batch(b)
            batch(B - 1, last=True)


def macaron_block(nc, x, qU, qVt, qb, kU, kVt, kb, vU, vVt, vb, w_router, w_qkvT, w_outT, g1, g2, w1T, w2T, w3T,
                  out):
    after_ffn = nc.dram_tensor("after_ffn", [B * S, D], F32).ap()
    attention = nc.dram_tensor("attention", [B * S, D], F32).ap()
    scores = nc.dram_tensor("router_scores", [P, P], F32).ap()
    qk = nc.dram_tensor("qk_parts", [B, 2, 2 * NG, P, S], F32).ap()
    v_dram = nc.dram_tensor("v_tokens", [B * S, D], F32).ap()
    ffn_weights = (w_qkvT, w_outT, g1, g2, w1T, w2T, w3T)
    with nc.sbuf_tensor("picked", [P, B], U32) as picked:
        score_pass(nc, "s1", x, None, w_router, after_ffn, scores)
        pick_tokens(nc, "t1", scores, picked[:])
        routed_ffn(nc, "f1", x, None, picked[:], *ffn_weights, after_ffn)
        project(nc, "pr", after_ffn, [(qU, qVt), (kU, kVt), (vU, vVt)], [qb, kb], vb, qk, v_dram)
        attend(nc, "at", qk, v_dram, attention)
        score_pass(nc, "s2", after_ffn, attention, w_router, out, scores)
        pick_tokens(nc, "t2", scores, picked[:])
        routed_ffn(nc, "f2", after_ffn, attention, picked[:], *ffn_weights, out)


def kernel(L0_attn_x, L0_attn_Uq, L0_attn_Vq, L0_attn_bq, L0_attn_Uk, L0_attn_Vk, L0_attn_bk, L0_attn_Uv, L0_attn_Vv,
           L0_attn_bv, L0_ffn_w_router, L0_ffn_W_qkv, L0_ffn_W_out, L0_ffn_g1, L0_ffn_g2, L0_ffn_W1, L0_ffn_W2,
           L0_ffn_W3):
    import numpy as np
    import concourse.bacc as bacc
    from concourse.bass_utils import run_bass_kernel_spmd

    def columns(a):
        return np.ascontiguousarray(np.asarray(a).reshape(-1, P).T)

    def turned(a):
        return np.ascontiguousarray(np.swapaxes(np.asarray(a), -1, -2))

    arrays = {
        "x": np.ascontiguousarray(np.asarray(L0_attn_x).reshape(B * S, D)),
        "qU": turned(L0_attn_Uq), "qV": np.ascontiguousarray(L0_attn_Vq), "qb": columns(L0_attn_bq),
        "kU": turned(L0_attn_Uk), "kV": np.ascontiguousarray(L0_attn_Vk), "kb": columns(L0_attn_bk),
        "vU": turned(L0_attn_Uv), "vV": np.ascontiguousarray(L0_attn_Vv),
        "vb": np.ascontiguousarray(np.asarray(L0_attn_bv).reshape(D)),
        "w_router": np.ascontiguousarray(L0_ffn_w_router),
        "w_qkvT": turned(L0_ffn_W_qkv), "w_outT": turned(L0_ffn_W_out),
        "g1": columns(L0_ffn_g1), "g2": columns(L0_ffn_g2),
        "w1T": turned(L0_ffn_W1), "w2T": turned(L0_ffn_W2), "w3T": turned(L0_ffn_W3),
    }
    nc = bacc.Bacc("TRN2", target_bir_lowering=False, num_devices=1)
    args = [nc.dram_tensor(f"in_{n}", a.shape, mybir.dt.from_np(a.dtype), kind="ExternalInput").ap()
            for n, a in arrays.items()]
    out = nc.dram_tensor("out", [B * S, D], F32, kind="ExternalOutput").ap()
    macaron_block(nc, *args, out)
    result = run_bass_kernel_spmd(nc, [{f"in_{n}": a for n, a in arrays.items()}], core_ids=[0])
    return result.results[0]["out"].reshape(B, S, D)
```
